# Optimizing a Trainium2 kernel written in Bass

```python
import numpy as np
import jax
import jax.numpy as jnp

def _softmax(x, axis=-1):
    return jax.nn.softmax(x, axis=axis)

def _gelu(x):
    return jax.nn.gelu(x, approximate=True)

def _silu(x):
    return jax.nn.silu(x)

def _sigmoid(x):
    return jax.nn.sigmoid(x)

def _layernorm(x, axis=-1, eps=1e-05):
    m = jnp.mean(x, axis=axis, keepdims=True)
    v = jnp.var(x, axis=axis, keepdims=True)
    return (x - m) / jnp.sqrt(v + eps)

def _scatter_add(tgt, idx, src, axis=0):
    return tgt.at[idx].add(src)

def _segment_sum(src, seg, n):
    return jax.ops.segment_sum(src, seg, n)
kernel_name = 'mk_decoder_postln_d2_seqx_r4_f6af41'

def setup_inputs(seed: int=0):
    np.random.seed(seed)
    _w = jnp.asarray

    def _rec_inputs():
        import jax
        import jax.numpy as jnp
        _rk = jax.random.key(seed)
        x = 0.002226 + 0.9996 * jax.random.normal(jax.random.fold_in(_rk, 1), (1, 2048, 256), jnp.float32)
        _lenS = 2048 - jax.random.randint(jax.random.fold_in(_rk, 7), (1,), 0, max(1, 2048 // 4) + 1, jnp.int32)
        _lenS2 = 1601 - jax.random.randint(jax.random.fold_in(_rk, 8), (1,), 0, max(1, 1601 // 4) + 1, jnp.int32)
        _ctx_1024P = jax.random.normal(jax.random.fold_in(_rk, 11), (1, 16, 256), jnp.float32)
        _ctx_1024c = jax.random.dirichlet(jax.random.fold_in(_rk, 511), 0.3 * jnp.ones((16,), jnp.float32), (1, 1601))
        _ctx_1024t = jnp.einsum('bsk,bkd->bsd', _ctx_1024c, _ctx_1024P)
        _ctx_1024t = _ctx_1024t * jax.lax.rsqrt(jnp.mean(jnp.square(_ctx_1024t)) + 1e-12) * 0.953939
        ctx_1024 = -0.000125008 + 0.999885 * (_ctx_1024t + 0.3 * jax.random.normal(jax.random.fold_in(_rk, 611), (1, 1601, 256), jnp.float32))
        fside_BxSxS2_0 = jax.random.uniform(jax.random.fold_in(_rk, 12), (1, 2048, 1601), jnp.float32, 0.0, 1)
        _validS = jnp.arange(2048)[None, :] < _lenS[:, None]
        _validS2 = jnp.arange(1601)[None, :] < _lenS2[:, None]
        _causal = jnp.tril(jnp.ones((2048, 2048), dtype=bool))
        mask_BxSxS2_ik1 = jnp.where(jnp.broadcast_to(_validS2[:, None, :], (1, 2048, 1601)), 1, 0).astype(jnp.int32)
        return (x, ctx_1024, fside_BxSxS2_0, mask_BxSxS2_ik1)
    x, ctx_1024, fside_BxSxS2_0, mask_BxSxS2_ik1 = _rec_inputs()

    def _L0_attn_setup():
        import jax, jax.numpy as jnp
        import numpy as np
        KERNEL_SIZE = 16

        def _pad_amounts(kernel_size):
            side = (kernel_size - 1) // 2
            if (kernel_size - 1) % 2:
                return (side, side + 1)
            return (side, side)
        key = jax.random.key(seed)
        k1, k2, k3, k4 = jax.random.split(key, 4)
        B, T, H = (4, 512, 256)
        inputs = jax.random.normal(k1, (B, T, H), dtype=jnp.float32)
        w1 = jax.random.normal(k2, (H, H), dtype=jnp.float32) / np.sqrt(H)
        w2 = jax.random.normal(k3, (H, H), dtype=jnp.float32) / np.sqrt(H)
        v = jax.random.normal(k4, (H, 1), dtype=jnp.float32) / np.sqrt(H)
        return {'inputs': inputs, 'w1': w1, 'w2': w2, 'v': v}
    _L0_attn_all = _L0_attn_setup()
    _L0_attn_in = {k: v for k, v in _L0_attn_all.items() if k in ('w1', 'w2', 'v')}
    del _L0_attn_all

    def _L0_xattn_setup():
        import jax, jax.numpy as jnp
        import numpy as np
        DIM = 256
        HEADS = 16
        DIM_HEAD = 64
        INNER = HEADS * DIM_HEAD
        EPS = 1e-05

        def _layernorm(t, w, b):
            mu = jnp.mean(t, axis=-1, keepdims=True)
            var = jnp.mean(jnp.square(t - mu), axis=-1, keepdims=True)
            return (t - mu) * jax.lax.rsqrt(var + EPS) * w + b
        key = jax.random.key(seed)
        ks = jax.random.split(key, 8)
        b, n, l = (8, 1024, 64)
        x = jax.random.normal(ks[0], (b, n, DIM), dtype=jnp.float32)
        latents = jax.random.normal(ks[1], (b, l, DIM), dtype=jnp.float32)
        ln1_w = jnp.ones((DIM,), jnp.float32)
        ln1_b = jnp.zeros((DIM,), jnp.float32)
        ln2_w = jnp.ones((DIM,), jnp.float32)
        ln2_b = jnp.zeros((DIM,), jnp.float32)
        Wq = jax.random.normal(ks[2], (DIM, INNER), dtype=jnp.float32) / np.sqrt(DIM)
        Wkv = jax.random.normal(ks[3], (DIM, 2 * INNER), dtype=jnp.float32) / np.sqrt(DIM)
        Wo = jax.random.normal(ks[4], (INNER, DIM), dtype=jnp.float32) / np.sqrt(INNER)
        return {'x': x, 'latents': latents, 'ln1_w': ln1_w, 'ln1_b': ln1_b, 'ln2_w': ln2_w, 'ln2_b': ln2_b, 'Wq': Wq, 'Wkv': Wkv, 'Wo': Wo}
    _L0_xattn_all = _L0_xattn_setup()
    _L0_xattn_in = {k: v for k, v in _L0_xattn_all.items() if k in ('ln1_w', 'ln1_b', 'ln2_w', 'ln2_b', 'Wq', 'Wkv', 'Wo')}
    del _L0_xattn_all

    def _L0_ffn_setup():
        import jax, jax.numpy as jnp
        import numpy as np
        BLOCK = 32
        W_BITS = 4
        ACT_BITS = 16

        def act_qdq(x):
            qmax = 2.0 ** (ACT_BITS - 1) - 1.0
            scale = jnp.maximum(jnp.max(jnp.abs(x)) / qmax, 1e-12)
            return jnp.clip(jnp.round(x / scale), -qmax - 1.0, qmax) * scale

        def fixed_qdq_u16(x):
            scale = 1.0 / 65536.0
            return jnp.clip(jnp.round(x / scale), 0.0, 65535.0) * scale

        def lpbq_dequant(w):
            O, I = w.shape
            qmax = 2.0 ** (W_BITS - 1) - 1.0
            wb = w.reshape(O, I // BLOCK, BLOCK)
            s = jnp.maximum(jnp.max(jnp.abs(wb), axis=-1, keepdims=True) / qmax, 1e-12)
            wq = jnp.clip(jnp.round(wb / s), -qmax - 1.0, qmax) * s
            return wq.reshape(O, I)
        key = jax.random.key(seed)
        k1, k2, k3, k4 = jax.random.split(key, 4)
        B, S, H, I = (2, 1024, 256, 768)
        x = jax.random.normal(k1, (B, S, H), jnp.float32)
        w_gate = jax.random.normal(k2, (I, H), jnp.float32) * 0.02
        w_up = jax.random.normal(k3, (I, H), jnp.float32) * 0.02
        w_down = jax.random.normal(k4, (H, I), jnp.float32) * 0.02
        return {'x': x, 'w_gate': w_gate, 'w_up': w_up, 'w_down': w_down}
    _L0_ffn_all = _L0_ffn_setup()
    _L0_ffn_in = {k: v for k, v in _L0_ffn_all.items() if k in ('w_gate', 'w_up', 'w_down')}
    del _L0_ffn_all

    def _L1_attn_setup():
        import jax, jax.numpy as jnp
        import numpy as np
        from jax import lax
        H = 4
        CHUNK = 64
        EPS = 1e-05

        def _rope(t, cos, sin):
            t1, t2 = jnp.split(t, 2, axis=-1)
            c = cos[None, :, None, :]
            s = sin[None, :, None, :]
            return jnp.concatenate([t1 * c - t2 * s, t2 * c + t1 * s], axis=-1)
        key = jax.random.key(seed)
        ks = jax.random.split(key, 8)
        B, T, D = (4, 1024, 256)
        s = lambda fan: 1.0 / np.sqrt(fan)
        return {'x': jax.random.normal(ks[0], (B, T, D), jnp.float32), 'ln_w': jnp.ones((D,), jnp.float32), 'ln_b': jnp.zeros((D,), jnp.float32), 'Wq': jax.random.normal(ks[1], (D, D), jnp.float32) * s(D), 'Wk': jax.random.normal(ks[2], (D, D), jnp.float32) * s(D), 'Wv': jax.random.normal(ks[3], (D, 2 * D), jnp.float32) * s(D), 'Wg': jax.random.normal(ks[4], (D, 2 * D), jnp.float32) * s(D), 'g_norm_w': jnp.ones((2 * D // H,), jnp.float32), 'Wo': jax.random.normal(ks[5], (2 * D, D), jnp.float32) * s(2 * D)}
    _L1_attn_all = _L1_attn_setup()
    _L1_attn_in = {k: v for k, v in _L1_attn_all.items() if k in ('ln_w', 'ln_b', 'Wq', 'Wk', 'Wv', 'Wg', 'g_norm_w', 'Wo')}
    del _L1_attn_all

    def _L1_xattn_setup():
        import jax, jax.numpy as jnp
        import numpy as np
        NUM_HEADS = 16
        HIDDEN = 256
        B, S = (2, 512)

        def _split_heads(x, H):
            b, s, d = x.shape
            return x.reshape(b, s, H, d // H).transpose(0, 2, 1, 3)
        key = jax.random.key(seed)
        ks = jax.random.split(key, 14)
        D = HIDDEN
        scale = 1.0 / np.sqrt(D)
        inp = {'query': jax.random.normal(ks[0], (B, S, D), jnp.float32), 'key_in': jax.random.normal(ks[1], (B, S, D), jnp.float32), 'value': jax.random.normal(ks[2], (B, S, D), jnp.float32), 'group_prob': jax.random.uniform(ks[3], (B, S, S), jnp.float32), 'mask': jax.random.randint(ks[4], (B, S, S), 0, 2, jnp.int32), 'wq_k': jax.random.normal(ks[5], (D, D), jnp.float32) * scale, 'wq_b': jnp.zeros((D,), jnp.float32), 'wk_k': jax.random.normal(ks[6], (D, D), jnp.float32) * scale, 'wk_b': jnp.zeros((D,), jnp.float32), 'wv_k': jax.random.normal(ks[7], (D, D), jnp.float32) * scale, 'wv_b': jnp.zeros((D,), jnp.float32), 'wo_k': jax.random.normal(ks[8], (D, D), jnp.float32) * scale, 'wo_b': jnp.zeros((D,), jnp.float32)}
        return inp
    _L1_xattn_all = _L1_xattn_setup()
    _L1_xattn_in = {k: v for k, v in _L1_xattn_all.items() if k in ('wq_k', 'wq_b', 'wk_k', 'wk_b', 'wv_k', 'wv_b', 'wo_k', 'wo_b')}
    del _L1_xattn_all

    def _L1_ffn_setup():
        import jax, jax.numpy as jnp
        import numpy as np
        TOP_K = 4
        N_GROUP = 4
        TOPK_GROUP = 2
        ROUTED_SCALING = 2.5

        def _route(x, gate_weight):
            scores = jax.nn.sigmoid(x @ gate_weight.T)
            T, E = scores.shape
            gs = E // N_GROUP
            top2, _ = jax.lax.top_k(scores.reshape(T, N_GROUP, gs), 2)
            group_scores = top2.sum(-1)
            _, gidx = jax.lax.top_k(group_scores, TOPK_GROUP)
            gmask = jax.nn.one_hot(gidx, N_GROUP, dtype=jnp.float32).sum(1)
            smask = jnp.repeat(gmask, gs, axis=1) > 0.5
            masked = jnp.where(smask, scores, 0.0)
            topk_idx = jax.lax.top_k(masked, TOP_K)[1]
            topk_w = jnp.take_along_axis(scores, topk_idx, axis=1)
            topk_w = topk_w / (topk_w.sum(-1, keepdims=True) + 1e-20)
            topk_w = topk_w * ROUTED_SCALING
            combine = jnp.zeros((T, E), jnp.float32).at[jnp.arange(T)[:, None], topk_idx].add(topk_w)
            return combine
        key = jax.random.key(seed)
        ks = jax.random.split(key, 6)
        B, S, H = (2, 256, 256)
        E, I, Is = (16, 128, 512)
        g = lambda k, shape, scale: jax.random.normal(k, shape, dtype=jnp.float32) * scale
        return {'hidden_states': g(ks[0], (B, S, H), 1.0), 'gate_weight': g(ks[1], (E, H), 0.02), 'expert_up': g(ks[2], (E, H, I), 0.02), 'expert_down': g(ks[3], (E, I, H), 0.02), 'shared_up': g(ks[4], (H, Is), 0.02), 'shared_down': g(ks[5], (Is, H), 0.02)}
    _L1_ffn_all = _L1_ffn_setup()
    _L1_ffn_in = {k: v for k, v in _L1_ffn_all.items() if k in ('gate_weight', 'expert_up', 'expert_down', 'shared_up', 'shared_down')}
    del _L1_ffn_all
    return {'x': x, 'ctx_1024': ctx_1024, 'fside_BxSxS2_0': fside_BxSxS2_0, 'mask_BxSxS2_ik1': mask_BxSxS2_ik1, 'L0_attn_w1': _L0_attn_in['w1'], 'L0_attn_w2': _L0_attn_in['w2'], 'L0_attn_v': _L0_attn_in['v'], 'L0_xattn_ln1_w': _L0_xattn_in['ln1_w'], 'L0_xattn_ln1_b': _L0_xattn_in['ln1_b'], 'L0_xattn_ln2_w': _L0_xattn_in['ln2_w'], 'L0_xattn_ln2_b': _L0_xattn_in['ln2_b'], 'L0_xattn_Wq': _L0_xattn_in['Wq'], 'L0_xattn_Wkv': _L0_xattn_in['Wkv'], 'L0_xattn_Wo': _L0_xattn_in['Wo'], 'L0_ffn_w_gate': _L0_ffn_in['w_gate'], 'L0_ffn_w_up': _L0_ffn_in['w_up'], 'L0_ffn_w_down': _L0_ffn_in['w_down'], 'L1_attn_ln_w': _L1_attn_in['ln_w'], 'L1_attn_ln_b': _L1_attn_in['ln_b'], 'L1_attn_Wq': _L1_attn_in['Wq'], 'L1_attn_Wk': _L1_attn_in['Wk'], 'L1_attn_Wv': _L1_attn_in['Wv'], 'L1_attn_Wg': _L1_attn_in['Wg'], 'L1_attn_g_norm_w': _L1_attn_in['g_norm_w'], 'L1_attn_Wo': _L1_attn_in['Wo'], 'L1_xattn_wq_k': _L1_xattn_in['wq_k'], 'L1_xattn_wq_b': _L1_xattn_in['wq_b'], 'L1_xattn_wk_k': _L1_xattn_in['wk_k'], 'L1_xattn_wk_b': _L1_xattn_in['wk_b'], 'L1_xattn_wv_k': _L1_xattn_in['wv_k'], 'L1_xattn_wv_b': _L1_xattn_in['wv_b'], 'L1_xattn_wo_k': _L1_xattn_in['wo_k'], 'L1_xattn_wo_b': _L1_xattn_in['wo_b'], 'L1_ffn_gate_weight': _L1_ffn_in['gate_weight'], 'L1_ffn_expert_up': _L1_ffn_in['expert_up'], 'L1_ffn_expert_down': _L1_ffn_in['expert_down'], 'L1_ffn_shared_up': _L1_ffn_in['shared_up'], 'L1_ffn_shared_down': _L1_ffn_in['shared_down']}

def reference(x, ctx_1024, fside_BxSxS2_0, mask_BxSxS2_ik1, L0_attn_w1, L0_attn_w2, L0_attn_v, L0_xattn_ln1_w, L0_xattn_ln1_b, L0_xattn_ln2_w, L0_xattn_ln2_b, L0_xattn_Wq, L0_xattn_Wkv, L0_xattn_Wo, L0_ffn_w_gate, L0_ffn_w_up, L0_ffn_w_down, L1_attn_ln_w, L1_attn_ln_b, L1_attn_Wq, L1_attn_Wk, L1_attn_Wv, L1_attn_Wg, L1_attn_g_norm_w, L1_attn_Wo, L1_xattn_wq_k, L1_xattn_wq_b, L1_xattn_wk_k, L1_xattn_wk_b, L1_xattn_wv_k, L1_xattn_wv_b, L1_xattn_wo_k, L1_xattn_wo_b, L1_ffn_gate_weight, L1_ffn_expert_up, L1_ffn_expert_down, L1_ffn_shared_up, L1_ffn_shared_down):
    import jax
    import jax.numpy as jnp

    def _L0_attn_ref(inputs, w1, w2, v):
        import jax, jax.numpy as jnp
        import numpy as np
        KERNEL_SIZE = 16

        def _pad_amounts(kernel_size):
            side = (kernel_size - 1) // 2
            if (kernel_size - 1) % 2:
                return (side, side + 1)
            return (side, side)
        B, T, H = inputs.shape
        K = KERNEL_SIZE
        pl, pr = _pad_amounts(K)
        x_pad = jnp.pad(inputs, ((0, 0), (pl, pr), (0, 0)))
        idx = jnp.arange(T)[:, None] + jnp.arange(K)[None, :]
        proj = x_pad @ w2
        local_proj = proj[:, idx]
        q = inputs @ w1
        score = jnp.squeeze(jnp.tanh(local_proj + q[:, :, None, :]) @ v, -1)
        weight = jax.nn.softmax(score, axis=-1)
        local = x_pad[:, idx]
        output = jnp.einsum('btk,btkh->bth', weight, local)
        return output

    def _L0_xattn_ref(x, latents, ln1_w, ln1_b, ln2_w, ln2_b, Wq, Wkv, Wo):
        import jax, jax.numpy as jnp
        import numpy as np
        DIM = 256
        HEADS = 16
        DIM_HEAD = 64
        INNER = HEADS * DIM_HEAD
        EPS = 1e-05

        def _layernorm(t, w, b):
            mu = jnp.mean(t, axis=-1, keepdims=True)
            var = jnp.mean(jnp.square(t - mu), axis=-1, keepdims=True)
            return (t - mu) * jax.lax.rsqrt(var + EPS) * w + b
        xn = _layernorm(x, ln1_w, ln1_b)
        latn = _layernorm(latents, ln2_w, ln2_b)
        b, l, _ = latn.shape
        q = latn @ Wq
        kv_input = jnp.concatenate([xn, latn], axis=1)
        kv = kv_input @ Wkv
        k, v = jnp.split(kv, 2, axis=-1)

        def heads(t):
            return t.reshape(t.shape[0], t.shape[1], HEADS, DIM_HEAD).transpose(0, 2, 1, 3)
        q, k, v = (heads(q), heads(k), heads(v))
        scale = 1.0 / np.sqrt(np.sqrt(DIM_HEAD))
        weight = jnp.einsum('bhld,bhnd->bhln', q * scale, k * scale)
        weight = jax.nn.softmax(weight.astype(jnp.float32), axis=-1).astype(weight.dtype)
        out = jnp.einsum('bhln,bhnd->bhld', weight, v)
        out = out.transpose(0, 2, 1, 3).reshape(b, l, INNER)
        return out @ Wo

    def _L0_ffn_ref(x, w_gate, w_up, w_down):
        import jax, jax.numpy as jnp
        import numpy as np
        BLOCK = 32
        W_BITS = 4
        ACT_BITS = 16

        def act_qdq(x):
            qmax = 2.0 ** (ACT_BITS - 1) - 1.0
            scale = jnp.maximum(jnp.max(jnp.abs(x)) / qmax, 1e-12)
            return jnp.clip(jnp.round(x / scale), -qmax - 1.0, qmax) * scale

        def fixed_qdq_u16(x):
            scale = 1.0 / 65536.0
            return jnp.clip(jnp.round(x / scale), 0.0, 65535.0) * scale

        def lpbq_dequant(w):
            O, I = w.shape
            qmax = 2.0 ** (W_BITS - 1) - 1.0
            wb = w.reshape(O, I // BLOCK, BLOCK)
            s = jnp.maximum(jnp.max(jnp.abs(wb), axis=-1, keepdims=True) / qmax, 1e-12)
            wq = jnp.clip(jnp.round(wb / s), -qmax - 1.0, qmax) * s
            return wq.reshape(O, I)
        x = act_qdq(x)
        up = act_qdq(x @ lpbq_dequant(w_up).T)
        gate = act_qdq(x @ lpbq_dequant(w_gate).T)
        sig = fixed_qdq_u16(jax.nn.sigmoid(gate))
        gate = act_qdq(gate * sig)
        o = act_qdq(gate * up)
        return o @ lpbq_dequant(w_down).T

    def _L1_attn_ref(x, ln_w, ln_b, Wq, Wk, Wv, Wg, g_norm_w, Wo):
        import jax, jax.numpy as jnp
        import numpy as np
        from jax import lax
        H = 4
        CHUNK = 64
        EPS = 1e-05

        def _rope(t, cos, sin):
            t1, t2 = jnp.split(t, 2, axis=-1)
            c = cos[None, :, None, :]
            s = sin[None, :, None, :]
            return jnp.concatenate([t1 * c - t2 * s, t2 * c + t1 * s], axis=-1)
        B, T, D = x.shape
        dk, dv = (D // H, 2 * D // H)
        C = CHUNK
        N = T // C
        mu = x.mean(-1, keepdims=True)
        var = ((x - mu) ** 2).mean(-1, keepdims=True)
        normed = (x - mu) * lax.rsqrt(var + EPS) * ln_w + ln_b
        q = (normed @ Wq).reshape(B, T, H, dk)
        k = (normed @ Wk).reshape(B, T, H, dk)
        v = (normed @ Wv).reshape(B, T, H, dv)
        g = (normed @ Wg).reshape(B, T, H, dv)
        inv_freq = 1.0 / 10000.0 ** (jnp.arange(0, dk, 2, dtype=jnp.float32) / dk)
        freqs = jnp.arange(T, dtype=jnp.float32)[:, None] * inv_freq[None, :]
        cos, sin = (jnp.cos(freqs), jnp.sin(freqs))
        q = _rope(q, cos, sin) * dk ** (-0.5)
        k = _rope(k, cos, sin)
        gamma = 1.0 - jnp.exp2(-5.0 - jnp.arange(H, dtype=jnp.float32))
        i = jnp.arange(C, dtype=jnp.float32)
        Dmask = jnp.where(i[:, None] >= i[None, :], gamma[:, None, None] ** (i[:, None] - i[None, :]), 0.0)
        cross = gamma[:, None] ** (i + 1.0)
        kdec = gamma[:, None] ** (C - 1.0 - i)
        gC = gamma ** C
        to_chunks = lambda t, d: t.reshape(B, N, C, H, d).transpose(1, 0, 3, 2, 4)
        qc, kc, vc = (to_chunks(q, dk), to_chunks(k, dk), to_chunks(v, dv))

        def step(S, inp):
            qn, kn, vn = inp
            attn = jnp.einsum('bhid,bhjd->bhij', qn, kn) * Dmask
            o = jnp.einsum('bhij,bhjv->bhiv', attn, vn) + jnp.einsum('bhid,bhdv->bhiv', qn * cross[None, :, :, None], S)
            S = S * gC[None, :, None, None] + jnp.einsum('bhid,bhiv->bhdv', kn * kdec[None, :, :, None], vn)
            return (S, o)
        S0 = jnp.zeros((B, H, dk, dv), x.dtype)
        _, o = lax.scan(step, S0, (qc, kc, vc))
        o = o.transpose(1, 0, 3, 2, 4).reshape(B, T, H, dv)
        o = o * lax.rsqrt((o ** 2).mean(-1, keepdims=True) + EPS) * g_norm_w
        o = o * (g * jax.nn.sigmoid(g))
        out = o.reshape(B, T, 2 * D) @ Wo
        return x + out

    def _L1_xattn_ref(query, key_in, value, group_prob, mask, wq_k, wq_b, wk_k, wk_b, wv_k, wv_b, wo_k, wo_b):
        import jax, jax.numpy as jnp
        import numpy as np
        NUM_HEADS = 16
        HIDDEN = 256
        B, S = (2, 512)

        def _split_heads(x, H):
            b, s, d = x.shape
            return x.reshape(b, s, H, d // H).transpose(0, 2, 1, 3)
        H = NUM_HEADS
        dh = query.shape[-1] // H
        q = _split_heads(query @ wq_k + wq_b, H)
        k = _split_heads(key_in @ wk_k + wk_b, H)
        v = _split_heads(value @ wv_k + wv_b, H)
        logits = jnp.einsum('bhqd,bhkd->bhqk', q, k) / jnp.sqrt(jnp.asarray(dh, q.dtype))
        neg = (1.0 - mask.astype(q.dtype)) * -1000000000.0
        logits = logits + neg[:, None, :, :]
        attn = jax.nn.softmax(logits, axis=-1)
        attn = attn * group_prob[:, None, :, :]
        out = jnp.einsum('bhqk,bhkd->bhqd', attn, v)
        out = out.transpose(0, 2, 1, 3).reshape(query.shape[0], -1, H * dh)
        return out @ wo_k + wo_b

    def _L1_ffn_ref(hidden_states, gate_weight, expert_up, expert_down, shared_up, shared_down):
        import jax, jax.numpy as jnp
        import numpy as np
        TOP_K = 4
        N_GROUP = 4
        TOPK_GROUP = 2
        ROUTED_SCALING = 2.5

        def _route(x, gate_weight):
            scores = jax.nn.sigmoid(x @ gate_weight.T)
            T, E = scores.shape
            gs = E // N_GROUP
            top2, _ = jax.lax.top_k(scores.reshape(T, N_GROUP, gs), 2)
            group_scores = top2.sum(-1)
            _, gidx = jax.lax.top_k(group_scores, TOPK_GROUP)
            gmask = jax.nn.one_hot(gidx, N_GROUP, dtype=jnp.float32).sum(1)
            smask = jnp.repeat(gmask, gs, axis=1) > 0.5
            masked = jnp.where(smask, scores, 0.0)
            topk_idx = jax.lax.top_k(masked, TOP_K)[1]
            topk_w = jnp.take_along_axis(scores, topk_idx, axis=1)
            topk_w = topk_w / (topk_w.sum(-1, keepdims=True) + 1e-20)
            topk_w = topk_w * ROUTED_SCALING
            combine = jnp.zeros((T, E), jnp.float32).at[jnp.arange(T)[:, None], topk_idx].add(topk_w)
            return combine
        B, S, H = hidden_states.shape
        x = hidden_states.reshape(-1, H)
        combine = _route(x.astype(jnp.float32), gate_weight)
        up = jnp.einsum('th,ehi->eti', x, expert_up)
        down = jnp.einsum('eti,eih->eth', jax.nn.silu(up), expert_down)
        moe_out = jnp.einsum('te,eth->th', combine, down)
        shared = jax.nn.silu(x @ shared_up) @ shared_down
        return (moe_out + shared).reshape(B, S, H)
    x = _layernorm(x + _L0_attn_ref(x, L0_attn_w1, L0_attn_w2, L0_attn_v), axis=-1)
    x = _layernorm(x + _L0_xattn_ref(ctx_1024, x, L0_xattn_ln1_w, L0_xattn_ln1_b, L0_xattn_ln2_w, L0_xattn_ln2_b, L0_xattn_Wq, L0_xattn_Wkv, L0_xattn_Wo), axis=-1)
    x = _layernorm(x + _L0_ffn_ref(x, L0_ffn_w_gate, L0_ffn_w_up, L0_ffn_w_down), axis=-1)
    x = _layernorm(x + _L1_attn_ref(x, L1_attn_ln_w, L1_attn_ln_b, L1_attn_Wq, L1_attn_Wk, L1_attn_Wv, L1_attn_Wg, L1_attn_g_norm_w, L1_attn_Wo), axis=-1)
    x = _layernorm(x + _L1_xattn_ref(x, ctx_1024, ctx_1024, fside_BxSxS2_0, mask_BxSxS2_ik1, L1_xattn_wq_k, L1_xattn_wq_b, L1_xattn_wk_k, L1_xattn_wk_b, L1_xattn_wv_k, L1_xattn_wv_b, L1_xattn_wo_k, L1_xattn_wo_b), axis=-1)
    x = _layernorm(x + _L1_ffn_ref(x, L1_ffn_gate_weight, L1_ffn_expert_up, L1_ffn_expert_down, L1_ffn_shared_up, L1_ffn_shared_down), axis=-1)
    return x

_drawn_inputs = setup_inputs


def setup_inputs(seed=0):
    import zlib

    import numpy as np

    out = dict(_drawn_inputs(seed))
    spreads = {'L0_xattn_ln1_w': (1.0, 0.2),
     'L0_xattn_ln1_b': (0.0, 0.1),
     'L0_xattn_ln2_w': (1.0, 0.6),
     'L0_xattn_ln2_b': (0.0, 0.1),
     'L1_attn_ln_w': (1.0, 0.2),
     'L1_attn_ln_b': (0.0, 0.1),
     'L1_attn_g_norm_w': (1.0, 0.2),
     'L1_xattn_wq_b': (0.0, 0.581),
     'L1_xattn_wk_b': (0.0, 2.0),
     'L1_xattn_wv_b': (0.0, 0.1),
     'L1_xattn_wo_b': (0.0, 0.1)}
    factors = {'fside_BxSxS2_0': 3.426}
    for name, (base, spread) in spreads.items():
        noise = np.random.default_rng([zlib.crc32(name.encode()), seed]).standard_normal(out[name].shape)
        drawn = base * np.exp(spread * noise) if base else spread * noise
        out[name] = jnp.asarray(drawn.astype(out[name].dtype))
    for name, factor in factors.items():
        out[name] = (out[name] * factor).astype(out[name].dtype)
    return out
```

```python
from contextlib import ExitStack, contextmanager
from itertools import count

import numpy as np

import concourse.bass as bass
from concourse import mybir

ALU = mybir.AluOpType
ACT = mybir.ActivationFunctionType
AX = mybir.AxisListType
F32 = mybir.dt.float32
F16 = mybir.dt.float16
I32 = mybir.dt.int32

P = 128
T = 2048
D = 256
NT = T // P
DC = D // P
CH = 512
NC_T = T // CH
S2 = 1601
CT = (S2 + P - 1) // P
CLAST = S2 - (CT - 1) * P
EPS = 1e-5
MAGIC = 12582912.0


USES = count()


@contextmanager
def semaphore(nc, name):
    yield nc.alloc_semaphore(f"{name}_{next(USES)}")


class Chain:

    def __init__(self, eng, sem):
        self.eng, self.sem, self.n = eng, sem, 0

    def __call__(self, ins):
        self.n += 1
        ins.then_inc(self.sem, 1)

    def wait(self):
        self.eng.wait_ge(self.sem, self.n)

    def step(self, ins):
        self(ins)
        self.wait()


def spread(ap, axis, n):
    shape = list(ap.shape)
    return ap.unsqueeze(axis).broadcast_to(shape[:axis] + [n] + shape[axis:])


def load_block(nc, loads):
    with semaphore(nc, "loaded_sync") as loaded_sync, semaphore(nc, "loaded_act") as loaded_act, nc.Block() as block:
        @block.sync
        def _(sync):
            mine = loads[0::2]
            for dst, src in mine:
                sync.dma_start(dst, src).then_inc(loaded_sync, 16)
            sync.wait_ge(loaded_sync, 16 * len(mine))

        if loads[1::2]:
            @block.scalar
            def _(act):
                mine = loads[1::2]
                for dst, src in mine:
                    act.dma_start(dst, src).then_inc(loaded_act, 16)
                act.wait_ge(loaded_act, 16 * len(mine))


def norm_block(nc, label, ident, src, dst, tiles, last_rows, normalise, turned=None, gain=None, shift=None):
    rows = [P] * (tiles - 1) + [last_rows]
    with ExitStack() as ctx:
        def sem(name):
            return ctx.enter_context(semaphore(nc, name))

        stats = ctx.enter_context(nc.sbuf_tensor(f"{label}_stats", [P, tiles, 6], F32))
        mean_var = ctx.enter_context(nc.sbuf_tensor(f"{label}_mean_var", [P, tiles, 2], F32))
        deviation = ctx.enter_context(nc.sbuf_tensor(f"{label}_deviation", [P, tiles], F32))
        inverse = ctx.enter_context(nc.sbuf_tensor(f"{label}_inverse", [P, tiles], F32))
        banks = ctx.enter_context(nc.psum_tensor(f"{label}_banks", [P, 8, CH], F32))
        vector_step = sem("norm_vector_step")
        variance_ready = sem("norm_variance_ready")
        deviation_ready = sem("norm_deviation_ready")
        tile_ready = sem("norm_tile_ready")
        bank_turned = sem("norm_bank_turned")
        groups = (tiles + 3) // 4
        block = ctx.enter_context(nc.Block())

        if normalise:
            @block.vector
            def _(dve):
                chain = Chain(dve, vector_step)
                if last_rows < P:
                    chain(dve.memset(mean_var[:], 1.0))
                for t in range(tiles):
                    chain(dve.bn_stats(stats[0:rows[t], t, :], src[0:rows[t], t, :]))
                chain.wait()
                for t in range(tiles):
                    chain(dve.bn_aggr(mean_var[0:rows[t], t, :], stats[0:rows[t], t, :]))
                chain.wait()
                dve.tensor_scalar(deviation[:], mean_var[:, :, 1], EPS, None, ALU.add).then_inc(variance_ready, 1)
                dve.wait_ge(deviation_ready, 1)
                chain.step(dve.reciprocal(inverse[:], deviation[:]))
                for t in range(tiles):
                    dve.tensor_scalar(dst[0:rows[t], t, :], src[0:rows[t], t, :], mean_var[0:rows[t], t, 0:1],
                                      inverse[0:rows[t], t:t + 1], ALU.subtract, ALU.mult).then_inc(tile_ready, 1)

        @block.scalar
        def _(act):
            if normalise:
                act.wait_ge(variance_ready, 1)
                act.activation(deviation[:], deviation[:], ACT.Sqrt).then_inc(deviation_ready, 1)
            if turned is not None:
                for g in range(groups):
                    lo, hi = g * CH, sum(rows[:4 * g + 4])
                    for c in range(DC):
                        act.wait_ge(bank_turned, DC * g + c + 1)
                        bank = banks[:, DC * g + c, 0:hi - lo]
                        if gain is None:
                            act.activation(turned[:, c, lo:hi], bank, ACT.Copy)
                        else:
                            act.activation(turned[:, c, lo:hi], bank, ACT.Identity,
                                           bias=shift[:, c:c + 1], scale=gain[:, c:c + 1])

        if turned is not None:
            @block.tensor
            def _(pe):
                for g in range(groups):
                    members = range(4 * g, min(4 * g + 4, tiles))
                    if normalise:
                        pe.wait_ge(tile_ready, members[-1] + 1)
                    for c in range(DC):
                        for t in members:
                            n = rows[t]
                            at = (t - 4 * g) * P
                            last = pe.transpose(banks[:, DC * g + c, at:at + n], dst[0:n, t, c * P:(c + 1) * P],
                                                ident[0:n, 0:n])
                        last.then_inc(bank_turned, 1)



K1 = 16
LEFT = (K1 - 1) // 2
PADDED = T + K1
GROUPS = PADDED // K1
BAND = P + K1


def local_attention(nc, io, ident, X, R):
    with ExitStack() as ctx:
        def sb(name, shape, dt=F32):
            return ctx.enter_context(nc.sbuf_tensor(name, shape, dt))

        x_pad = sb("x_pad", [P, NT + 1, D])
        band_mask = sb("band_mask", [P, BAND])
        weights = sb("slot_weights", [P, NT, K1])
        with ExitStack() as inner:
            def isb(name, shape, dt=F32):
                return inner.enter_context(nc.sbuf_tensor(name, shape, dt))

            x_turned = isb("x_turned", [P, DC, T])
            w1 = isb("w1", [P, DC, D])
            w2 = isb("w2", [P, DC, D])
            v_window = isb("v_window", [P, DC, 2 * K1 + K1 - 1])
            query = isb("query", [P, DC, K1 - 1 + T + K1])
            proj = isb("proj", [P, DC, PADDED])
            z = isb("z", [P, 3, DC, PADDED])
            score_rows = isb("score_rows", [P, CH])
            slot_max = isb("slot_max", [P, NT])
            slot_sum = isb("slot_sum", [P, NT])
            x_rows = io["x"].rearrange("a (i p) d -> p (a i) d", p=P)
            x_flat = io["x"].rearrange("a t d -> (a t) d")
            with semaphore(nc, "zeroed") as zeroed, semaphore(nc, "late_loaded") as loaded, nc.Block() as block:
                @block.vector
                def _(dve):
                    dve.memset(x_pad[:, 0, :], 0.0).then_inc(zeroed, 1)
                    dve.memset(x_pad[:, NT, :], 0.0).then_inc(zeroed, 1)
                    dve.memset(v_window[:], 0.0).then_inc(zeroed, 1)
                    dve.memset(query[:], 0.0)
                    dve.memset(proj[:], 0.0)

                @block.scalar
                def _(act):
                    act.dma_start(w1[:], io["L0_attn_w1"].rearrange("(c p) n -> p c n", p=P)).then_inc(loaded, 16)
                    act.dma_start(w2[:], io["L0_attn_w2"].rearrange("(c p) n -> p c n", p=P)).then_inc(loaded, 16)
                    act.dma_start(ident[:], io["const_identity"]).then_inc(loaded, 16)
                    act.dma_start(band_mask[:], io["const_band"]).then_inc(loaded, 16)

                @block.sync
                def _(sync):
                    sync.dma_start(X[:], x_rows).then_inc(loaded, 16)
                    sync.wait_ge(zeroed, 3)
                    first = P - LEFT
                    sync.dma_start(x_pad[LEFT:P, 0, :], x_flat[0:first, :]).then_inc(loaded, 16)
                    sync.dma_start(x_pad[:, 1:NT, :], x_flat[first:first + (NT - 1) * P, :].rearrange(
                        "(i p) d -> p i d", p=P)).then_inc(loaded, 16)
                    sync.dma_start(x_pad[0:LEFT, NT, :], x_flat[T - LEFT:T, :]).then_inc(loaded, 16)
                    with nc.allow_non_contiguous_dma(reason="v is 256 values"):
                        sync.dma_start(v_window[:, :, K1 - 1:K1], io["L0_attn_v"].rearrange(
                            "(c p) a -> p c a", p=P)).then_inc(loaded, 16)
                    sync.wait_ge(loaded, 16 * 9)

            norm_block(nc, "turn_x", ident, X, X, NT, P, False, turned=x_turned)

            with ExitStack() as sems:
                def sem(name):
                    return sems.enter_context(semaphore(nc, name))

                projected = sem("projected")
                evacuated = sem("evacuated")
                added_first = sem("added_first")
                added_second = sem("added_second")
                added_pool = sem("added_pool")
                squashed = sem("squashed")
                dotted = sem("dotted")
                rows_ready = sem("rows_ready")
                rows_copied = sem("rows_copied")
                turned_ready = sem("turned_ready")
                shifted = sem("shifted")
                exp_done = sem("exp_done")
                step = sem("softmax_step")
                pq = sems.enter_context(nc.psum_tensor("pq", [P, 4, CH], F32))
                score_bank = sems.enter_context(nc.psum_tensor("score_bank", [P, CH], F32))
                turned_bank = sems.enter_context(nc.psum_tensor("turned_bank", [P, CH], F32))
                block = sems.enter_context(nc.Block())
                jobs = [(w, out, off, c, n) for w, out, off in ((w1, query, K1 - 1), (w2, proj, LEFT))
                        for c in range(DC) for n in range(NC_T)]

                def on_pool(m, c):
                    return c == 1 and m % 3 != 1

                def added(m, c):
                    if c == 0:
                        return added_first, m + 1
                    mine = sum(on_pool(i, 1) == on_pool(m, 1) for i in range(m + 1))
                    return (added_pool if on_pool(m, 1) else added_second), mine

                def add_slot(eng, m, c):
                    s = m % 3
                    eng.tensor_tensor(
                        z[:, s, c, :].rearrange("p (g j) -> p g j", j=K1),
                        query[:, c, m:m + PADDED].rearrange("p (g j) -> p g j", j=K1),
                        spread(proj[:, c, :].rearrange("p (g j) -> p g j", j=K1)[:, :, m], 2, K1),
                        ALU.add).then_inc(added(m, c)[0], 1)

                @block.tensor
                def _(pe):
                    for i, (w, _, _, c, n) in enumerate(jobs):
                        if i >= 4:
                            pe.wait_ge(evacuated, i - 3)
                        for k in range(DC):
                            last = pe.matmul(pq[:, i % 4, :], w[:, k, c * P:(c + 1) * P],
                                             x_turned[:, k, n * CH:(n + 1) * CH], start=(k == 0), stop=(k == DC - 1))
                        last.then_inc(projected, 1)
                    for m in range(K1):
                        for c in range(DC):
                            pe.wait_ge(squashed, m * DC + c + 1)
                            for n in range(NC_T):
                                at = K1 - 1 - m + n * CH
                                last = pe.matmul(score_bank[32 * n:32 * n + 32, :],
                                                 v_window[:, c, K1 - 1 - m:K1 - 1 - m + 32],
                                                 z[:, m % 3, c, at:at + CH], start=(m == 0 and c == 0),
                                                 stop=(m == K1 - 1 and c == DC - 1))
                        last.then_inc(dotted, 1)
                    pe.wait_ge(rows_copied, 1)
                    for j in range(4):
                        last = pe.transpose(turned_bank[:, j * P:(j + 1) * P], score_rows[:, j * P:(j + 1) * P],
                                            ident[:])
                    last.then_inc(turned_ready, 1)

                @block.scalar
                def _(act):
                    for i, (_, out, off, c, n) in enumerate(jobs):
                        act.wait_ge(projected, i + 1)
                        act.activation(out[:, c, off + n * CH:off + (n + 1) * CH], pq[:, i % 4, :],
                                       ACT.Copy).then_inc(evacuated, 1)
                    for m in range(K1):
                        for c in range(DC):
                            act.wait_ge(*added(m, c))
                            at = K1 - 1 - m
                            zc = z[:, m % 3, c, at:at + T]
                            act.activation(zc, zc, ACT.Tanh).then_inc(squashed, 1)
                    act.wait_ge(shifted, 1)
                    act.activation(weights[:], weights[:], ACT.Exp).then_inc(exp_done, 1)

                @block.gpsimd
                def _(pool):
                    pool.wait_ge(evacuated, len(jobs))
                    for m in range(K1):
                        if on_pool(m, 1):
                            if m >= 3:
                                pool.wait_ge(dotted, m - 2)
                            add_slot(pool, m, 1)

                @block.vector
                def _(dve):
                    dve.wait_ge(evacuated, len(jobs))
                    for m in range(K1):
                        if m >= 3:
                            dve.wait_ge(dotted, m - 2)
                        for c in range(DC):
                            if not on_pool(m, c):
                                add_slot(dve, m, c)
                    dve.wait_ge(dotted, K1)
                    dve.tensor_copy(score_rows[:], score_bank[:]).then_inc(rows_copied, 1)
                    dve.wait_ge(turned_ready, 1)
                    chain = Chain(dve, step)
                    slots = turned_bank[:].rearrange("p (j n m) -> p j n m", j=4, n=4)[:, :, :, 0:K1]
                    by_tile = "p (n j) -> p j n"
                    chain.step(dve.tensor_reduce(slot_max[:].rearrange(by_tile, n=4), slots, AX.X, ALU.max))
                    for j in range(4):
                        last = dve.tensor_tensor(weights[:].rearrange("p (n j) m -> p j n m", n=4)[:, j],
                                                 slots[:, j],
                                                 spread(slot_max[:].rearrange(by_tile, n=4)[:, j], 2, K1),
                                                 ALU.subtract)
                    last.then_inc(shifted, 1)
                    dve.wait_ge(exp_done, 1)
                    chain.step(dve.tensor_reduce(slot_sum[:], weights[:], AX.X, ALU.add))
                    chain.step(dve.reciprocal(slot_max[:], slot_sum[:]))
                    dve.tensor_tensor(weights[:], weights[:], spread(slot_max[:], 2, K1), ALU.mult)

        band = sb("band", [P, NT, BAND])
        band_turned = sb("band_turned", [P, NT, P])
        edge_turned = sb("edge_turned", [K1, NT, P])
        with ExitStack() as sems:
            def sem(name):
                return sems.enter_context(semaphore(nc, name))

            banded = sem("banded")
            main_turned = sem("main_turned")
            edges_turned = sem("edges_turned")
            main_copied = sem("main_copied")
            edges_copied = sem("edges_copied")
            mixed = sem("mixed")
            banks = sems.enter_context(nc.psum_tensor("band_banks", [P, 8, CH], F32))
            block = sems.enter_context(nc.Block())

            @block.vector
            def _(dve):
                for i in range(NT):
                    dve.tensor_tensor(band[:, i, :].rearrange("p (r m) -> p r m", m=K1),
                                      spread(weights[:, i, :], 1, BAND // K1),
                                      band_mask[:].rearrange("p (r m) -> p r m", m=K1), ALU.mult).then_inc(banded, 1)
                for q in range(4):
                    dve.wait_ge(edges_turned, q + 1)
                    dve.tensor_copy(edge_turned[:, 4 * q:4 * q + 4, :].rearrange("p a b -> p (a b)"),
                                    banks[0:K1, 4 + q, :]).then_inc(edges_copied, 1)
                for q in range(NT // 2):
                    dve.wait_ge(mixed, q + 1)
                    dve.tensor_tensor(R[:, 2 * q:2 * q + 2, :].rearrange("p a b -> p (a b)"), banks[:, q, :],
                                      X[:, 2 * q:2 * q + 2, :].rearrange("p a b -> p (a b)"), ALU.add)

            @block.scalar
            def _(act):
                for q in range(4):
                    act.wait_ge(main_turned, q + 1)
                    act.activation(band_turned[:, 4 * q:4 * q + 4, :].rearrange("p a b -> p (a b)"),
                                   banks[:, q, :], ACT.Copy).then_inc(main_copied, 1)

            @block.tensor
            def _(pe):
                for q in range(4):
                    pe.wait_ge(banded, 4 * q + 4)
                    for j in range(4):
                        last = pe.transpose(banks[:, q, j * P:(j + 1) * P], band[:, 4 * q + j, 0:P], ident[:])
                    last.then_inc(main_turned, 1)
                    for j in range(4):
                        last = pe.transpose(banks[0:K1, 4 + q, j * P:(j + 1) * P], band[:, 4 * q + j, P:BAND], ident[:])
                    last.then_inc(edges_turned, 1)
                for i in range(NT):
                    q = i // 2
                    if i % 2 == 0:
                        if q < 4:
                            pe.wait_ge(main_copied, q + 1)
                            pe.wait_ge(edges_copied, (i + 1) // 4 + 1)
                        else:
                            pe.wait_ge(edges_copied, 4)
                            pe.wait_ge(main_copied, 4)
                    out = banks[:, q, (i % 2) * D:(i % 2 + 1) * D]
                    pe.matmul(out, band_turned[:, i, :], x_pad[:, i, :], start=True, stop=False)
                    last = pe.matmul(out, edge_turned[:, i, :], x_pad[0:K1, i + 1, :], start=False, stop=True)
                    if i % 2:
                        last.then_inc(mixed, 1)


def basic_constants():
    p = np.arange(P)[:, None]
    j = np.arange(BAND)[None, :]
    band = ((j >= p) & (j < p + K1)).astype(np.float32)
    return {"const_identity": np.eye(P, dtype=np.float32), "const_band": band}



FF = 768
FC = FF // P
WB = 32
W_QMAX = 7.0
A_QMAX = 32767.0
SCALE_FLOOR = 1e-12


def quantised_ffn(nc, ident, io, X, R):
    with ExitStack() as ctx:
        def sb(name, shape, dt=F32):
            return ctx.enter_context(nc.sbuf_tensor(name, shape, dt))

        gate = sb("gate", [P, FC, T])
        up = sb("up", [P, FC, T])
        in_turned = sb("w_in_turned", [P, 2, DC, FF])
        down_turned = sb("w_down_turned", [P, FC, D])
        peak = sb("peak", [P, 5, FC])
        peak_one = sb("peak_one", [P, 5])
        peak_all = sb("peak_all", [P, 5])
        scale = sb("act_scale", [P, 5])
        inverse = sb("act_inverse", [P, 5])
        with ExitStack() as inner:
            x_turned = inner.enter_context(nc.sbuf_tensor("ffn_x_turned", [P, DC, T], F32))
            raw = gate[:, 0:3, :].rearrange("p a t -> p (a t)")[:, 0:3 * 1536].rearrange("p (w n) -> p w n", w=3)
            blocks = 1536 // WB
            w_peak = gate[:, 3, 0:3 * blocks].rearrange("p (w b) -> p w b", w=3)
            w_scale = gate[:, 3, 256:256 + 3 * blocks].rearrange("p (w b) -> p w b", w=3)
            w_inverse = gate[:, 3, 512:512 + 3 * blocks].rearrange("p (w b) -> p w b", w=3)
            x_quant = up[:, 0:2, :].rearrange("p a t -> p (a t)").rearrange("p (i d) -> p i d", i=NT)
            load_block(nc, [
                (raw[:, 0, :].rearrange("p (a d) -> p a d", d=D), io["L0_ffn_w_gate"].rearrange("(a p) d -> p a d", p=P)),
                (raw[:, 1, :].rearrange("p (a d) -> p a d", d=D), io["L0_ffn_w_up"].rearrange("(a p) d -> p a d", p=P)),
                (raw[:, 2, :].rearrange("p (a d) -> p a d", d=FF), io["L0_ffn_w_down"].rearrange("(a p) d -> p a d", p=P)),
            ])
            with ExitStack() as sems:
                def sem(name):
                    return sems.enter_context(semaphore(nc, name))

                step = sem("quant_step")
                x_peak = sem("x_peak")
                x_peak_all = sem("x_peak_all")
                weights_ready = sem("weights_ready")
                w_turned = sem("w_turned")
                w_copied = sem("w_copied")
                banks = sems.enter_context(nc.psum_tensor("w_banks", [P, 8, CH], F32))
                block = sems.enter_context(nc.Block())
                jobs = []
                for w in range(2):
                    for c in range(DC):
                        for part in ((0, 4), (4, 6)):
                            jobs.append([(raw[:, w, a * D + c * P:a * D + (c + 1) * P], k) for k, a in
                                         enumerate(range(*part))] + [in_turned[:, w, c, part[0] * P:part[1] * P]])
                for q in range(FC // 2):
                    jobs.append([(raw[:, 2, a * FF + i * P:a * FF + (i + 1) * P], 2 * k + a)
                                 for k, i in enumerate((2 * q, 2 * q + 1)) for a in range(2)]
                                + [down_turned[:, 2 * q:2 * q + 2, :].rearrange("p a b -> p (a b)")])

                @block.vector
                def _(dve):
                    chain = Chain(dve, step)
                    dve.tensor_reduce(peak_one[:, 0:1], X[:].rearrange("p i d -> p (i d)"), AX.X, ALU.max,
                                      apply_absolute_value=True).then_inc(x_peak, 1)
                    by_block = raw[:].rearrange("p w (b k) -> p w b k", k=WB)
                    chain.step(dve.tensor_reduce(w_peak, by_block, AX.X, ALU.max, apply_absolute_value=True))
                    chain.step(dve.tensor_scalar(w_scale, w_peak, 1.0 / W_QMAX, SCALE_FLOOR, ALU.mult, ALU.max))
                    chain.step(dve.reciprocal(w_inverse, w_scale))
                    for w in range(3):
                        wb = by_block[:, w]
                        chain.step(dve.tensor_tensor(wb, wb, spread(w_inverse[:, w], 2, WB), ALU.mult))
                        chain.step(dve.tensor_scalar(raw[:, w], raw[:, w], MAGIC, MAGIC, ALU.add, ALU.subtract))
                        dve.tensor_tensor(wb, wb, spread(w_scale[:, w], 2, WB), ALU.mult).then_inc(weights_ready, 1)
                    dve.wait_ge(x_peak_all, 1)
                    chain.step(dve.tensor_scalar(scale[:, 0:1], peak_all[:, 0:1], 1.0 / A_QMAX, SCALE_FLOOR,
                                                 ALU.mult, ALU.max))
                    chain.step(dve.reciprocal(inverse[:, 0:1], scale[:, 0:1]))
                    chain.step(dve.tensor_scalar(x_quant, X[:], inverse[:, 0:1], MAGIC, ALU.mult, ALU.add))
                    dve.tensor_scalar(x_quant, x_quant, MAGIC, scale[:, 0:1], ALU.subtract, ALU.mult)

                @block.gpsimd
                def _(pool):
                    pool.wait_ge(x_peak, 1)
                    pool.partition_all_reduce(peak_all[:, 0:1], peak_one[:, 0:1], P,
                                              bass.bass_isa.ReduceOp.max).then_inc(x_peak_all, 1)

                @block.tensor
                def _(pe):
                    for n, job in enumerate(jobs):
                        pe.wait_ge(weights_ready, 1 + n // 4 if n < 8 else 3)
                        if n >= 8:
                            pe.wait_ge(w_copied, n - 7)
                        for src, k in job[:-1]:
                            last = pe.transpose(banks[:, n % 8, k * P:(k + 1) * P], src, ident[:])
                        last.then_inc(w_turned, 1)

                @block.scalar
                def _(act):
                    for n, job in enumerate(jobs):
                        act.wait_ge(w_turned, n + 1)
                        act.activation(job[-1], banks[:, n % 8, 0:job[-1].shape[1]], ACT.Copy).then_inc(w_copied, 1)

            norm_block(nc, "turn_quant", ident, x_quant, x_quant, NT, P, False, turned=x_turned)

            with ExitStack() as sems:
                def sem(name):
                    return sems.enter_context(semaphore(nc, name))

                multiplied = sem("ffn_multiplied")
                copied = sem("ffn_copied")
                banks = sems.enter_context(nc.psum_tensor("ffn_banks", [P, 2, 4, CH], F32))
                block = sems.enter_context(nc.Block())

                @block.tensor
                def _(pe):
                    for n in range(2 * FC):
                        w, i = n // FC, n % FC
                        if n >= 2:
                            pe.wait_ge(copied, n - 1)
                        for q in range(NC_T):
                            for k in range(DC):
                                last = pe.matmul(banks[:, n % 2, q, :], in_turned[:, w, k, i * P:(i + 1) * P],
                                                 x_turned[:, k, q * CH:(q + 1) * CH], start=(k == 0), stop=(k == DC - 1))
                        last.then_inc(multiplied, 1)

                @block.scalar
                def _(act):
                    for n in range(2 * FC):
                        act.wait_ge(multiplied, n + 1)
                        act.activation((gate if n < FC else up)[:, n % FC, :],
                                       banks[:, n % 2].rearrange("p q n -> p (q n)"), ACT.Copy).then_inc(copied, 1)

                @block.vector
                def _(dve):
                    for n in range(2 * FC):
                        dve.wait_ge(copied, n + 1)
                        w = n // FC
                        dve.tensor_reduce(peak[:, 1 + w, n % FC:n % FC + 1], (up if w else gate)[:, n % FC, :], AX.X,
                                          ALU.max, apply_absolute_value=True)

        half = sb("sigmoid", [P, 3, T])
        with ExitStack() as sems:
            def sem(name):
                return sems.enter_context(semaphore(nc, name))

            step = sem("qdq_step")
            peaks_ready = sem("peaks_ready")
            peaks_all = sem("peaks_all")
            scales_ready = sem("scales_ready")
            gate_ready = sem("gate_ready")
            sigmoid_done = sem("sigmoid_done")
            half_free = sem("half_free")
            pool_step = sem("pool_step")
            up_ready = sem("up_ready")
            hidden_ready = sem("hidden_ready")
            down_done = sem("down_done")
            banks = sems.enter_context(nc.psum_tensor("down_banks", [P, 8, CH], F32))
            block = sems.enter_context(nc.Block())

            @block.vector
            def _(dve):
                chain = Chain(dve, step)

                def scales(lo, hi, number):
                    chain.step(dve.tensor_reduce(peak_one[:, lo:hi], peak[:, lo:hi, :], AX.X, ALU.max))
                    dve.tensor_scalar(peak_one[:, lo:hi], peak_one[:, lo:hi], 1.0 / A_QMAX, SCALE_FLOOR,
                                      ALU.mult, ALU.max).then_inc(peaks_ready, 1)
                    dve.wait_ge(peaks_all, number)
                    dve.reciprocal(inverse[:, lo:hi], scale[:, lo:hi]).then_inc(scales_ready, 1)
                    dve.wait_ge(scales_ready, number)

                def quantise(x, a):
                    chain.step(dve.tensor_scalar(x, x, inverse[:, a:a + 1], MAGIC, ALU.mult, ALU.add))
                    return dve.tensor_scalar(x, x, MAGIC, scale[:, a:a + 1], ALU.subtract, ALU.mult)

                scales(1, 3, 1)
                for i in range(FC + 1):
                    if i < FC:
                        quantise(gate[:, i, :], 1).then_inc(gate_ready, 1)
                    if i:
                        g, h = gate[:, i - 1, :], half[:, (i - 1) % 3, :]
                        dve.wait_ge(sigmoid_done, i)
                        chain.step(dve.tensor_scalar(h, h, 65536.0, MAGIC, ALU.mult, ALU.add))
                        chain.step(dve.tensor_scalar(h, h, MAGIC, 65535.0, ALU.subtract, ALU.min))
                        dve.scalar_tensor_tensor(out=g, in0=h, scalar=1.0 / 65536.0, in1=g, op0=ALU.mult,
                                                 op1=ALU.mult).then_inc(half_free, 1)
                        dve.wait_ge(half_free, i)
                        chain(dve.tensor_reduce(peak[:, 3, i - 1:i], g, AX.X, ALU.max, apply_absolute_value=True))
                chain.wait()
                scales(3, 4, 2)
                for i in range(FC):
                    g = gate[:, i, :]
                    chain.step(quantise(g, 3))
                    dve.wait_ge(up_ready, i + 1)
                    chain.step(dve.tensor_tensor(g, g, up[:, i, :], ALU.mult))
                    chain(dve.tensor_reduce(peak[:, 4, i:i + 1], g, AX.X, ALU.max, apply_absolute_value=True))
                chain.wait()
                scales(4, 5, 3)
                for i in range(FC):
                    quantise(gate[:, i, :], 4).then_inc(hidden_ready, 1)
                for q in range(NT // 2):
                    dve.wait_ge(down_done, q + 1)
                    dve.tensor_tensor(R[:, 2 * q:2 * q + 2, :].rearrange("p a b -> p (a b)"), banks[:, q, :],
                                      X[:, 2 * q:2 * q + 2, :].rearrange("p a b -> p (a b)"), ALU.add)

            @block.gpsimd
            def _(pool):
                def reduce_all(lo, hi, number):
                    pool.wait_ge(peaks_ready, number)
                    pool.partition_all_reduce(scale[:, lo:hi], peak_one[:, lo:hi], P,
                                              bass.bass_isa.ReduceOp.max).then_inc(peaks_all, 1)

                reduce_all(1, 3, 1)
                pool.wait_ge(scales_ready, 1)
                for i in range(FC):
                    u = up[:, i, :]
                    pool.tensor_scalar(u, u, inverse[:, 2:3], MAGIC, ALU.mult, ALU.add).then_inc(pool_step, 1)
                    pool.wait_ge(pool_step, i + 1)
                    pool.tensor_scalar(u, u, -MAGIC, scale[:, 2:3], ALU.add, ALU.mult).then_inc(up_ready, 1)
                reduce_all(3, 4, 2)
                reduce_all(4, 5, 3)

            @block.scalar
            def _(act):
                for i in range(FC):
                    act.wait_ge(gate_ready, i + 1)
                    if i >= 3:
                        act.wait_ge(half_free, i - 2)
                    act.activation(half[:, i % 3, :], gate[:, i, :], ACT.Sigmoid).then_inc(sigmoid_done, 1)

            @block.tensor
            def _(pe):
                pe.wait_ge(hidden_ready, FC)
                for t in range(NT):
                    for i in range(FC):
                        last = pe.matmul(banks[:, t // 2, (t % 2) * D:(t % 2 + 1) * D], gate[:, i, t * P:(t + 1) * P],
                                         down_turned[:, i, :], start=(i == 0), stop=(i == FC - 1))
                    if t % 2:
                        last.then_inc(down_done, 1)



RH = 4
DK = D // RH
DV = 2 * D // RH
HALF = DK // 2
QK = 2 * D
VW = 2 * D
GAMMA = [1.0 - 2.0 ** (-5.0 - h) for h in range(RH)]
CHUNK_DECAY = [g ** P for g in GAMMA]


def retention(nc, ident, io, X, R):
    with ExitStack() as ctx:
        def sb(name, shape, dt=F32):
            return ctx.enter_context(nc.sbuf_tensor(name, shape, dt))

        qk = sb("ret_qk", [P, NT, QK])
        values = sb("ret_values", [P, NT, VW])
        gates = sb("ret_gates", [P, NT, VW])
        w_out = sb("ret_w_out", [P, RH, D])
        norm_w = sb("ret_norm_w", [P, 1])
        decay = sb("ret_decay", [P, RH, P])
        cross = sb("ret_cross", [P, RH])
        key_decay = sb("ret_key_decay", [P, RH])
        mean_square = sb("ret_mean_square", [P, NT, RH])
        with ExitStack() as inner:
            def isb(name, shape, dt=F32):
                return inner.enter_context(nc.sbuf_tensor(name, shape, dt))

            turned = isb("ret_x_turned", [P, DC, T])
            w_all = isb("ret_w_all", [P, DC, 3, CH])
            affine = isb("ret_affine", [P, 2, DC])
            rope = isb("ret_rope", [P, 2, NT, HALF])
            products = isb("ret_products", [P, 2, 2, QK])
            sigmoids = isb("ret_sigmoids", [P, 2, VW])

            def rows(name):
                return io[name].rearrange("(c p) n -> p c n", p=P)

            with nc.allow_non_contiguous_dma(reason="vectors of 256 values"):
                load_block(nc, [
                    (w_all[:, :, 0, 0:D], rows("L1_attn_Wq")), (w_all[:, :, 0, D:QK], rows("L1_attn_Wk")),
                    (w_all[:, :, 1, :], rows("L1_attn_Wv")), (w_all[:, :, 2, :], rows("L1_attn_Wg")),
                    (w_out[:], io["L1_attn_Wo"].rearrange("(h p) n -> p h n", p=P)),
                    (affine[:, 0, :], io["L1_attn_ln_w"].rearrange("(c p) -> p c", p=P)),
                    (affine[:, 1, :], io["L1_attn_ln_b"].rearrange("(c p) -> p c", p=P)),
                    (norm_w[:], io["L1_attn_g_norm_w"].rearrange("(p a) -> p a", a=1)),
                    (rope[:], io["const_rope"]), (decay[:], io["const_decay"]), (cross[:], io["const_cross"]),
                    (key_decay[:], io["const_key_decay"]),
                ])
            norm_block(nc, "ret_norm", ident, X, R, NT, P, True, turned=turned, gain=affine[:, 0, :],
                       shift=affine[:, 1, :])

            with ExitStack() as sems:
                def sem(name):
                    return sems.enter_context(semaphore(nc, name))

                projected = sem("ret_projected")
                multiplied = sem("ret_multiplied")
                rotated = sem("ret_rotated")
                values_out = sem("ret_values_out")
                sigmoid_out = sem("ret_sigmoid_out")
                gates_out = sem("ret_gates_out")
                banks = sems.enter_context(nc.psum_tensor("ret_banks", [P, 2, 3, CH], F32))
                block = sems.enter_context(nc.Block())

                @block.tensor
                def _(pe):
                    for t in range(NT):
                        if t >= 2:
                            pe.wait_ge(gates_out, t - 1)
                            pe.wait_ge(sigmoid_out, t - 1)
                            pe.wait_ge(values_out, t - 1)
                            pe.wait_ge(multiplied, t - 1)
                        for w in range(3):
                            for k in range(DC):
                                last = pe.matmul(banks[:, t % 2, w, :], turned[:, k, t * P:(t + 1) * P],
                                                 w_all[:, k, w, :], start=(k == 0), stop=(k == DC - 1))
                        last.then_inc(projected, 1)

                @block.scalar
                def _(act):
                    for t in range(NT):
                        act.wait_ge(projected, t + 1)
                        act.activation(values[:, t, :], banks[:, t % 2, 1, :], ACT.Copy).then_inc(values_out, 1)
                        if t >= 2:
                            act.wait_ge(gates_out, t - 1)
                        act.activation(sigmoids[:, t % 2, :], banks[:, t % 2, 2, :], ACT.Sigmoid).then_inc(sigmoid_out, 1)

                @block.vector
                def _(dve):
                    for t in range(NT):
                        dve.wait_ge(projected, t + 1)
                        if t >= 2:
                            dve.wait_ge(rotated, t - 1)
                        for f in range(2):
                            last = dve.tensor_tensor(
                                products[:, t % 2, f, :].rearrange("p (h j) -> p h j", j=HALF),
                                banks[:, t % 2, 0, :].rearrange("p (h j) -> p h j", j=HALF),
                                spread(rope[:, f, t, :], 1, QK // HALF), ALU.mult)
                        last.then_inc(multiplied, 1)
                        dve.wait_ge(sigmoid_out, t + 1)
                        dve.tensor_tensor(gates[:, t, :], banks[:, t % 2, 2, :], sigmoids[:, t % 2, :],
                                          ALU.mult).then_inc(gates_out, 1)

                @block.gpsimd
                def _(pool):
                    for t in range(NT):
                        pool.wait_ge(multiplied, t + 1)
                        cos_x, sin_x = (products[:, t % 2, f, :].rearrange("p (h u j) -> p h u j", u=2, j=HALF)
                                        for f in range(2))
                        out = qk[:, t, :].rearrange("p (h u j) -> p h u j", u=2, j=HALF)
                        pool.tensor_tensor(out[:, :, 0], cos_x[:, :, 0], sin_x[:, :, 1], ALU.subtract)
                        pool.tensor_tensor(out[:, :, 1], cos_x[:, :, 1], sin_x[:, :, 0], ALU.add).then_inc(rotated, 1)

        with ExitStack() as sems:
            def sem(name):
                return sems.enter_context(semaphore(nc, name))

            def isb(name, shape, dt=F32):
                return sems.enter_context(nc.sbuf_tensor(name, shape, dt))

            qk_turned = isb("ret_qk_turned", [DK, 2, 2 * RH, P])
            decayed = isb("ret_decayed", [P, 2, RH, P])
            keys_decayed = isb("ret_keys_decayed", [P, 2, RH, DK])
            state = isb("ret_state", [DK, RH, DV])
            squares = isb("ret_squares", [P, 2, VW])
            turned_banks = sems.enter_context(nc.psum_tensor("ret_turned", [DK, 2 * RH, P], F32))
            score_banks = sems.enter_context(nc.psum_tensor("ret_scores", [P, 2, RH, P], F32))
            out_banks = sems.enter_context(nc.psum_tensor("ret_out", [P, 2, RH, DV], F32))
            state_bank = sems.enter_context(nc.psum_tensor("ret_state_bank", [DK, RH, DV], F32))
            qk_transposed = sem("ret_qk_transposed")
            turned_copied = sem("ret_turned_copied")
            scored = sem("ret_scored")
            decayed_out = sem("ret_decayed_out")
            keys_out = sem("ret_keys_out")
            chunk_out = sem("ret_chunk_out")
            state_out = sem("ret_state_out")
            state_in = sem("ret_state_in")
            head_out = sem("ret_head_out")
            squared = sem("ret_squared")
            reduced = sem("ret_reduced")
            block = sems.enter_context(nc.Block())

            @block.tensor
            def _(pe):
                def turn(t):
                    if t:
                        pe.wait_ge(turned_copied, t)
                    for b in range(2 * RH):
                        last = pe.transpose(turned_banks[:, b, :], qk[:, t, b * DK:(b + 1) * DK], ident[:])
                    last.then_inc(qk_transposed, 1)

                def score(t):
                    pe.wait_ge(turned_copied, t + 1)
                    if t >= 2:
                        pe.wait_ge(decayed_out, t - 1)
                    for h in range(RH):
                        last = pe.matmul(score_banks[:, t % 2, h, :], qk_turned[:, t % 2, RH + h, :],
                                         qk_turned[:, t % 2, h, :], start=True, stop=True)
                    last.then_inc(scored, 1)

                turn(0)
                score(0)
                for t in range(NT):
                    if t + 1 < NT:
                        turn(t + 1)
                        score(t + 1)
                    pe.wait_ge(decayed_out, t + 1)
                    if t >= 2:
                        pe.wait_ge(head_out, t - 1)
                    if t:
                        pe.wait_ge(state_in, t)
                    for h in range(RH):
                        out = out_banks[:, t % 2, h, :]
                        last = pe.matmul(out, decayed[:, t % 2, h, :], values[:, t, h * DV:(h + 1) * DV],
                                         start=True, stop=(t == 0))
                        if t:
                            last = pe.matmul(out, qk_turned[:, t % 2, h, :], state[:, h, :],
                                             start=False, stop=True)
                    last.then_inc(chunk_out, 1)
                    if t + 1 < NT:
                        pe.wait_ge(keys_out, t + 1)
                        for h in range(RH):
                            last = pe.matmul(state_bank[:, h, :], keys_decayed[:, t % 2, h, :],
                                             values[:, t, h * DV:(h + 1) * DV], start=True, stop=True)
                        last.then_inc(state_out, 1)

            @block.scalar
            def _(act):
                for t in range(NT + 1):
                    if t < NT:
                        act.wait_ge(qk_transposed, t + 1)
                        if t >= 2:
                            act.wait_ge(chunk_out, t - 1)
                        act.activation(qk_turned[:, t % 2].rearrange("p b n -> p (b n)"),
                                       turned_banks[:].rearrange("p b n -> p (b n)"), ACT.Copy).then_inc(turned_copied, 1)
                    if t:
                        u = t - 1
                        act.wait_ge(head_out, u + 1)
                        if u >= 2:
                            act.wait_ge(reduced, u - 1)
                        act.activation(squares[:, u % 2, :], qk[:, u, :], ACT.Square).then_inc(squared, 1)

            @block.gpsimd
            def _(pool):
                for t in range(NT - 1):
                    if t >= 2:
                        pool.wait_ge(state_out, t - 1)
                    pool.tensor_tensor(keys_decayed[:, t % 2], qk[:, t, D:QK].rearrange("p (h d) -> p h d", h=RH),
                                       spread(key_decay[:], 2, DK), ALU.mult).then_inc(keys_out, 1)

            @block.vector
            def _(dve):
                def decay_scores(t):
                    dve.wait_ge(scored, t + 1)
                    if t >= 2:
                        dve.wait_ge(chunk_out, t - 1)
                    dve.tensor_tensor(decayed[:, t % 2], score_banks[:, t % 2], decay[:], ALU.mult).then_inc(decayed_out, 1)

                decay_scores(0)
                for t in range(NT):
                    if t + 1 < NT:
                        decay_scores(t + 1)
                        dve.wait_ge(state_out, t + 1)
                        if t == 0:
                            dve.tensor_copy(state[:], state_bank[:]).then_inc(state_in, 1)
                        else:
                            for h in range(RH):
                                last = dve.scalar_tensor_tensor(
                                    out=state[:, h, :], in0=state[:, h, :], scalar=CHUNK_DECAY[h],
                                    in1=state_bank[:, h, :], op0=ALU.mult, op1=ALU.add)
                            last.then_inc(state_in, 1)
                    dve.wait_ge(chunk_out, t + 1)
                    if t + 1 < NT:
                        dve.wait_ge(keys_out, t + 1)
                    dve.tensor_tensor(qk[:, t, :].rearrange("p (h d) -> p h d", h=RH), out_banks[:, t % 2],
                                      spread(cross[:], 2, DV), ALU.mult).then_inc(head_out, 1)
                    if t:
                        dve.wait_ge(squared, t)
                        dve.tensor_reduce(mean_square[:, t - 1, :], squares[:, (t - 1) % 2].rearrange(
                            "p (h d) -> p h d", h=RH), AX.X, ALU.add).then_inc(reduced, 1)
                dve.wait_ge(squared, NT)
                dve.tensor_reduce(mean_square[:, NT - 1, :], squares[:, (NT - 1) % 2].rearrange(
                    "p (h d) -> p h d", h=RH), AX.X, ALU.add).then_inc(reduced, 1)

        with ExitStack() as sems:
            def sem(name):
                return sems.enter_context(semaphore(nc, name))

            out_turned = sems.enter_context(nc.sbuf_tensor("ret_out_turned", [P, 2, CH], F32))
            inverse = sems.enter_context(nc.sbuf_tensor("ret_inverse", [P, NT, RH], F32))
            step = sem("ret_norm_step")
            variance = sem("ret_variance")
            rooted = sem("ret_rooted")
            normed = sem("ret_normed")
            gated = sem("ret_gated")
            w_scaled = sem("ret_w_scaled")
            heads_turned = sem("ret_heads_turned")
            heads_copied = sem("ret_heads_copied")
            out_done = sem("ret_out_done")
            summed = sem("ret_summed")
            turned_banks = sems.enter_context(nc.psum_tensor("ret_heads_banks", [P, 2, CH], F32))
            out_banks = sems.enter_context(nc.psum_tensor("ret_proj_banks", [P, 2, CH], F32))
            block = sems.enter_context(nc.Block())

            @block.vector
            def _(dve):
                chain = Chain(dve, step)
                dve.tensor_scalar(mean_square[:], mean_square[:], 1.0 / DV, EPS, ALU.mult, ALU.add).then_inc(variance, 1)
                for h in range(RH):
                    last = dve.tensor_scalar(w_out[:, h, :], w_out[:, h, :], norm_w[:, 0:1], None, ALU.mult)
                last.then_inc(w_scaled, 1)
                dve.wait_ge(rooted, 1)
                chain.step(dve.reciprocal(inverse[:], mean_square[:]))
                for t in range(NT + 2):
                    if t < NT:
                        heads = qk[:, t, :].rearrange("p (h d) -> p h d", h=RH)
                        dve.tensor_tensor(heads, heads, spread(inverse[:, t, :], 2, DV), ALU.mult).then_inc(normed, 1)
                    if t >= 2:
                        u = t - 2
                        dve.wait_ge(out_done, u + 1)
                        dve.scalar_tensor_tensor(out=R[:, u, :], in0=X[:, u, :], scalar=2.0,
                                                 in1=out_banks[:, u % 2, 0:D], op0=ALU.mult, op1=ALU.add).then_inc(summed, 1)

            @block.gpsimd
            def _(pool):
                for t in range(NT):
                    pool.wait_ge(normed, t + 1)
                    pool.tensor_tensor(qk[:, t, :], qk[:, t, :], gates[:, t, :], ALU.mult).then_inc(gated, 1)

            @block.scalar
            def _(act):
                act.wait_ge(variance, 1)
                act.activation(mean_square[:], mean_square[:], ACT.Sqrt).then_inc(rooted, 1)
                for t in range(NT):
                    act.wait_ge(heads_turned, t + 1)
                    if t >= 2:
                        act.wait_ge(out_done, t - 1)
                    act.activation(out_turned[:, t % 2, :], turned_banks[:, t % 2, :], ACT.Copy).then_inc(heads_copied, 1)

            @block.tensor
            def _(pe):
                pe.wait_ge(w_scaled, 1)
                for t in range(NT + 1):
                    if t < NT:
                        pe.wait_ge(gated, t + 1)
                        if t >= 2:
                            pe.wait_ge(heads_copied, t - 1)
                        for h in range(RH):
                            last = pe.transpose(turned_banks[:, t % 2, h * P:(h + 1) * P], qk[:, t, h * DV:(h + 1) * DV],
                                                ident[:])
                        last.then_inc(heads_turned, 1)
                    if t:
                        u = t - 1
                        pe.wait_ge(heads_copied, u + 1)
                        if u >= 2:
                            pe.wait_ge(summed, u - 1)
                        for h in range(RH):
                            last = pe.matmul(out_banks[:, u % 2, 0:D], out_turned[:, u % 2, h * P:(h + 1) * P],
                                             w_out[:, h, :], start=(h == 0), stop=(h == RH - 1))
                        last.then_inc(out_done, 1)


def retention_constants():
    f4 = np.float32
    inv_freq = (f4(1) / f4(10000) ** (np.arange(0, DK, 2, dtype=f4) / f4(DK))).astype(f4)
    angles = np.arange(T, dtype=f4)[:, None] * inv_freq[None, :]
    rope = np.stack([np.cos(angles), np.sin(angles)]).astype(f4).reshape(2, NT, P, HALF).transpose(2, 0, 1, 3)
    gamma = np.array(GAMMA)
    i = np.arange(P)
    decay = np.where(i[None, None, :] >= i[:, None, None], gamma[None, :, None] ** -(1.0 + i[:, None, None]), 0.0)
    cross = gamma[None, :] ** (i[:, None] + 1.0) * DK ** -0.5
    key_decay = gamma[None, :] ** (P - 1.0 - i[:, None])
    return {"const_rope": np.ascontiguousarray(rope), "const_decay": decay.astype(f4), "const_cross": cross.astype(f4),
            "const_key_decay": key_decay.astype(f4)}


BF16 = mybir.dt.bfloat16
I16 = mybir.dt.int16
BF16_ONE = 0x3F80


E = 16
EG = 4
GS = E // EG
EI = 128
SC = 4
UNITS = E + SC
TOP_K = 4
TOPK_GROUP = 2
ROUTED_SCALING = 2.5


def experts_ffn(nc, ident, io, X, R):
    with ExitStack() as ctx:
        def sb(name, shape, dt=F32):
            return ctx.enter_context(nc.sbuf_tensor(name, shape, dt))

        x_turned = sb("moe_x_turned", [P, DC, T])
        w_up = sb("moe_w_up", [P, UNITS, DC, EI])
        w_down = sb("moe_w_down", [P, UNITS, D])
        combine = sb("moe_combine", [P, T], BF16)
        pick = sb("moe_pick", [P, E, EI], BF16)
        with ExitStack() as sems:
            def isb(name, shape, dt=F32):
                return sems.enter_context(nc.sbuf_tensor(name, shape, dt))

            gate_rows = isb("moe_gate_rows", [E, D])
            gate_turned = isb("moe_gate_turned", [P, DC, E])
            earlier = isb("moe_earlier", [P, E, E])
            load_block(nc, [
                (gate_rows[:], io["L1_ffn_gate_weight"]), (earlier[:], io["const_earlier"]), (pick[:].bitcast(I16), io["const_pick"]),
                (w_up[:, 0:E], io["L1_ffn_expert_up"].rearrange("e (c p) n -> p e c n", p=P)),
                (w_down[:, 0:E, :], io["L1_ffn_expert_down"].rearrange("e p n -> p e n")),
            ] + [(w_up[:, E + s], io["L1_ffn_shared_up"].rearrange("(c p) (s n) -> p s c n", p=P, n=EI)[:, s])
                 for s in range(SC)]
                + [(w_down[:, E:UNITS, :], io["L1_ffn_shared_down"].rearrange("(s p) n -> p s n", p=P))])
            norm_block(nc, "moe_turn", ident, X, X, NT, P, False, turned=x_turned)

            scores = isb("moe_scores", [P, NT, E])
            masked = isb("moe_masked", [P, NT, E])
            chosen = isb("moe_chosen", [P, NT, E])
            compare = isb("moe_compare", [P, NT, E, E])
            ties = isb("moe_ties", [P, NT, E, E])
            rank = isb("moe_rank", [P, NT, E])
            group_score = isb("moe_group_score", [P, NT, EG])
            total = isb("moe_total", [P, NT])
            rest = isb("moe_rest", [E, 2, T])
            banks = sems.enter_context(nc.psum_tensor("moe_route_banks", [P, 8, CH], F32))

            def sem(name):
                return sems.enter_context(semaphore(nc, name))

            gate_done = sem("moe_gate_done")
            gate_copied = sem("moe_gate_copied")
            logits_done = sem("moe_logits_done")
            scores_done = sem("moe_scores_done")
            step = sem("moe_route_step")
            combined = sem("moe_combined")
            combine_turned = sem("moe_combine_turned")
            block = sems.enter_context(nc.Block())

            @block.tensor
            def _(pe):
                for c in range(DC):
                    last = pe.transpose(banks[:, 0, c * E:(c + 1) * E], gate_rows[:, c * P:(c + 1) * P], ident[0:E, 0:E])
                last.then_inc(gate_done, 1)
                pe.wait_ge(gate_copied, 1)
                for t in range(NT):
                    for c in range(DC):
                        last = pe.matmul(banks[:, 1, t * E:(t + 1) * E], x_turned[:, c, t * P:(t + 1) * P],
                                         gate_turned[:, c, :], start=(c == 0), stop=(c == DC - 1))
                last.then_inc(logits_done, 1)
                pe.wait_ge(combined, 1)
                for t in range(NT):
                    last = pe.transpose(banks[0:E, 4 + t // 4, (t % 4) * P:(t % 4 + 1) * P], masked[:, t, :], ident[:])
                last.then_inc(combine_turned, 1)

            @block.scalar
            def _(act):
                act.wait_ge(gate_done, 1)
                act.activation(gate_turned[:].rearrange("p c e -> p (c e)"), banks[:, 0, 0:DC * E], ACT.Copy).then_inc(gate_copied, 1)
                act.wait_ge(logits_done, 1)
                act.activation(scores[:].rearrange("p t e -> p (t e)"), banks[:, 1, 0:NT * E], ACT.Sigmoid).then_inc(scores_done, 1)

            @block.vector
            def _(dve):
                chain = Chain(dve, step)

                def select(values, n, k, count, out):
                    def square(ap):
                        return ap.rearrange("p t e j -> p (t e j)")[:, 0:n * k * k].rearrange(
                            "p (n a b) -> p n a b", a=k, b=k)
                    larger, equal = square(compare[:]), square(ties[:])
                    other, own = spread(values, 2, k), spread(values, 3, k)
                    chain(dve.tensor_tensor(larger, other, own, ALU.is_gt))
                    chain.step(dve.tensor_tensor(equal, other, own, ALU.is_equal))
                    before = spread(earlier[:, 0:k, 0:k], 1, n)
                    chain.step(dve.tensor_tensor(equal, equal, before, ALU.mult))
                    chain.step(dve.tensor_tensor(larger, larger, equal, ALU.add))
                    ranks = rank[:].rearrange("p t e -> p (t e)")[:, 0:n * k].rearrange("p (n e) -> p n e", e=k)
                    chain.step(dve.tensor_reduce(ranks, larger, AX.X, ALU.add))
                    chain.step(dve.tensor_scalar(out, ranks, float(count), None, ALU.is_lt))

                dve.wait_ge(scores_done, 1)
                by_group = scores[:].rearrange("p t (g s) -> p (t g) s", s=GS)
                chosen_by_group = chosen[:].rearrange("p t (g s) -> p (t g) s", s=GS)
                select(by_group, NT * EG, GS, 2, chosen_by_group)
                chain.step(dve.tensor_tensor(chosen[:], chosen[:], scores[:], ALU.mult))
                chain.step(dve.tensor_reduce(group_score[:].rearrange("p t g -> p (t g)"), chosen_by_group, AX.X, ALU.add))
                group_chosen = masked[:, :, 0:EG]
                select(group_score[:], NT, EG, TOPK_GROUP, group_chosen)
                chain.step(dve.tensor_copy(group_score[:], group_chosen))
                chain.step(dve.tensor_tensor(masked[:].rearrange("p t (g s) -> p (t g) s", s=GS), by_group,
                                             spread(group_score[:].rearrange("p t g -> p (t g)"), 2, GS), ALU.mult))
                select(masked[:], NT, E, TOP_K, chosen[:])
                chain.step(dve.tensor_tensor(chosen[:], chosen[:], scores[:], ALU.mult))
                chain.step(dve.tensor_reduce(total[:], chosen[:], AX.X, ALU.add))
                chain.step(dve.tensor_scalar(total[:], total[:], 1e-20, None, ALU.add))
                chain.step(dve.reciprocal(total[:], total[:]))
                chain.step(dve.tensor_tensor(chosen[:], chosen[:], spread(total[:], 2, E), ALU.mult))
                chain(dve.memset(combine[:], 0.0))
                dve.tensor_scalar(masked[:], chosen[:], ROUTED_SCALING, None, ALU.mult).then_inc(combined, 1)
                dve.wait_ge(combine_turned, 1)
                chain.wait()
                turned = banks[0:E, 4:8, :].rearrange("p b n -> p (b n)")
                chain.step(dve.tensor_copy(combine[0:E, :], turned))
                chain.step(dve.tensor_tensor(rest[:, 0, :], turned, combine[0:E, :], ALU.subtract))
                chain.step(dve.tensor_copy(combine[32:32 + E, :], rest[:, 0, :]))
                chain.step(dve.tensor_copy(rest[:, 1, :], combine[32:32 + E, :]))
                chain.step(dve.tensor_tensor(rest[:, 1, :], rest[:, 0, :], rest[:, 1, :], ALU.subtract))
                dve.tensor_copy(combine[64:64 + E, :], rest[:, 1, :])

        with ExitStack() as sems:
            def sem(name):
                return sems.enter_context(semaphore(nc, name))

            def isb(name, shape, dt=F32):
                return sems.enter_context(nc.sbuf_tensor(name, shape, dt))

            sigmoids = isb("moe_sigmoids", [P, 2, CH])
            hidden = isb("moe_hidden", [P, 2, CH])
            out_rows = isb("moe_out_rows", [P, DC, CH])
            up_banks = sems.enter_context(nc.psum_tensor("moe_up_banks", [P, 2, CH], F32))
            weight_banks = sems.enter_context(nc.psum_tensor("moe_weight_banks", [P, 2, CH], F32))
            out_banks = sems.enter_context(nc.psum_tensor("moe_out_banks", [P, DC, CH], F32))
            turned_banks = sems.enter_context(nc.psum_tensor("moe_turned_banks", [P, DC, CH], F32))
            up_done = sem("moe_up_done")
            sigmoid_done = sem("moe_sigmoid_done")
            gated = sem("moe_gated")
            hidden_done = sem("moe_hidden_done")
            down_done = sem("moe_down_done")
            out_copied = sem("moe_out_copied")
            out_turned = sem("moe_out_turned")
            summed = sem("moe_summed")
            block = sems.enter_context(nc.Block())

            @block.tensor
            def _(pe):
                pe.sem_inc(down_done, 2)
                with pe.Fori(0, NC_T, 1) as n:
                    def up(u):
                        pe.wait_ge(hidden_done, n * UNITS + (u + 1))
                        for k in range(DC):
                            last = pe.matmul(up_banks[:, u % 2, :], w_up[:, u, k, :], x_turned[:, k, bass.ds(n * CH, CH)],
                                             start=(k == 0), stop=(k == DC - 1))
                        if u < E:
                            last = pe.matmul(weight_banks[:, u % 2, :], pick[:, u, :], combine[:, bass.ds(n * CH, CH)],
                                             start=True, stop=True)
                        last.then_inc(up_done, 1)

                    up(0)
                    for u in range(UNITS):
                        if u + 1 < UNITS:
                            up(u + 1)
                        if u == 0:
                            pe.wait_ge(out_copied, n + 1)
                        pe.wait_ge(hidden_done, n * UNITS + (u + 3))
                        for c in range(DC):
                            last = pe.matmul(out_banks[:, c, :], w_down[:, u, c * P:(c + 1) * P], hidden[:, u % 2, :],
                                             start=(u == 0), stop=(u == UNITS - 1))
                        last.then_inc(down_done, 1)
                    pe.wait_ge(out_copied, n + 2)
                    pe.wait_ge(summed, n + 1)
                    for j in range(4):
                        for c in range(DC):
                            last = pe.transpose(turned_banks[:, j // 2, ((j % 2) * DC + c) * P:((j % 2) * DC + c + 1) * P],
                                                out_rows[:, c, j * P:(j + 1) * P], ident[:])
                    last.then_inc(out_turned, 1)

            @block.scalar
            def _(act):
                act.sem_inc(out_copied, 1)
                with act.Fori(0, NC_T, 1) as n:
                    for u in range(UNITS):
                        act.wait_ge(up_done, n * UNITS + (u + 1))
                        act.wait_ge(hidden_done, n * UNITS + (u + 1))
                        act.activation(sigmoids[:, u % 2, :], up_banks[:, u % 2, :], ACT.Sigmoid).then_inc(sigmoid_done, 1)
                    act.wait_ge(down_done, n * UNITS + (UNITS + 2))
                    act.wait_ge(summed, n + 1)
                    for c in range(DC):
                        last = act.activation(out_rows[:, c, :], out_banks[:, c, :], ACT.Copy)
                    last.then_inc(out_copied, 1)

            @block.vector
            def _(dve):
                dve.sem_inc(hidden_done, 2)
                dve.sem_inc(summed, 1)
                with dve.Fori(0, NC_T, 1) as n:
                    for u in range(UNITS):
                        dve.wait_ge(sigmoid_done, n * UNITS + (u + 1))
                        dve.wait_ge(down_done, n * UNITS + (u + 1))
                        s = sigmoids[:, u % 2, :]
                        if u < E:
                            dve.tensor_tensor(s, up_banks[:, u % 2, :], s, ALU.mult).then_inc(gated, 1)
                            dve.wait_ge(gated, n * E + (u + 1))
                            dve.tensor_tensor(hidden[:, u % 2, :], weight_banks[:, u % 2, :], s, ALU.mult).then_inc(hidden_done, 1)
                        else:
                            dve.tensor_tensor(hidden[:, u % 2, :], up_banks[:, u % 2, :], s, ALU.mult).then_inc(hidden_done, 1)
                    dve.wait_ge(out_turned, n + 1)
                    for b in range(2):
                        last = dve.tensor_tensor(R[:, bass.ds(n * 4 + 2 * b, 2), :].rearrange("p a b -> p (a b)"),
                                                 turned_banks[:, b, :],
                                                 X[:, bass.ds(n * 4 + 2 * b, 2), :].rearrange("p a b -> p (a b)"), ALU.add)
                    last.then_inc(summed, 1)


def expert_constants():
    e = np.arange(E)
    earlier = np.broadcast_to((e[None, :] < e[:, None]).astype(np.float32), (P, E, E))
    row = np.arange(P)
    pick = np.where((row[:, None] % 32 == e[None, :]) & (row[:, None] < 96), BF16_ONE, 0).astype(np.int16)
    return {"const_earlier": np.ascontiguousarray(earlier),
            "const_pick": np.ascontiguousarray(np.broadcast_to(pick[:, :, None], (P, E, EI)))}



XH = 16
XD = D // XH
PAIRS = XH // 2
NEG = -1e9
S_CH = [(n * CH, min(CH, S2 - n * CH)) for n in range((S2 + CH - 1) // CH)]
KEY_ROWS = [P] * (CT - 1) + [CLAST]
LT = 3
L_SLOTS = 4
PT_SLOTS = 8
BY_SCALAR = (1, 3, 5, 7, 9, 11, 13)


def masked_attention(nc, ident, io, X, scratch):
    q_parts = nc.dram_tensor("xa_q_parts", (2, D, T), F16, kind="Internal").ap()
    k_parts = nc.dram_tensor("xa_k_parts", (2, D, S2), F16, kind="Internal").ap()
    with ExitStack() as ctx:
        def sb(name, shape, dt=F32):
            return ctx.enter_context(nc.sbuf_tensor(name, shape, dt))

        k_stack = sb("xa_k_stack", [P, PAIRS, S2], F16)
        q_stack = sb("xa_q_stack", [P, 2, XH, P], F16)
        v = sb("xa_v", [P, CT, D + XD])
        w_out = sb("xa_w_out", [P, DC, D])
        k_rows, q_rows = (1, 1, 0, 0), (1, 0, 1, 0)

        with ExitStack() as inner:
            def isb(name, shape, dt=F32):
                return inner.enter_context(nc.sbuf_tensor(name, shape, dt))

            def sem(name):
                return inner.enter_context(semaphore(nc, name))

            context = isb("xa_context", [P, CT, D])
            c_turned = isb("xa_c_turned", [P, DC, S2])
            x_turned = isb("xa_x_turned", [P, DC, T])
            w = isb("xa_w", [P, 3, DC, D])
            bias = isb("xa_bias", [P, 2, DC])
            v_bias = isb("xa_v_bias", [P, D])
            out_bias = isb("xa_out_bias", [P, D])
            parts = isb("xa_parts", [P, 2, DC, T], F16)
            ctx_rows = io["ctx_1024"].rearrange("a s d -> (a s) d")
            with nc.allow_non_contiguous_dma(reason="vectors of 256 values"):
                load_block(nc, [
                    (context[:, 0:CT - 1, :], ctx_rows[0:(CT - 1) * P].rearrange("(i p) d -> p i d", p=P)),
                    (context[0:CLAST, CT - 1, :], ctx_rows[(CT - 1) * P:S2]),
                    (w_out[:], io["L1_xattn_wo_k"].rearrange("(c p) n -> p c n", p=P)),
                    (v_bias[:], io["L1_xattn_wv_b"].rearrange("(a n) -> a n", a=1).broadcast_to([P, D])),
                    (out_bias[:], io["L1_xattn_wo_b"].rearrange("(a n) -> a n", a=1).broadcast_to([P, D])),
                ] + [(w[:, n], io[f"L1_xattn_w{x}_k"].rearrange("(c p) n -> p c n", p=P)) for n, x in enumerate("qkv")]
                    + [(bias[:, n, :], io[f"L1_xattn_w{x}_b"].rearrange("(c p) -> p c", p=P)) for n, x in enumerate("qk")])
            norm_block(nc, "xa_turn_x", ident, X, X, NT, P, False, turned=x_turned)
            norm_block(nc, "xa_turn_c", ident, context, context, CT, CLAST, False, turned=c_turned)

            projected = sem("xa_projected")
            high_out = sem("xa_high_out")
            low_out = sem("xa_low_out")
            v_out = sem("xa_v_out")
            cleared = sem("xa_cleared")
            kept = sem("xa_kept")
            banks = inner.enter_context(nc.psum_tensor("xa_prep_banks", [P, 4, CH], F32))
            v_banks = inner.enter_context(nc.psum_tensor("xa_v_banks", [P, 4, 2, D], F32))
            v_done = sem("xa_v_done")
            jobs = [(1, c, lo, n) for c in range(DC) for lo, n in S_CH]
            k_jobs = len(jobs)
            jobs += [(0, c, lo, CH) for c in range(DC) for lo in range(0, T, CH)]
            v_pairs = (CT + 1) // 2
            block = inner.enter_context(nc.Block())

            @block.tensor
            def _(pe):
                for j, (n, c, lo, width) in enumerate(jobs):
                    if j >= 4:
                        pe.wait_ge(low_out, j - 3)
                    src = x_turned if n == 0 else c_turned
                    for k in range(DC):
                        last = pe.matmul(banks[:, j % 4, 0:width], w[:, n, k, c * P:(c + 1) * P],
                                         src[:, k, lo:lo + width], start=(k == 0), stop=(k == DC - 1))
                    last.then_inc(projected, 1)
                for i in range(v_pairs):
                    if i >= 4:
                        pe.wait_ge(v_out, i - 3)
                    for t in range(2 * i, min(2 * i + 2, CT)):
                        n = KEY_ROWS[t]
                        for k in range(DC):
                            last = pe.matmul(v_banks[0:n, i % 4, t % 2, :], c_turned[:, k, t * P:t * P + n], w[:, 2, k, :],
                                             start=(k == 0), stop=(k == DC - 1))
                    last.then_inc(v_done, 1)

            @block.scalar
            def _(act):
                for j, (n, c, lo, width) in enumerate(jobs):
                    act.wait_ge(projected, j + 1)
                    if j == k_jobs:
                        act.wait_ge(kept, 16)
                    act.activation(parts[:, 0, c, lo:lo + width], banks[:, j % 4, 0:width], ACT.Identity,
                                   bias=bias[:, n, c:c + 1]).then_inc(high_out, 1)

            @block.vector
            def _(dve):
                for j, (n, c, lo, width) in enumerate(jobs):
                    dve.wait_ge(high_out, j + 1)
                    dve.scalar_tensor_tensor(out=parts[:, 1, c, lo:lo + width], in0=banks[:, j % 4, 0:width],
                                             scalar=bias[:, n, c:c + 1], in1=parts[:, 0, c, lo:lo + width],
                                             op0=ALU.add, op1=ALU.subtract).then_inc(low_out, 1)
                for i in range(v_pairs):
                    dve.wait_ge(v_done, i + 1)
                    members = range(2 * i, min(2 * i + 2, CT))
                    for t in members:
                        n = KEY_ROWS[t]
                        last = dve.tensor_tensor(v[0:n, t, 0:D], v_banks[0:n, i % 4, t % 2, :], v_bias[0:n, :], ALU.add)
                    last.then_inc(v_out, 1)

            @block.gpsimd
            def _(pool):
                pool.memset(v[:, :, D:D + XD], 0.0)
                pool.memset(q_stack[:], 0.0)
                pool.tensor_tensor(X[:], X[:], spread(out_bias[:], 1, NT), ALU.add)

            @block.sync
            def _(sync):
                sync.wait_ge(high_out, k_jobs)
                sync.wait_ge(low_out, k_jobs)
                sync.dma_start(k_parts.rearrange("u (c p) s -> p (u c) s", p=P),
                               parts[:, :, :, 0:S2].rearrange("p u c s -> p (u c) s")).then_inc(kept, 16)
                sync.wait_ge(low_out, len(jobs))
                sync.wait_ge(kept, 16)
                sync.dma_start(q_parts.rearrange("u (c p) s -> p (u c) s", p=P),
                               parts[:].rearrange("p u c s -> p (u c) s")).then_inc(kept, 16)
                sync.wait_ge(kept, 32)

        def stack_rows(parity, term):
            lo = 64 * parity + XD * term
            return slice(lo, lo + XD)

        load_block(nc, [(k_stack[stack_rows(parity, b)], k_parts[k_rows[b]].rearrange(
            "(i a j) s -> a j i s", a=2, j=XD)[parity]) for b in range(4) for parity in range(2)])

        with ExitStack() as inner:
            def isb(name, shape, dt=F32):
                return inner.enter_context(nc.sbuf_tensor(name, shape, dt))

            def sem(name):
                return inner.enter_context(semaphore(nc, name))

            negative = isb("xa_negative", [P, 2, S2])
            group = isb("xa_group", [P, 2, S2])
            group_turned = isb("xa_group_turned", [P, 2, CT, P])
            more_rows = isb("xa_more_rows", [P, 2, S2])
            spare = scratch[:].rearrange("p i d -> p (i d)")
            rows = [spare[:, 0:S2], spare[:, S2 + 7:2 * S2 + 7], more_rows[:, 0, :], more_rows[:, 1, :]]
            turned = isb("xa_probs_turned", [P, PT_SLOTS, CT, P])
            peaks = isb("xa_peaks", [P, 2 * XH])
            sums = isb("xa_sums", [P, 2, XH])
            inverse = isb("xa_inverse", [P, 2, XH])
            heads = isb("xa_heads", [P, 4, P])
            heads_normed = isb("xa_heads_normed", [P, D])
            heads_turned = isb("xa_heads_turned", [P, DC, P])
            gate = isb("xa_gate", [P, 4])
            score_banks = inner.enter_context(nc.psum_tensor("xa_score_banks", [P, 4 * CH], F32))
            turn_banks = inner.enter_context(nc.psum_tensor("xa_turn_banks", [P, 2, CH], F32))
            value_bank = inner.enter_context(nc.psum_tensor("xa_value_bank", [P, 4, P], F32))
            misc_bank = inner.enter_context(nc.psum_tensor("xa_misc_bank", [P, CH], F32))

            q_loaded = [sem(f"xa_q_loaded_{b}") for b in range(2)]
            mask_loaded = [sem(f"xa_mask_loaded_{b}") for b in range(2)]
            group_loaded = [sem(f"xa_group_loaded_{b}") for b in range(2)]
            negated = sem("xa_negated")
            mask_flipped = sem("xa_mask_flipped")
            scored = sem("xa_scored")
            logits_out = sem("xa_logits_out")
            exp_out = sem("xa_exp_out")
            weighted = sem("xa_weighted")
            bank_turned = [sem(f"xa_bank_turned_{b}") for b in range(2)]
            bank_moved = [sem(f"xa_bank_moved_{b}") for b in range(2)]
            group_valued = sem("xa_group_valued")
            heads_copied = sem("xa_heads_copied")
            misc_ready = sem("xa_misc_ready")
            misc_read = sem("xa_misc_read")
            inverted = sem("xa_inverted")
            gate_cleared = sem("xa_gate_cleared")
            block = inner.enter_context(nc.Block())

            n_pairs = NT // 2

            def await_(eng, semaphore, value):
                if not isinstance(value, int) or value > 0:
                    eng.wait_ge(semaphore, value)

            def back(j, u, lag):
                return (j, u - lag) if u >= lag else (j - 1, u - lag + 2 * XH)

            def by_scalar(u):
                return u % XH in BY_SCALAR

            def weighted_heads(j, u):
                return j * (2 * len(BY_SCALAR)) + sum(by_scalar(h) for h in range(u))

            def misc_number(j, u, k):
                if isinstance(j, int) and j == n_pairs:
                    return j * 14 + (1 + k) - 4
                return j * 14 + (7 * (u // XH) + 1 + k)

            class Step:

                def __init__(self, u, first, last, tail):
                    h = u % XH
                    self.head = not tail
                    self.turn = (not first or u >= LT) and (not tail or u < LT)
                    self.value = u % 4 == LT and (not first or u >= LT + 4) and (not tail or u == LT)
                    self.copy_heads = h == 3 and (not first or u >= XH)
                    self.finish = h - 4 if 4 <= h < 7 and (not first or u >= XH) else None
                    self.next_group = h - 8 if 8 <= h < 12 and not tail and not (last and u >= XH) else None

            def stream(eng, step):
                def pair(j, first=False, last=False):
                    for u in range(2 * XH):
                        step(j, u, Step(u, first, last, False))
                pair(0, first=True)
                with eng.Fori(1, n_pairs - 1, 1) as j:
                    pair(j)
                pair(n_pairs - 1, last=True)
                for u in range(7):
                    step(n_pairs, u, Step(u, False, False, True))

            def group_blocks(b):
                return [(i, KEY_ROWS[i]) for i in range(4 * b, min(4 * b + 4, CT))]

            @block.tensor
            def _(pe):
                def turn_group(tile, b):
                    for i, n in group_blocks(b):
                        last = pe.transpose(misc_bank[0:n, (i % 4) * P:(i % 4 + 1) * P], group[:, tile, i * P:i * P + n],
                                            ident[:])
                    last.then_inc(misc_ready, 1)

                def step(j, u, what):
                    tile, h = u // XH, u % XH
                    if what.head:
                        if h == 0:
                            pe.wait_ge(q_loaded[tile], j * 128 + 128)
                        await_(pe, logits_out, j * 32 + u)
                        for lo, n in S_CH:
                            last = pe.matmul(score_banks[:, lo:lo + n], q_stack[:, tile, h, :],
                                             k_stack[:, h // 2, lo:lo + n], start=True, stop=True)
                        last.then_inc(scored, 1)
                    if what.turn:
                        tj, tu = back(j, u, LT)
                        if by_scalar(tu):
                            pe.wait_ge(weighted, weighted_heads(tj, tu + 1))
                        else:
                            pe.wait_ge(exp_out, tj * 32 + (tu + 1))
                        for b in range(4):
                            await_(pe, bank_moved[b % 2], tj * 64 + (2 * tu + b // 2))
                            for i, n in group_blocks(b):
                                last = pe.transpose(turn_banks[0:n, b % 2, (i % 4) * P:(i % 4 + 1) * P],
                                                    rows[tu % L_SLOTS][:, i * P:i * P + n], ident[:])
                            last.then_inc(bank_turned[b % 2], 1)
                    if what.value:
                        vj, vu = back(j, u, LT + 1)
                        g = vu % XH // 4
                        if g == 0:
                            await_(pe, heads_copied, vj * 2 + vu // XH)
                        for b in range(2):
                            pe.wait_ge(bank_moved[b], vj * 64 + (2 * vu + 2))
                        for i in range(CT):
                            n = KEY_ROWS[i]
                            for q in range(4):
                                at = (4 * g + q) * XD
                                last = pe.matmul(value_bank[32 * q:32 * q + 32, g, :], v[0:n, i, at:at + 2 * XD],
                                                 turned[0:n, (vu - 3 + q) % PT_SLOTS, i, :], start=(i == 0), stop=(i == CT - 1))
                        last.then_inc(group_valued, 1)
                    if what.finish is not None:
                        k = what.finish
                        pe.wait_ge(misc_read, misc_number(j, u, k))
                        if k == 0:
                            pe.wait_ge(heads_copied, j * 2 + u // XH)
                            for g in range(4):
                                last = pe.transpose(misc_bank[:, g * P:(g + 1) * P], heads[:, g, :], ident[:])
                        elif k == 1:
                            for c in range(DC):
                                last = pe.transpose(misc_bank[:, c * P:(c + 1) * P], heads_normed[:, c * P:(c + 1) * P],
                                                    ident[:])
                        else:
                            for c in range(DC):
                                last = pe.matmul(misc_bank[:, 0:D], heads_turned[:, c, :], w_out[:, c, :],
                                                 start=(c == 0), stop=(c == DC - 1))
                        last.then_inc(misc_ready, 1)
                    if what.next_group is not None:
                        b = what.next_group
                        pe.wait_ge(misc_read, misc_number(j, u, 3 + b))
                        if b == 0:
                            pe.wait_ge(group_loaded[1 - tile], j * 16 + 16 * (tile + 1))
                        turn_group(1 - tile, b)

                pe.wait_ge(group_loaded[0], 16)
                for b in range(4):
                    await_(pe, misc_read, b)
                    turn_group(0, b)
                stream(pe, step)

            def move_bank(j, u, b, eng):
                eng.wait_ge(bank_turned[b % 2], j * 64 + (2 * u + b // 2 + 1))
                if b == 0:
                    await_(eng, group_valued, j * 8 + ((u - PT_SLOTS) // 4 + 1))

            @block.scalar
            def _(act):
                def copy_group(tile, b):
                    members = group_blocks(b)
                    n = members[0][1]
                    act.activation(group_turned[0:n, tile, 4 * b:4 * b + len(members), :].rearrange("p i n -> p (i n)"),
                                   misc_bank[0:n, 0:P * len(members)], ACT.Copy).then_inc(misc_read, 1)

                def step(j, u, what):
                    tile, h = u // XH, u % XH
                    if what.head:
                        act.wait_ge(logits_out, j * 32 + (u + 1))
                        act.activation(rows[u % L_SLOTS], rows[u % L_SLOTS], ACT.Exp, bias=peaks[:, u:u + 1], scale=-1.0,
                                       accum_out=sums[:, tile, h:h + 1]).then_inc(exp_out, 1)
                    tj, tu = back(j, u, LT)
                    if what.turn and by_scalar(tu):
                        for b in range(4):
                            move_bank(tj, tu, b, act)
                            members = group_blocks(b)
                            n = members[0][1]
                            act.activation(turned[0:n, tu % PT_SLOTS, 4 * b:4 * b + len(members), :].rearrange(
                                "p i n -> p (i n)"), turn_banks[0:n, b % 2, 0:P * len(members)], ACT.Copy).then_inc(
                                bank_moved[b % 2], 1)
                    if what.copy_heads:
                        act.wait_ge(group_valued, j * 8 + 4 * tile)
                        act.wait_ge(misc_ready, j * 14 + (7 * tile - 5))
                        act.activation(heads[:], value_bank[:], ACT.Copy).then_inc(heads_copied, 1)
                    if what.finish == 1:
                        act.wait_ge(misc_ready, misc_number(j, u, 1) + 1)
                        act.activation(heads_turned[:].rearrange("p c n -> p (c n)"), misc_bank[:, 0:D],
                                       ACT.Copy).then_inc(misc_read, 1)
                    if what.next_group is not None:
                        b = what.next_group
                        act.wait_ge(misc_ready, misc_number(j, u, 3 + b) + 1)
                        if b == 0:
                            for bank in range(2):
                                await_(act, bank_moved[bank], j * 64 + 32 * tile)
                        copy_group(1 - tile, b)

                for b in range(4):
                    act.wait_ge(misc_ready, b + 1)
                    copy_group(0, b)
                stream(act, step)

            @block.vector
            def _(dve):
                def step(j, u, what):
                    tile, h = u // XH, u % XH
                    if what.head:
                        dve.wait_ge(scored, j * 32 + (u + 1))
                        if h == 0:
                            dve.wait_ge(negated, j * 2 + (tile + 1))
                        for b in range(2):
                            await_(dve, bank_turned[b], j * 64 + (2 * (u - L_SLOTS) + 2))
                        dve.memset(gate[:, 0:1], 0.0)
                        dve.tensor_tensor_reduce(rows[u % L_SLOTS], score_banks[:, 0:S2], negative[:, tile, :],
                                                 -(XD ** -0.5), 3e38, ALU.add, ALU.min,
                                                 peaks[:, u:u + 1]).then_inc(logits_out, 1)
                    tj, tu = back(j, u, LT)
                    if what.turn and not by_scalar(tu):
                        if tu % XH == 0:
                            dve.wait_ge(misc_read, tj * 14 + (7 * (tu // XH) + 1))
                        for b in range(4):
                            move_bank(tj, tu, b, dve)
                            members = group_blocks(b)
                            n = members[0][1]
                            dve.tensor_tensor(turned[0:n, tu % PT_SLOTS, 4 * b:4 * b + len(members), :].rearrange(
                                "p i n -> p (i n)"), turn_banks[0:n, b % 2, 0:P * len(members)],
                                group_turned[0:n, tu // XH, 4 * b:4 * b + len(members), :].rearrange("p i n -> p (i n)"),
                                ALU.mult).then_inc(bank_moved[b % 2], 1)
                    before = (tile + 1) % 2
                    if what.finish == 0:
                        dve.wait_ge(exp_out, j * 32 + XH * tile)
                        dve.reciprocal(inverse[:, before, :], sums[:, before, :]).then_inc(inverted, 1)
                        dve.wait_ge(inverted, j * 2 + tile)
                        dve.wait_ge(misc_ready, misc_number(j, u, 0) + 1)
                        dve.tensor_tensor(heads_normed[:].rearrange("p (h d) -> p h d", h=XH),
                                          misc_bank[:].rearrange("p (h e) -> p h e", h=XH)[:, :, 0:XD],
                                          spread(inverse[:, before, :], 2, XD), ALU.mult).then_inc(misc_read, 1)
                    if what.finish == 2:
                        dve.wait_ge(misc_ready, misc_number(j, u, 2) + 1)
                        x = X[:, bass.ds(j * 2 + (tile - 1), 1), :].rearrange("p a d -> p (a d)")
                        dve.tensor_tensor(x, x, misc_bank[:, 0:D], ALU.add).then_inc(misc_read, 1)

                stream(dve, step)

            @block.gpsimd
            def _(pool):
                def negate(tile, loads, number):
                    pool.wait_ge(mask_loaded[tile], loads)
                    mask = negative[:, tile, :]
                    pool.tensor_tensor(gate[:, 1:2], gate[:, 3:4], gate[:, 3:4], ALU.add)
                    pool.tensor_scalar(mask, mask.bitcast(I32), -1.0, 1.0, ALU.mult, ALU.add).then_inc(mask_flipped, 1)
                    pool.wait_ge(mask_flipped, number)
                    pool.tensor_tensor(gate[:, 2:3], gate[:, 3:4], gate[:, 3:4], ALU.add)
                    pool.tensor_scalar(mask, mask, NEG, XD ** 0.5, ALU.mult, ALU.mult).then_inc(negated, 1)

                def step(j, u, what):
                    tile, h = u // XH, u % XH
                    if what.head and by_scalar(u):
                        pool.wait_ge(exp_out, j * 32 + (u + 1))
                        if h == BY_SCALAR[0]:
                            pool.wait_ge(group_loaded[tile], j * 16 + 16)
                        r = rows[u % L_SLOTS]
                        pool.tensor_tensor(r, r, group[:, tile, :], ALU.mult).then_inc(weighted, 1)
                    if what.next_group == 3:
                        negate(1 - tile, j * 16 + 16 * (tile + 1), j * 2 + (tile + 2))

                pool.memset(gate[:, 3:4], 0.0).then_inc(gate_cleared, 1)
                pool.wait_ge(gate_cleared, 1)
                negate(0, 16, 1)
                stream(pool, step)

            @block.sync
            def _(sync):
                def load(parity, row):
                    for b in range(4):
                        for a in range(2):
                            sync.dma_start(q_stack[stack_rows(a, b), parity, a::2, :], q_parts[q_rows[b]].rearrange(
                                "(i a j) t -> a j i t", a=2, j=XD)[a][:, :, bass.ds(row, P)]).then_inc(q_loaded[parity], 16)

                def load_rows(parity, row):
                    sync.dma_start(negative[:, parity, :].bitcast(I32), io["mask_BxSxS2_ik1"].rearrange(
                        "a t s -> (a t) s")[bass.ds(row, P), :]).then_inc(mask_loaded[parity], 16)

                def load_group(parity, row):
                    sync.dma_start(group[:, parity, :], io["fside_BxSxS2_0"].rearrange(
                        "a t s -> (a t) s")[bass.ds(row, P), :]).then_inc(group_loaded[parity], 16)

                def following(j, last=False):
                    for tile in range(1 if last else 2):
                        row = j * (2 * P) + (tile + 1) * P
                        await_(sync, scored, j * 32 + XH * tile)
                        load(1 - tile, row)
                        await_(sync, logits_out, j * 32 + XH * tile)
                        load_rows(1 - tile, row)
                        await_(sync, weighted, weighted_heads(j, XH * tile))
                        load_group(1 - tile, row)

                load(0, 0)
                load_rows(0, 0)
                load_group(0, 0)
                following(0)
                with sync.Fori(1, n_pairs - 1, 1) as j:
                    following(j)
                following(n_pairs - 1, last=True)



AH = 16
AD = 64
NK = T + S2
KT = (NK + P - 1) // P
K_ROWS = [P] * (KT - 1) + [NK - (KT - 1) * P]
K_CH = [(lo, min(CH, NK - lo)) for lo in range(0, NK, CH)]
QW = 2 * CH
PASSES = T // QW
HS = PASSES * KT
PS = 2 * HS
P_SLOTS = 4
MAX_UNIT = 64.0


def big_attention(nc, ident, io, X, R):
    with ExitStack() as ctx:
        def sb(name, shape, dt=F32):
            return ctx.enter_context(nc.sbuf_tensor(name, shape, dt))

        def sem(name):
            return ctx.enter_context(semaphore(nc, name))

        kv = sb("ba_kv", [P, DC, NK])
        affine = sb("ba_affine", [P, 4, DC])
        with nc.allow_non_contiguous_dma(reason="vectors of 256 values"):
            load_block(nc, [(affine[:, n, :], io[f"L0_xattn_ln{n // 2 + 1}_{'wb'[n % 2]}"].rearrange("(c p) -> p c", p=P))
                            for n in range(4)])
        norm_block(nc, "ba_norm_x", ident, X, R, NT, P, True, turned=kv, gain=affine[:, 2, :], shift=affine[:, 3, :])
        with nc.sbuf_tensor("ba_context", [P, CT, D], F32) as context:
            rows = io["ctx_1024"].rearrange("a s d -> (a s) d")
            load_block(nc, [(context[:, 0:CT - 1, :], rows[0:(CT - 1) * P].rearrange("(i p) d -> p i d", p=P)),
                            (context[0:CLAST, CT - 1, :], rows[(CT - 1) * P:S2])])
            norm_block(nc, "ba_norm_c", ident, context, context, CT, CLAST, True, turned=kv[:, :, T:NK],
                       gain=affine[:, 0, :], shift=affine[:, 1, :])

        k_high = sb("ba_k_high", [P, 2, NK], F16)
        k_low = sb("ba_k_low", [P, 2, NK], F16)
        q_both = sb("ba_q_both", [P, 2, T], F16)
        q_high = sb("ba_q_high", [P, 2, T], F16)
        q_part = sb("ba_q_part", [P, 2, CH], F16)
        v_next = sb("ba_v_next", [P, KT, P])
        v_use = sb("ba_v_use", [P, KT, P])
        probs = sb("ba_probs", [P, P_SLOTS, QW])
        sums_pool = sb("ba_sums_pool", [P, 2, QW])
        sums_vector = sb("ba_sums_vector", [P, 2, QW])
        out_raw = sb("ba_out_raw", [P, CH])
        out_pair = sb("ba_out_pair", [P, T])
        inverse = sb("ba_inverse", [P, CH])
        chunk_max = sb("ba_chunk_max", [P, NT, len(K_CH)])
        row_max = sb("ba_row_max", [P, NT])
        tile_rows = sb("ba_tile_rows", [NT, NT])
        lower_half = sb("ba_lower_half", [P, 1])
        ones = sb("ba_ones", [P, AD])
        w_qk = sb("ba_w_qk", [P, 2, 2, DC, P])
        w_v = sb("ba_w_v", [P, DC, P])
        w_o = sb("ba_w_o", [P, D])
        score_banks = ctx.enter_context(nc.psum_tensor("ba_score_banks", [P, 2, 2, CH], F32))
        value_bank = ctx.enter_context(nc.psum_tensor("ba_value_bank", [P, CH], F32))
        misc_bank = ctx.enter_context(nc.psum_tensor("ba_misc_bank", [P, CH], F32))
        unit_banks = ctx.enter_context(nc.psum_tensor("ba_unit_banks", [P, 2, CH], F32))

        qk_loaded = [sem(f"ba_qk_loaded_{b}") for b in range(2)]
        v_loaded = sem("ba_v_loaded")
        o_loaded = sem("ba_o_loaded")
        set_up = sem("ba_set_up")
        scored = sem("ba_scored")
        exp_out = sem("ba_exp_out")
        valued = sem("ba_valued")
        pool_summed = sem("ba_pool_summed")
        vector_summed = sem("ba_vector_summed")
        unit_ready = [sem(f"ba_unit_ready_{b}") for b in range(2)]
        unit_free = [sem(f"ba_unit_free_{b}") for b in range(2)]
        high_out = sem("ba_high_out")
        v_copied = sem("ba_v_copied")
        vector_set = sem("ba_vector_set")
        out_copied = sem("ba_out_copied")
        out_placed = sem("ba_out_placed")
        max_ready = sem("ba_max_ready")
        misc_ready = sem("ba_misc_ready")
        misc_read = sem("ba_misc_read")
        block = ctx.enter_context(nc.Block())

        def units_of(even):
            units = [("q", n, 0) for n in range(T // CH)]
            for c in range(len(K_CH)):
                units.append(("k", c, 0))
                if even:
                    units.append(("v", c, 0))
                units += [("max", c, t) for t in range(NT)]
            return units

        EVEN, ODD = units_of(True), units_of(False)
        BOTH = len(EVEN) + len(ODD)
        assert len(EVEN) % 2 == 0 and len(ODD) % 2 == 0
        LAST_UNIT = 51
        MAX_STEP, ROWS_STEP = 51, 53
        SUM_STEPS = (4, KT + 4)
        OUT_STEPS = tuple(range(8, 24, 2))
        V_COPY = {87 + 4 * c + 5: c for c in range(6)} | {115: 6}
        MISC = len(OUT_STEPS) + 6
        n_pairs = AH // 2

        def await_(eng, semaphore, value):
            if not isinstance(value, int) or value > 0:
                eng.wait_ge(semaphore, value)

        def unit_plan(odd_window):
            units, base = (EVEN, len(ODD)) if odd_window else (ODD, 0)
            plan = {}
            for i, unit in enumerate(units):
                plan.setdefault(i * LAST_UNIT // len(units), []).append((base + i, unit))
            return plan

        PLANS = unit_plan(False), unit_plan(True)

        def on_vector(s):
            return s % 3 == 2

        POOL_OPS = sum(not on_vector(s) for s in range(KT)) - 1
        VECTOR_OPS = sum(on_vector(s) for s in range(KT))

        def summed(j, u):
            f, s = u // KT, u % KT
            if on_vector(s):
                return vector_summed, j * (4 * VECTOR_OPS) + (f * VECTOR_OPS + sum(on_vector(i) for i in range(s + 1)))
            mine = max(1, sum(not on_vector(i) for i in range(s + 1)) - 1)
            return pool_summed, j * (4 * POOL_OPS) + (f * POOL_OPS + mine)

        def misc_number(j, k):
            number = j * MISC + (k - len(OUT_STEPS))
            return number - 1 if isinstance(j, int) and j == n_pairs else number

        def sums_use(f):
            return ((0, 9), (0, 11), (0, 12), (1, 0))[f]

        class Step:

            def __init__(self, u, first, last, tail):
                odd, w = u // HS, u % HS
                self.main = not tail
                self.units = [] if tail or (last and odd) else PLANS[odd].get(w, [])
                self.score_ahead = not tail and not (last and u >= PS - 2)
                self.sums = None
                if w in SUM_STEPS and not (first and u == SUM_STEPS[0]) and (not tail or u == SUM_STEPS[0]):
                    self.sums = (0, 9, 11, 12)[2 * odd + SUM_STEPS.index(w)]
                self.project = OUT_STEPS.index(u) if u in OUT_STEPS and not first else None
                self.maximum = w == MAX_STEP and not tail and not (last and odd)
                self.rows = (13 if odd else 10) if w == ROWS_STEP and not tail and not (last and odd) else None
                self.copy_out = u % KT == 0 and not (first and u == 0) and (not tail or u == 0)
                self.copy_v = V_COPY.get(u) if not last and not tail else None
                if u == 2 and not first and not tail:
                    self.copy_v = 7

        def stream(eng, step):
            def pair(j, first=False, last=False):
                for u in range(PS):
                    step(j, u, Step(u, first, last, False))
            pair(0, first=True)
            with eng.Fori(1, n_pairs - 1, 1) as j:
                pair(j)
            pair(n_pairs - 1, last=True)
            for u in range(OUT_STEPS[-1] + 1):
                step(n_pairs, u, Step(u, False, False, True))

        def slot_uses(j, i):
            return j * (BOTH // 2) + (len(EVEN) + i) // 2

        def qk_units(j, odd_window, c):
            per = T // CH + len(K_CH)
            return j * (2 * per) + (per * (1 + odd_window) + c + 1)

        def qk_index(unit):
            kind, c, _ = unit
            return c if kind == "q" else T // CH + c

        def value_tiles(c):
            return [(i, K_ROWS[i]) for i in range(4 * c, min(4 * c + 4, KT))]

        @block.tensor
        def _(pe):
            def do_unit(j, i, unit, odd_window):
                kind, c, t = unit
                slot = i % 2
                target = 1 - odd_window
                bank = unit_banks[:, slot, :]
                await_(pe, unit_free[slot], slot_uses(j, i))
                if kind in "qk":
                    if kind == "q" and c == 0:
                        pe.wait_ge(qk_loaded[target], j * 64 + 64 * (1 + odd_window))
                    lo, n = (c * CH, CH) if kind == "q" else K_CH[c]
                    for k in range(DC):
                        last = pe.matmul(bank[:, 0:n], w_qk[:, target, 0 if kind == "q" else 1, k, :], kv[:, k, lo:lo + n],
                                         start=(k == 0), stop=(k == DC - 1))
                elif kind == "v":
                    if c == 0:
                        pe.wait_ge(v_loaded, j * 16 + 32)
                    for m, (key, n) in enumerate(value_tiles(c)):
                        for k in range(DC):
                            last = pe.matmul(bank[0:n, m * P:(m + 1) * P], kv[:, k, key * P:key * P + n], w_v[:, k, :],
                                             start=(k == 0), stop=(k == DC - 1))
                else:
                    lo, n = K_CH[c]
                    if t == 0:
                        base = (len(ODD) if odd_window else 0) + T // CH + c * (NT + 1 + odd_window)
                        pe.wait_ge(unit_free[base % 2], slot_uses(j, base) + 1)
                        if c == 0:
                            pe.wait_ge(unit_free[(base - 1) % 2], slot_uses(j, base - 1) + 1)
                    last = pe.matmul(bank[:, 0:n], q_both[:, target, t * P:(t + 1) * P], k_high[:, target, lo:lo + n],
                                     start=True, stop=True)
                last.then_inc(unit_ready[slot], 1)

            def score(u):
                h, f, key = u // HS % 2, u // KT % 2, u % KT
                n = K_ROWS[key]
                for part_k, part_q, which in ((k_high, q_both, 0), (k_low, q_high, 1)):
                    for half in range(2):
                        at = f * QW + half * CH
                        last = pe.matmul(score_banks[0:n, u % 2, half, :], part_k[:, h, key * P:key * P + n],
                                         part_q[:, h, at:at + CH], start=(which == 0), stop=(which == 1))
                last.then_inc(scored, 1)

            def turn_maxima(number, use):
                pe.wait_ge(max_ready, number)
                await_(pe, misc_read, use)
                pe.transpose(misc_bank[0:NT, 0:P], row_max[:], ident[:]).then_inc(misc_ready, 1)

            def step(j, u, what):
                odd, w, key = u // HS, u % HS, u % KT
                units = list(what.units)
                if units:
                    do_unit(j, *units.pop(0), odd)
                if what.main:
                    pe.wait_ge(exp_out, j * PS + (u + 1))
                    if key == 0:
                        await_(pe, out_copied, j * 4 + u // KT)
                    if u < KT and key % 4 == 0:
                        pe.wait_ge(v_copied, j * 8 + (key // 4 + 1))
                    n = K_ROWS[key]
                    for half in range(2):
                        last = pe.matmul(value_bank[half * AD:(half + 1) * AD, :], v_use[0:n, key, odd * AD:(odd + 1) * AD],
                                         probs[0:n, u % P_SLOTS, half * CH:(half + 1) * CH],
                                         start=(key == 0), stop=(key == KT - 1))
                    last.then_inc(valued, 1)
                if units:
                    do_unit(j, *units.pop(0), odd)
                if what.score_ahead:
                    if w == HS - 2:
                        pe.wait_ge(misc_read, misc_number(j, 13 if odd else 10) + 1)
                    score(u + 2)
                for unit in units:
                    do_unit(j, *unit, odd)
                if what.sums is not None:
                    k = what.sums
                    f = {0: 3, 9: 0, 11: 1, 12: 2}[k]
                    fj = j - 1 if k == 0 else j
                    pe.wait_ge(misc_read, misc_number(j, k))
                    pe.wait_ge(*summed(fj, f * KT + KT - 1))
                    pe.wait_ge(*summed(fj, f * KT + KT - 3))
                    for half in range(2):
                        out = misc_bank[half * AD:(half + 1) * AD, :]
                        pe.matmul(out, ones[:], sums_pool[:, f % 2, half * CH:(half + 1) * CH], start=True, stop=False)
                        last = pe.matmul(out, ones[:], sums_vector[:, f % 2, half * CH:(half + 1) * CH],
                                         start=False, stop=True)
                    last.then_inc(misc_ready, 1)
                if what.project is not None:
                    k = what.project
                    pe.wait_ge(misc_read, misc_number(j, 1 + k))
                    if k == 0:
                        pe.wait_ge(o_loaded, j * 16)
                        pe.wait_ge(out_placed, j * 4)
                    for m in range(2):
                        t = 2 * k + m
                        last = pe.matmul(misc_bank[:, m * D:(m + 1) * D], out_pair[:, t * P:(t + 1) * P], w_o[:],
                                         start=True, stop=True)
                    last.then_inc(misc_ready, 1)
                if what.rows is not None:
                    turn_maxima(j * 2 + (2 + odd), misc_number(j, what.rows))

            pe.wait_ge(set_up, 1)
            for i, unit in enumerate(EVEN):
                do_unit(-1, len(ODD) + i, unit, 1)
            turn_maxima(1, 0)
            pe.wait_ge(misc_read, 1)
            score(0)
            score(1)
            stream(pe, step)

        @block.scalar
        def _(act):
            def do_unit(j, i, unit, odd_window):
                kind, c, _ = unit
                slot, target = i % 2, 1 - odd_window
                if kind == "max":
                    return
                act.wait_ge(unit_ready[slot], slot_uses(j, i) + 1)
                bank = unit_banks[:, slot, :]
                if kind == "v":
                    if c == 0:
                        await_(act, v_copied, j * 8 + 8)
                    members = value_tiles(c)
                    n = members[0][1]
                    act.activation(v_next[0:n, 4 * c:4 * c + len(members), :].rearrange("p i n -> p (i n)"),
                                   bank[0:n, 0:P * len(members)], ACT.Copy).then_inc(unit_free[slot], 1)
                    return
                if kind == "q":
                    if c == 0:
                        await_(act, scored, j * PS + HS * odd_window)
                    act.activation(q_part[:, c % 2, :], bank, ACT.Copy, scale=lower_half[:, 0:1])
                    last = act.activation(q_high[0:AD, target, c * CH:(c + 1) * CH], bank[0:AD, :], ACT.Copy)
                else:
                    lo, n = K_CH[c]
                    last = act.activation(k_high[:, target, lo:lo + n], bank[:, 0:n], ACT.Copy)
                last.then_inc(high_out, 1)

            def copy_v(j, c, staged):
                act.wait_ge(unit_free[staged[0]], staged[1])
                members = value_tiles(c)
                n = members[0][1]
                act.activation(v_use[0:n, 4 * c:4 * c + len(members), :], v_next[0:n, 4 * c:4 * c + len(members), :],
                               ACT.Copy).then_inc(v_copied, 1)

            def staged_by(j, c):
                i = len(ODD) + EVEN.index(("v", c, 0))
                return i % 2, slot_uses(j, i) + 1

            def step(j, u, what):
                odd, key = u // HS, u % KT
                if what.main:
                    act.wait_ge(scored, j * PS + (u + 1))
                    await_(act, valued, j * PS + (u - 3))
                    if not (isinstance(j, int) and j == 0 and u < P_SLOTS):
                        act.wait_ge(*(summed(j, u - 4) if u >= 4 else summed(j - 1, u - 4 + PS)))
                    n = K_ROWS[key]
                    act.activation(probs[0:n, u % P_SLOTS, :], score_banks[0:n, u % 2].rearrange("p a n -> p (a n)"),
                                   ACT.Exp, scale=AD ** -0.5).then_inc(exp_out, 1)
                if what.copy_out:
                    act.wait_ge(valued, j * PS + u)
                    await_(act, out_placed, j * 4 + (u // KT - 1))
                    act.activation(out_raw[:], value_bank[:], ACT.Copy).then_inc(out_copied, 1)
                for i, unit in what.units:
                    do_unit(j, i, unit, odd)
                if what.copy_v is not None:
                    c = what.copy_v
                    if c == 7:
                        act.wait_ge(valued, j * PS)
                        copy_v(j, c, staged_by(j - 1, c))
                    else:
                        act.wait_ge(valued, j * PS + (3 * KT + 4 * c + 4))
                        copy_v(j, c, staged_by(j, c))

            act.wait_ge(set_up, 1)
            for i, unit in enumerate(EVEN):
                do_unit(-1, len(ODD) + i, unit, 1)
            for c in range(8):
                copy_v(-1, c, staged_by(-1, c))
            stream(act, step)

        @block.vector
        def _(dve):
            def do_unit(j, i, unit, odd_window):
                kind, c, t = unit
                slot, target = i % 2, 1 - odd_window
                bank = unit_banks[:, slot, :]
                if kind == "v":
                    return
                if kind == "max":
                    n = K_CH[c][1]
                    dve.wait_ge(unit_ready[slot], slot_uses(j, i) + 1)
                    dve.tensor_reduce(chunk_max[:, t, c:c + 1], bank[:, 0:n], AX.X, ALU.max).then_inc(unit_free[slot], 1)
                    return
                dve.wait_ge(high_out, qk_units(j, odd_window, qk_index(unit)))
                if kind == "q":
                    at = slice(c * CH, (c + 1) * CH)
                    dve.tensor_tensor(q_both[:, target, at], bank, q_part[:, c % 2, :], ALU.subtract).then_inc(unit_free[slot], 1)
                else:
                    lo, n = K_CH[c]
                    dve.tensor_tensor(k_low[0:AD, target, lo:lo + n], bank[0:AD, 0:n], k_high[0:AD, target, lo:lo + n],
                                      ALU.subtract).then_inc(unit_free[slot], 1)

            def finish_max(j, odd_window):
                end = (len(ODD) if not odd_window else BOTH)
                for i in (end - 2, end - 1):
                    dve.wait_ge(unit_free[i % 2], slot_uses(j, i) + 1)
                dve.tensor_reduce(row_max[:], chunk_max[:], AX.X, ALU.max).then_inc(max_ready, 1)

            def place_rows(target, use):
                dve.wait_ge(misc_ready, use + 1)
                dve.tensor_tensor(q_high[AD:AD + NT, target, :].rearrange("r (t n) -> r t n", t=NT),
                                  spread(misc_bank[0:NT, 0:P], 1, NT), spread(tile_rows[:], 2, P),
                                  ALU.mult).then_inc(misc_read, 1)

            def step(j, u, what):
                odd, s, f = u // HS, u % KT, u // KT
                for i, unit in what.units:
                    do_unit(j, i, unit, odd)
                if what.main and on_vector(s):
                    dve.wait_ge(exp_out, j * PS + (u + 1))
                    total, part = sums_vector[:, f % 2, :], probs[:, u % P_SLOTS, :]
                    if s == 2:
                        if not (isinstance(j, int) and j == 0 and f < 2):
                            later, use = sums_use((f - 2) % 4)
                            dve.wait_ge(misc_ready, misc_number(j - 1 + later if f < 2 else j + later, use) + 1)
                        dve.tensor_copy(total, part).then_inc(vector_summed, 1)
                    else:
                        sem_, value = summed(j, u - 3)
                        dve.wait_ge(sem_, value)
                        dve.tensor_tensor(total, total, part, ALU.add).then_inc(vector_summed, 1)
                if what.sums is not None:
                    k = what.sums
                    g = {0: 3, 9: 0, 11: 1, 12: 2}[k]
                    number = misc_number(j, k)
                    done = (j - 1 if k == 0 else j) * 4 + g
                    dve.wait_ge(misc_ready, number + 1)
                    await_(dve, out_placed, done)
                    dve.reciprocal(inverse[:], misc_bank[:]).then_inc(misc_read, 1)
                    dve.wait_ge(misc_read, number + 1)
                    dve.wait_ge(out_copied, done + 1)
                    for half in range(2):
                        rows = slice(half * AD, (half + 1) * AD)
                        at = (g % 2) * QW + half * CH
                        last = dve.tensor_tensor(out_pair[g // 2 * AD:(g // 2 + 1) * AD, at:at + CH], out_raw[rows, :],
                                                 inverse[rows, :], ALU.mult)
                    last.then_inc(out_placed, 1)
                if what.project is not None:
                    k = what.project
                    dve.wait_ge(misc_ready, misc_number(j, 1 + k) + 1)
                    r = R[:, 2 * k:2 * k + 2, :].rearrange("p a d -> p (a d)")
                    dve.tensor_tensor(r, r, misc_bank[:], ALU.add).then_inc(misc_read, 1)
                if what.maximum:
                    finish_max(j, odd)
                if what.rows is not None:
                    place_rows(1 - odd, misc_number(j, what.rows))

            dve.tensor_copy(R[:], X[:])
            dve.tensor_scalar(tile_rows[:], ident[0:NT, 0:NT], -1.0 / MAX_UNIT, None, ALU.mult)
            dve.memset(ones[:], 1.0)
            dve.memset(lower_half[0:AD, :], 0.0)
            dve.memset(lower_half[AD:P, :], 1.0)
            dve.memset(sums_vector[:], 0.0)
            dve.memset(k_low[AD:P, :, :], 0.0).then_inc(vector_set, 1)
            dve.memset(q_high[AD:P, :, :], 0.0).then_inc(vector_set, 1)
            dve.wait_ge(vector_set, 2)
            dve.memset(k_low[AD:AD + NT, :, :], MAX_UNIT).then_inc(set_up, 1)
            for i, unit in enumerate(EVEN):
                do_unit(-1, len(ODD) + i, unit, 1)
            finish_max(-1, 1)
            place_rows(0, 0)
            stream(dve, step)

        @block.gpsimd
        def _(pool):
            def step(j, u, what):
                s, f = u % KT, u // KT
                if not what.main or on_vector(s) or s == 0:
                    return
                pool.wait_ge(exp_out, j * PS + (u + 1))
                n = K_ROWS[s]
                total, part = sums_pool[0:n, f % 2, :], probs[0:n, u % P_SLOTS, :]
                if s == 1:
                    if not (isinstance(j, int) and j == 0 and f < 2):
                        later, use = sums_use((f - 2) % 4)
                        pool.wait_ge(misc_ready, misc_number(j - 1 + later if f < 2 else j + later, use) + 1)
                    total, other = sums_pool[:, f % 2, :], probs[:, (u - 1) % P_SLOTS, :]
                else:
                    before = u - 1 if not on_vector(s - 1) else u - 2
                    pool.wait_ge(*summed(j, before))
                    other = total
                pool.tensor_tensor(total, other, part, ALU.add).then_inc(pool_summed, 1)

            stream(pool, step)

        @block.sync
        def _(sync):
            def load_qk(parity, head):
                for n, name in enumerate(("L0_xattn_Wq", "L0_xattn_Wkv")):
                    src = io[name].rearrange("(c p) n -> p c n", p=P)[:, :, bass.ds(head * AD, AD)]
                    for half in range(2):
                        sync.dma_start(w_qk[:, parity, n, :, half * AD:(half + 1) * AD], src).then_inc(qk_loaded[parity], 16)

            def load_v(pair):
                src = io["L0_xattn_Wkv"].rearrange("(c p) n -> p c n", p=P)[:, :, bass.ds(pair * P + AH * AD, P)]
                sync.dma_start(w_v[:], src).then_inc(v_loaded, 16)

            def windows(j, last=False):
                if not last:
                    sync.wait_ge(unit_ready[1], slot_uses(j, 0))
                    load_qk(0, j * 2 + 2)
                    load_v(j + 1)
                if not (isinstance(j, int) and j == 0):
                    sync.wait_ge(misc_ready, misc_number(j, 8) + 1)
                sync.dma_start(w_o[:], io["L0_xattn_Wo"][bass.ds(j * P, P), :]).then_inc(o_loaded, 16)
                if not last:
                    sync.wait_ge(unit_ready[1], slot_uses(j, len(ODD)))
                    load_qk(1, j * 2 + 3)

            load_qk(0, 0)
            load_qk(1, 1)
            load_v(0)
            windows(0)
            with sync.Fori(1, n_pairs - 1, 1) as j:
                windows(j)
            windows(n_pairs - 1, last=True)


def decoder(nc, io, out):
    with ExitStack() as ctx:
        ident = ctx.enter_context(nc.sbuf_tensor("identity", [P, P], F32))
        X = ctx.enter_context(nc.sbuf_tensor("X", [P, NT, D], F32))
        R = ctx.enter_context(nc.sbuf_tensor("R", [P, NT, D], F32))
        with nc.cleanup_on_exit():
            local_attention(nc, io, ident, X, R)
            norm_block(nc, "norm_0a", ident, R, X, NT, P, True)
        with nc.cleanup_on_exit():
            big_attention(nc, ident, io, X, R)
            norm_block(nc, "norm_0b", ident, R, X, NT, P, True)
        with nc.cleanup_on_exit():
            quantised_ffn(nc, ident, io, X, R)
            norm_block(nc, "norm_0c", ident, R, X, NT, P, True)
        with nc.cleanup_on_exit():
            retention(nc, ident, io, X, R)
            norm_block(nc, "norm_1a", ident, R, X, NT, P, True)
        with nc.cleanup_on_exit():
            masked_attention(nc, ident, io, X, R)
            norm_block(nc, "norm_1b", ident, X, X, NT, P, True)
        with nc.cleanup_on_exit():
            experts_ffn(nc, ident, io, X, R)
            norm_block(nc, "norm_1c", ident, R, X, NT, P, True)
        with semaphore(nc, "stored") as stored, nc.Block() as block:
            @block.sync
            def _(sync):
                sync.dma_start(out.rearrange("a (i p) d -> p (a i) d", p=P), X[:]).then_inc(stored, 16)
                sync.wait_ge(stored, 16)


def kernel(**inputs):
    import concourse.bacc as bacc
    from concourse.bass_utils import run_bass_kernel_spmd

    nc = bacc.Bacc("TRN2", target_bir_lowering=False, num_devices=1)
    constants = {**basic_constants(), **retention_constants(), **expert_constants()}
    arrays, io = {}, {}
    for name, value in {**inputs, **constants}.items():
        a = np.ascontiguousarray(value)
        arrays[f"in_{name}"] = a
        io[name] = nc.dram_tensor(f"in_{name}", a.shape, mybir.dt.from_np(a.dtype), kind="ExternalInput").ap()
    out = nc.dram_tensor("out_0", (1, T, D), F32, kind="ExternalOutput").ap()
    decoder(nc, io, out)
    r = run_bass_kernel_spmd(nc, [arrays], core_ids=[0])
    return r.results[0]["out_0"]
```

```python
from contextlib import ExitStack, contextmanager
from itertools import count

import numpy as np

import concourse.bass as bass
from concourse import mybir

ALU = mybir.AluOpType
ACT = mybir.ActivationFunctionType
AX = mybir.AxisListType
F32 = mybir.dt.float32
F16 = mybir.dt.float16
I32 = mybir.dt.int32

P = 128
T = 2048
D = 256
NT = T // P
DC = D // P
CH = 512
NC_T = T // CH
S2 = 1601
CT = (S2 + P - 1) // P
CLAST = S2 - (CT - 1) * P
EPS = 1e-5
MAGIC = 12582912.0


USES = count()


@contextmanager
def semaphore(nc, name):
    yield nc.alloc_semaphore(f"{name}_{next(USES)}")


class Chain:

    def __init__(self, eng, sem):
        self.eng, self.sem, self.n = eng, sem, 0

    def __call__(self, ins):
        self.n += 1
        ins.then_inc(self.sem, 1)

    def wait(self):
        self.eng.wait_ge(self.sem, self.n)

    def step(self, ins):
        self(ins)
        self.wait()


def spread(ap, axis, n):
    shape = list(ap.shape)
    return ap.unsqueeze(axis).broadcast_to(shape[:axis] + [n] + shape[axis:])


def load_block(nc, loads):
    with semaphore(nc, "loaded_sync") as loaded_sync, semaphore(nc, "loaded_act") as loaded_act, nc.Block() as block:
        @block.sync
        def _(sync):
            mine = loads[0::2]
            for dst, src in mine:
                sync.dma_start(dst, src).then_inc(loaded_sync, 16)
            sync.wait_ge(loaded_sync, 16 * len(mine))

        if loads[1::2]:
            @block.scalar
            def _(act):
                mine = loads[1::2]
                for dst, src in mine:
                    act.dma_start(dst, src).then_inc(loaded_act, 16)
                act.wait_ge(loaded_act, 16 * len(mine))


def norm_block(nc, label, ident, src, dst, tiles, last_rows, normalise, turned=None, gain=None, shift=None, loads=()):
    rows = [P] * (tiles - 1) + [last_rows]
    with ExitStack() as ctx:
        def sem(name):
            return ctx.enter_context(semaphore(nc, name))

        stats = ctx.enter_context(nc.sbuf_tensor(f"{label}_stats", [P, tiles, 6], F32))
        mean_var = ctx.enter_context(nc.sbuf_tensor(f"{label}_mean_var", [P, tiles, 2], F32))
        deviation = ctx.enter_context(nc.sbuf_tensor(f"{label}_deviation", [P, tiles], F32))
        inverse = ctx.enter_context(nc.sbuf_tensor(f"{label}_inverse", [P, tiles], F32))
        banks = ctx.enter_context(nc.psum_tensor(f"{label}_banks", [P, 8, CH], F32))
        vector_step = sem("norm_vector_step")
        variance_ready = sem("norm_variance_ready")
        deviation_ready = sem("norm_deviation_ready")
        tile_ready = sem("norm_tile_ready")
        bank_turned = sem("norm_bank_turned")
        groups = (tiles + 3) // 4
        block = ctx.enter_context(nc.Block())

        if loads:
            loaded = sem("norm_loaded")

            @block.sync
            def _(sync):
                for destination, source in loads:
                    sync.dma_start(destination, source).then_inc(loaded, 16)
                sync.wait_ge(loaded, 16 * len(loads))

        if normalise:
            @block.vector
            def _(dve):
                chain = Chain(dve, vector_step)
                if last_rows < P:
                    chain(dve.memset(mean_var[:], 1.0))
                for t in range(tiles):
                    chain(dve.bn_stats(stats[0:rows[t], t, :], src[0:rows[t], t, :]))
                chain.wait()
                for t in range(tiles):
                    chain(dve.bn_aggr(mean_var[0:rows[t], t, :], stats[0:rows[t], t, :]))
                chain.wait()
                dve.tensor_scalar(deviation[:], mean_var[:, :, 1], EPS, None, ALU.add).then_inc(variance_ready, 1)
                dve.wait_ge(deviation_ready, 1)
                chain.step(dve.reciprocal(inverse[:], deviation[:]))
                for t in range(tiles):
                    dve.tensor_scalar(dst[0:rows[t], t, :], src[0:rows[t], t, :], mean_var[0:rows[t], t, 0:1],
                                      inverse[0:rows[t], t:t + 1], ALU.subtract, ALU.mult).then_inc(tile_ready, 1)

        @block.scalar
        def _(act):
            if normalise:
                act.wait_ge(variance_ready, 1)
                act.activation(deviation[:], deviation[:], ACT.Sqrt).then_inc(deviation_ready, 1)
            if turned is not None:
                for g in range(groups):
                    lo, hi = g * CH, sum(rows[:4 * g + 4])
                    for c in range(DC):
                        act.wait_ge(bank_turned, DC * g + c + 1)
                        bank = banks[:, DC * g + c, 0:hi - lo]
                        if gain is None:
                            act.activation(turned[:, c, lo:hi], bank, ACT.Copy)
                        else:
                            act.activation(turned[:, c, lo:hi], bank, ACT.Identity,
                                           bias=shift[:, c:c + 1], scale=gain[:, c:c + 1])

        if turned is not None:
            @block.tensor
            def _(pe):
                for g in range(groups):
                    members = range(4 * g, min(4 * g + 4, tiles))
                    if normalise:
                        pe.wait_ge(tile_ready, members[-1] + 1)
                    for c in range(DC):
                        for t in members:
                            n = rows[t]
                            at = (t - 4 * g) * P
                            last = pe.transpose(banks[:, DC * g + c, at:at + n], dst[0:n, t, c * P:(c + 1) * P],
                                                ident[0:n, 0:n])
                        last.then_inc(bank_turned, 1)



K1 = 16
LEFT = (K1 - 1) // 2
PADDED = T + K1
GROUPS = PADDED // K1
BAND = P + K1


def local_attention(nc, io, ident, X, R):
    with ExitStack() as ctx:
        def sb(name, shape, dt=F32):
            return ctx.enter_context(nc.sbuf_tensor(name, shape, dt))

        x_pad = sb("x_pad", [P, NT + 1, D])
        band_mask = sb("band_mask", [P, BAND])
        weights = sb("slot_weights", [P, NT, K1])
        with ExitStack() as inner:
            def isb(name, shape, dt=F32):
                return inner.enter_context(nc.sbuf_tensor(name, shape, dt))

            x_turned = isb("x_turned", [P, DC, T])
            w1 = isb("w1", [P, DC, D])
            w2 = isb("w2", [P, DC, D])
            v_window = isb("v_window", [P, DC, 2 * K1 + K1 - 1])
            query = isb("query", [P, DC, K1 - 1 + T + K1])
            proj = isb("proj", [P, DC, PADDED])
            z = isb("z", [P, 3, DC, PADDED])
            score_rows = isb("score_rows", [P, CH])
            slot_max = isb("slot_max", [P, NT])
            slot_sum = isb("slot_sum", [P, NT])
            x_rows = io["x"].rearrange("a (i p) d -> p (a i) d", p=P)
            x_flat = io["x"].rearrange("a t d -> (a t) d")
            with semaphore(nc, "zeroed") as zeroed, semaphore(nc, "late_loaded") as loaded, nc.Block() as block:
                @block.vector
                def _(dve):
                    dve.memset(x_pad[:, 0, :], 0.0).then_inc(zeroed, 1)
                    dve.memset(x_pad[:, NT, :], 0.0).then_inc(zeroed, 1)
                    dve.memset(v_window[:], 0.0).then_inc(zeroed, 1)
                    dve.memset(query[:], 0.0)
                    dve.memset(proj[:], 0.0)

                @block.scalar
                def _(act):
                    act.dma_start(w1[:], io["L0_attn_w1"].rearrange("(c p) n -> p c n", p=P)).then_inc(loaded, 16)
                    act.dma_start(w2[:], io["L0_attn_w2"].rearrange("(c p) n -> p c n", p=P)).then_inc(loaded, 16)
                    act.dma_start(ident[:], io["const_identity"]).then_inc(loaded, 16)
                    act.dma_start(band_mask[:], io["const_band"]).then_inc(loaded, 16)

                @block.sync
                def _(sync):
                    sync.dma_start(X[:], x_rows).then_inc(loaded, 16)
                    sync.wait_ge(zeroed, 3)
                    first = P - LEFT
                    sync.dma_start(x_pad[LEFT:P, 0, :], x_flat[0:first, :]).then_inc(loaded, 16)
                    sync.dma_start(x_pad[:, 1:NT, :], x_flat[first:first + (NT - 1) * P, :].rearrange(
                        "(i p) d -> p i d", p=P)).then_inc(loaded, 16)
                    sync.dma_start(x_pad[0:LEFT, NT, :], x_flat[T - LEFT:T, :]).then_inc(loaded, 16)
                    with nc.allow_non_contiguous_dma(reason="v is 256 values"):
                        sync.dma_start(v_window[:, :, K1 - 1:K1], io["L0_attn_v"].rearrange(
                            "(c p) a -> p c a", p=P)).then_inc(loaded, 16)
                    sync.wait_ge(loaded, 16 * 9)

            norm_block(nc, "turn_x", ident, X, X, NT, P, False, turned=x_turned)

            with ExitStack() as sems:
                def sem(name):
                    return sems.enter_context(semaphore(nc, name))

                projected = sem("projected")
                evacuated = sem("evacuated")
                added_first = sem("added_first")
                added_second = sem("added_second")
                added_pool = sem("added_pool")
                squashed = sem("squashed")
                dotted = sem("dotted")
                rows_ready = sem("rows_ready")
                rows_copied = sem("rows_copied")
                turned_ready = sem("turned_ready")
                shifted = sem("shifted")
                exp_done = sem("exp_done")
                step = sem("softmax_step")
                pq = sems.enter_context(nc.psum_tensor("pq", [P, 4, CH], F32))
                score_bank = sems.enter_context(nc.psum_tensor("score_bank", [P, CH], F32))
                turned_bank = sems.enter_context(nc.psum_tensor("turned_bank", [P, CH], F32))
                block = sems.enter_context(nc.Block())
                jobs = [(w, out, off, c, n) for w, out, off in ((w1, query, K1 - 1), (w2, proj, LEFT))
                        for c in range(DC) for n in range(NC_T)]

                def on_pool(m, c):
                    return c == 1 and m % 3 != 1

                def added(m, c):
                    if c == 0:
                        return added_first, m + 1
                    mine = sum(on_pool(i, 1) == on_pool(m, 1) for i in range(m + 1))
                    return (added_pool if on_pool(m, 1) else added_second), mine

                def add_slot(eng, m, c):
                    s = m % 3
                    eng.tensor_tensor(
                        z[:, s, c, :].rearrange("p (g j) -> p g j", j=K1),
                        query[:, c, m:m + PADDED].rearrange("p (g j) -> p g j", j=K1),
                        spread(proj[:, c, :].rearrange("p (g j) -> p g j", j=K1)[:, :, m], 2, K1),
                        ALU.add).then_inc(added(m, c)[0], 1)

                @block.tensor
                def _(pe):
                    for i, (w, _, _, c, n) in enumerate(jobs):
                        if i >= 4:
                            pe.wait_ge(evacuated, i - 3)
                        for k in range(DC):
                            last = pe.matmul(pq[:, i % 4, :], w[:, k, c * P:(c + 1) * P],
                                             x_turned[:, k, n * CH:(n + 1) * CH], start=(k == 0), stop=(k == DC - 1))
                        last.then_inc(projected, 1)
                    for m in range(K1):
                        for c in range(DC):
                            pe.wait_ge(squashed, m * DC + c + 1)
                            for n in range(NC_T):
                                at = K1 - 1 - m + n * CH
                                last = pe.matmul(score_bank[32 * n:32 * n + 32, :],
                                                 v_window[:, c, K1 - 1 - m:K1 - 1 - m + 32],
                                                 z[:, m % 3, c, at:at + CH], start=(m == 0 and c == 0),
                                                 stop=(m == K1 - 1 and c == DC - 1))
                        last.then_inc(dotted, 1)
                    pe.wait_ge(rows_copied, 1)
                    for j in range(4):
                        last = pe.transpose(turned_bank[:, j * P:(j + 1) * P], score_rows[:, j * P:(j + 1) * P],
                                            ident[:])
                    last.then_inc(turned_ready, 1)

                @block.scalar
                def _(act):
                    for i, (_, out, off, c, n) in enumerate(jobs):
                        act.wait_ge(projected, i + 1)
                        act.activation(out[:, c, off + n * CH:off + (n + 1) * CH], pq[:, i % 4, :],
                                       ACT.Copy).then_inc(evacuated, 1)
                    for m in range(K1):
                        for c in range(DC):
                            act.wait_ge(*added(m, c))
                            at = K1 - 1 - m
                            zc = z[:, m % 3, c, at:at + T]
                            act.activation(zc, zc, ACT.Tanh).then_inc(squashed, 1)
                    act.wait_ge(shifted, 1)
                    act.activation(weights[:], weights[:], ACT.Exp).then_inc(exp_done, 1)

                @block.gpsimd
                def _(pool):
                    pool.wait_ge(evacuated, len(jobs))
                    for m in range(K1):
                        if on_pool(m, 1):
                            if m >= 3:
                                pool.wait_ge(dotted, m - 2)
                            add_slot(pool, m, 1)

                @block.vector
                def _(dve):
                    dve.wait_ge(evacuated, len(jobs))
                    for m in range(K1):
                        if m >= 3:
                            dve.wait_ge(dotted, m - 2)
                        for c in range(DC):
                            if not on_pool(m, c):
                                add_slot(dve, m, c)
                    dve.wait_ge(dotted, K1)
                    dve.tensor_copy(score_rows[:], score_bank[:]).then_inc(rows_copied, 1)
                    dve.wait_ge(turned_ready, 1)
                    chain = Chain(dve, step)
                    slots = turned_bank[:].rearrange("p (j n m) -> p j n m", j=4, n=4)[:, :, :, 0:K1]
                    by_tile = "p (n j) -> p j n"
                    chain.step(dve.tensor_reduce(slot_max[:].rearrange(by_tile, n=4), slots, AX.X, ALU.max))
                    for j in range(4):
                        last = dve.tensor_tensor(weights[:].rearrange("p (n j) m -> p j n m", n=4)[:, j],
                                                 slots[:, j],
                                                 spread(slot_max[:].rearrange(by_tile, n=4)[:, j], 2, K1),
                                                 ALU.subtract)
                    last.then_inc(shifted, 1)
                    dve.wait_ge(exp_done, 1)
                    chain.step(dve.tensor_reduce(slot_sum[:], weights[:], AX.X, ALU.add))
                    chain.step(dve.reciprocal(slot_max[:], slot_sum[:]))
                    dve.tensor_tensor(weights[:], weights[:], spread(slot_max[:], 2, K1), ALU.mult)

        band = sb("band", [P, NT, BAND])
        band_turned = sb("band_turned", [P, NT, P])
        edge_turned = sb("edge_turned", [K1, NT, P])
        with ExitStack() as sems:
            def sem(name):
                return sems.enter_context(semaphore(nc, name))

            banded = sem("banded")
            main_turned = sem("main_turned")
            edges_turned = sem("edges_turned")
            main_copied = sem("main_copied")
            edges_copied = sem("edges_copied")
            mixed = sem("mixed")
            banks = sems.enter_context(nc.psum_tensor("band_banks", [P, 8, CH], F32))
            block = sems.enter_context(nc.Block())

            @block.vector
            def _(dve):
                for i in range(NT):
                    dve.tensor_tensor(band[:, i, :].rearrange("p (r m) -> p r m", m=K1),
                                      spread(weights[:, i, :], 1, BAND // K1),
                                      band_mask[:].rearrange("p (r m) -> p r m", m=K1), ALU.mult).then_inc(banded, 1)
                for q in range(4):
                    dve.wait_ge(edges_turned, q + 1)
                    dve.tensor_copy(edge_turned[:, 4 * q:4 * q + 4, :].rearrange("p a b -> p (a b)"),
                                    banks[0:K1, 4 + q, :]).then_inc(edges_copied, 1)
                for q in range(NT // 2):
                    dve.wait_ge(mixed, q + 1)
                    dve.tensor_tensor(R[:, 2 * q:2 * q + 2, :].rearrange("p a b -> p (a b)"), banks[:, q, :],
                                      X[:, 2 * q:2 * q + 2, :].rearrange("p a b -> p (a b)"), ALU.add)

            @block.scalar
            def _(act):
                for q in range(4):
                    act.wait_ge(main_turned, q + 1)
                    act.activation(band_turned[:, 4 * q:4 * q + 4, :].rearrange("p a b -> p (a b)"),
                                   banks[:, q, :], ACT.Copy).then_inc(main_copied, 1)

            @block.tensor
            def _(pe):
                for q in range(4):
                    pe.wait_ge(banded, 4 * q + 4)
                    for j in range(4):
                        last = pe.transpose(banks[:, q, j * P:(j + 1) * P], band[:, 4 * q + j, 0:P], ident[:])
                    last.then_inc(main_turned, 1)
                    for j in range(4):
                        last = pe.transpose(banks[0:K1, 4 + q, j * P:(j + 1) * P], band[:, 4 * q + j, P:BAND], ident[:])
                    last.then_inc(edges_turned, 1)
                for i in range(NT):
                    q = i // 2
                    if i % 2 == 0:
                        if q < 4:
                            pe.wait_ge(main_copied, q + 1)
                            pe.wait_ge(edges_copied, (i + 1) // 4 + 1)
                        else:
                            pe.wait_ge(edges_copied, 4)
                            pe.wait_ge(main_copied, 4)
                    out = banks[:, q, (i % 2) * D:(i % 2 + 1) * D]
                    pe.matmul(out, band_turned[:, i, :], x_pad[:, i, :], start=True, stop=False)
                    last = pe.matmul(out, edge_turned[:, i, :], x_pad[0:K1, i + 1, :], start=False, stop=True)
                    if i % 2:
                        last.then_inc(mixed, 1)


def basic_constants():
    p = np.arange(P)[:, None]
    j = np.arange(BAND)[None, :]
    band = ((j >= p) & (j < p + K1)).astype(np.float32)
    return {"const_identity": np.eye(P, dtype=np.float32), "const_band": band}



FF = 768
FC = FF // P
WB = 32
W_QMAX = 7.0
A_QMAX = 32767.0
SCALE_FLOOR = 1e-12
HALVES = 3


def quantised_ffn(nc, ident, io, X, R):
    with ExitStack() as ctx:
        def sb(name, shape, dt=F32):
            return ctx.enter_context(nc.sbuf_tensor(name, shape, dt))

        gate = sb("gate", [P, FC, T])
        up = sb("up", [P, FC, T])
        in_turned = sb("w_in_turned", [P, 2, DC, FF])
        down_turned = sb("w_down_turned", [P, FC, D])
        peak = sb("peak", [P, 5, FC])
        peak_one = sb("peak_one", [P, 5])
        peak_all = sb("peak_all", [P, 5])
        scale = sb("act_scale", [P, 5])
        inverse = sb("act_inverse", [P, 5])
        x_turned = sb("ffn_x_turned", [P, DC, T])
        raw = gate[:, 0:3, :].rearrange("p a t -> p (a t)")[:, 0:3 * 1536].rearrange("p (w n) -> p w n", w=3)
        blocks = 1536 // WB
        w_peak = gate[:, 3, 0:3 * blocks].rearrange("p (w b) -> p w b", w=3)
        w_scale = gate[:, 3, 256:256 + 3 * blocks].rearrange("p (w b) -> p w b", w=3)
        w_inverse = gate[:, 3, 512:512 + 3 * blocks].rearrange("p (w b) -> p w b", w=3)
        x_quant = up[:, 0:2, :].rearrange("p a t -> p (a t)").rearrange("p (i d) -> p i d", i=NT)
        norm_block(nc, "norm_0b", ident, R, X, NT, P, True, loads=[
            (raw[:, 0, :].rearrange("p (a d) -> p a d", d=D), io["L0_ffn_w_gate"].rearrange("(a p) d -> p a d", p=P)),
            (raw[:, 1, :].rearrange("p (a d) -> p a d", d=D), io["L0_ffn_w_up"].rearrange("(a p) d -> p a d", p=P)),
            (raw[:, 2, :].rearrange("p (a d) -> p a d", d=FF), io["L0_ffn_w_down"].rearrange("(a p) d -> p a d", p=P)),
        ])
        with ExitStack() as sems:
            def sem(name):
                return sems.enter_context(semaphore(nc, name))

            step = sem("quant_step")
            x_peak = sem("x_peak")
            x_peak_all = sem("x_peak_all")
            weights_ready = sem("weights_ready")
            w_turned = sem("w_turned")
            w_copied = sem("w_copied")
            banks = sems.enter_context(nc.psum_tensor("w_banks", [P, 8, CH], F32))
            block = sems.enter_context(nc.Block())
            jobs = []
            for w in range(2):
                for c in range(DC):
                    for part in ((0, 4), (4, 6)):
                        jobs.append([(raw[:, w, a * D + c * P:a * D + (c + 1) * P], k) for k, a in
                                     enumerate(range(*part))] + [in_turned[:, w, c, part[0] * P:part[1] * P]])
            for q in range(FC // 2):
                jobs.append([(raw[:, 2, a * FF + i * P:a * FF + (i + 1) * P], 2 * k + a)
                             for k, i in enumerate((2 * q, 2 * q + 1)) for a in range(2)]
                            + [down_turned[:, 2 * q:2 * q + 2, :].rearrange("p a b -> p (a b)")])

            @block.vector
            def _(dve):
                chain = Chain(dve, step)
                dve.tensor_reduce(peak_one[:, 0:1], X[:].rearrange("p i d -> p (i d)"), AX.X, ALU.max,
                                  apply_absolute_value=True).then_inc(x_peak, 1)
                by_block = raw[:].rearrange("p w (b k) -> p w b k", k=WB)
                chain.step(dve.tensor_reduce(w_peak, by_block, AX.X, ALU.max, apply_absolute_value=True))
                chain.step(dve.tensor_scalar(w_scale, w_peak, 1.0 / W_QMAX, SCALE_FLOOR, ALU.mult, ALU.max))
                chain.step(dve.reciprocal(w_inverse, w_scale))
                for w in range(3):
                    wb = by_block[:, w]
                    chain.step(dve.tensor_tensor(wb, wb, spread(w_inverse[:, w], 2, WB), ALU.mult))
                    chain.step(dve.tensor_scalar(raw[:, w], raw[:, w], MAGIC, MAGIC, ALU.add, ALU.subtract))
                    dve.tensor_tensor(wb, wb, spread(w_scale[:, w], 2, WB), ALU.mult).then_inc(weights_ready, 1)
                dve.wait_ge(x_peak_all, 1)
                chain.step(dve.tensor_scalar(scale[:, 0:1], peak_all[:, 0:1], 1.0 / A_QMAX, SCALE_FLOOR,
                                             ALU.mult, ALU.max))
                chain.step(dve.reciprocal(inverse[:, 0:1], scale[:, 0:1]))
                chain.step(dve.tensor_scalar(x_quant, X[:], inverse[:, 0:1], MAGIC, ALU.mult, ALU.add))
                dve.tensor_scalar(x_quant, x_quant, MAGIC, scale[:, 0:1], ALU.subtract, ALU.mult)

            @block.gpsimd
            def _(pool):
                pool.wait_ge(x_peak, 1)
                pool.partition_all_reduce(peak_all[:, 0:1], peak_one[:, 0:1], P,
                                          bass.bass_isa.ReduceOp.max).then_inc(x_peak_all, 1)

            @block.tensor
            def _(pe):
                for n, job in enumerate(jobs):
                    pe.wait_ge(weights_ready, 1 + n // 4 if n < 8 else 3)
                    if n >= 8:
                        pe.wait_ge(w_copied, n - 7)
                    for src, k in job[:-1]:
                        last = pe.transpose(banks[:, n % 8, k * P:(k + 1) * P], src, ident[:])
                    last.then_inc(w_turned, 1)

            @block.scalar
            def _(act):
                for n, job in enumerate(jobs):
                    act.wait_ge(w_turned, n + 1)
                    act.activation(job[-1], banks[:, n % 8, 0:job[-1].shape[1]], ACT.Copy).then_inc(w_copied, 1)

        norm_block(nc, "turn_quant", ident, x_quant, x_quant, NT, P, False, turned=x_turned)

        half = sb("sigmoid", [P, HALVES, T])
        rounding = sb("rounding", [P, 2])
        with ExitStack() as sems:
            def sem(name):
                return sems.enter_context(semaphore(nc, name))

            step = sem("qdq_step")
            peaks_ready = sem("peaks_ready")
            peaks_all = sem("peaks_all")
            scales_ready = sem("scales_ready")
            gate_ready = sem("gate_ready")
            sigmoid_done = sem("sigmoid_done")
            half_free = sem("half_free")
            pool_step = sem("pool_step")
            scalar_step = sem("scalar_step")
            rounding_set = sem("rounding_set")
            up_ready = sem("up_ready")
            hidden_ready = sem("hidden_ready")
            down_done = sem("down_done")
            multiplied = sem("ffn_multiplied")
            copied = sem("ffn_copied")
            banks = sems.enter_context(nc.psum_tensor("ffn_banks", [P, 8, CH], F32))
            block = sems.enter_context(nc.Block())

            @block.vector
            def _(dve):
                chain = Chain(dve, step)

                def scales(lo, hi, number):
                    chain.step(dve.tensor_reduce(peak_one[:, lo:hi], peak[:, lo:hi, :], AX.X, ALU.max))
                    dve.tensor_scalar(peak_one[:, lo:hi], peak_one[:, lo:hi], 1.0 / A_QMAX, SCALE_FLOOR,
                                      ALU.mult, ALU.max).then_inc(peaks_ready, 1)
                    dve.wait_ge(peaks_all, number)
                    dve.reciprocal(inverse[:, lo:hi], scale[:, lo:hi]).then_inc(scales_ready, 1)
                    dve.wait_ge(scales_ready, number)

                def quantise(x, a):
                    chain.step(dve.tensor_scalar(x, x, inverse[:, a:a + 1], MAGIC, ALU.mult, ALU.add))
                    return dve.tensor_scalar(x, x, MAGIC, scale[:, a:a + 1], ALU.subtract, ALU.mult)

                def find_peak(x, a, i):
                    chain(dve.tensor_reduce(peak[:, a, i:i + 1], x[:, i, :], AX.X, ALU.max, apply_absolute_value=True))

                for i in range(FC):
                    dve.wait_ge(copied, i + 1)
                    find_peak(gate, 1, i)
                chain.wait()
                scales(1, 2, 1)
                for i in range(FC + 1):
                    if i < FC:
                        quantise(gate[:, i, :], 1).then_inc(gate_ready, 1)
                    if i:
                        g, h = gate[:, i - 1, :], half[:, (i - 1) % HALVES, :]
                        dve.wait_ge(sigmoid_done, i)
                        dve.scalar_tensor_tensor(out=g, in0=h, scalar=65535.0 / 65536.0, in1=g, op0=ALU.min,
                                                 op1=ALU.mult).then_inc(half_free, 1)
                        dve.wait_ge(half_free, i)
                        find_peak(gate, 3, i - 1)
                        dve.wait_ge(copied, FC + i)
                        find_peak(up, 2, i - 1)
                chain.wait()
                scales(2, 4, 2)
                for i in range(FC):
                    g = gate[:, i, :]
                    chain.step(quantise(g, 3))
                    dve.wait_ge(up_ready, i + 1)
                    chain.step(dve.tensor_tensor(g, g, up[:, i, :], ALU.mult))
                    find_peak(gate, 4, i)
                chain.wait()
                scales(4, 5, 3)
                for i in range(FC):
                    quantise(gate[:, i, :], 4).then_inc(hidden_ready, 1)
                for q in range(NT // 2):
                    dve.wait_ge(down_done, q + 1)
                    dve.tensor_tensor(R[:, 2 * q:2 * q + 2, :].rearrange("p a b -> p (a b)"), banks[:, q, :],
                                      X[:, 2 * q:2 * q + 2, :].rearrange("p a b -> p (a b)"), ALU.add)

            @block.gpsimd
            def _(pool):
                def reduce_all(lo, hi, number):
                    pool.wait_ge(peaks_ready, number)
                    pool.partition_all_reduce(scale[:, lo:hi], peak_one[:, lo:hi], P,
                                              bass.bass_isa.ReduceOp.max).then_inc(peaks_all, 1)

                pool.memset(rounding[:, 0:1], MAGIC).then_inc(rounding_set, 1)
                pool.memset(rounding[:, 1:2], -MAGIC / 65536.0).then_inc(rounding_set, 1)
                pool.wait_ge(rounding_set, 2)
                reduce_all(1, 2, 1)
                reduce_all(2, 4, 2)
                pool.wait_ge(scales_ready, 2)
                for i in range(FC):
                    u = up[:, i, :]
                    pool.tensor_scalar(u, u, inverse[:, 2:3], MAGIC, ALU.mult, ALU.add).then_inc(pool_step, 1)
                    pool.wait_ge(pool_step, i + 1)
                    pool.tensor_scalar(u, u, -MAGIC, scale[:, 2:3], ALU.add, ALU.mult).then_inc(up_ready, 1)
                reduce_all(4, 5, 3)

            @block.scalar
            def _(act):
                chain = Chain(act, scalar_step)
                act.wait_ge(rounding_set, 2)

                def copy(n):
                    act.wait_ge(multiplied, n + 1)
                    half_banks = banks[:, n % 2 * 4:n % 2 * 4 + 4, :].rearrange("p q n -> p (q n)")
                    act.activation((gate if n < FC else up)[:, n % FC, :], half_banks, ACT.Copy).then_inc(copied, 1)

                for n in range(FC):
                    copy(n)
                for i in range(FC):
                    copy(FC + i)
                    act.wait_ge(gate_ready, i + 1)
                    if i >= HALVES:
                        act.wait_ge(half_free, i - HALVES + 1)
                    h = half[:, i % HALVES, :]
                    chain.step(act.activation(h, gate[:, i, :], ACT.Sigmoid))
                    chain.step(act.activation(h, h, ACT.Identity, bias=rounding[:, 0:1], scale=65536.0))
                    act.activation(h, h, ACT.Identity, bias=rounding[:, 1:2], scale=1.0 / 65536.0).then_inc(sigmoid_done, 1)

            @block.tensor
            def _(pe):
                for n in range(2 * FC):
                    w, i = n // FC, n % FC
                    if n >= 2:
                        pe.wait_ge(copied, n - 1)
                    for q in range(NC_T):
                        for k in range(DC):
                            last = pe.matmul(banks[:, n % 2 * 4 + q, :], in_turned[:, w, k, i * P:(i + 1) * P],
                                             x_turned[:, k, q * CH:(q + 1) * CH], start=(k == 0), stop=(k == DC - 1))
                    last.then_inc(multiplied, 1)
                pe.wait_ge(copied, 2 * FC)
                for i in range(FC):
                    pe.wait_ge(hidden_ready, i + 1)
                    for t in range(NT):
                        last = pe.matmul(banks[:, t // 2, (t % 2) * D:(t % 2 + 1) * D], gate[:, i, t * P:(t + 1) * P],
                                         down_turned[:, i, :], start=(i == 0 and t % 2 == 0), stop=(i == FC - 1 and t % 2 == 1))
                        if i == FC - 1 and t % 2:
                            last.then_inc(down_done, 1)



RH = 4
DK = D // RH
DV = 2 * D // RH
HALF = DK // 2
QK = 2 * D
VW = 2 * D
GAMMA = [1.0 - 2.0 ** (-5.0 - h) for h in range(RH)]
CHUNK_DECAY = [g ** P for g in GAMMA]


def retention(nc, ident, io, X, R):
    with ExitStack() as ctx:
        def sb(name, shape, dt=F32):
            return ctx.enter_context(nc.sbuf_tensor(name, shape, dt))

        qk = sb("ret_qk", [P, NT, QK])
        values = sb("ret_values", [P, NT, VW])
        gates = sb("ret_gates", [P, NT, VW])
        w_out = sb("ret_w_out", [P, RH, D])
        norm_w = sb("ret_norm_w", [P, 1])
        decay = sb("ret_decay", [P, RH, P])
        cross = sb("ret_cross", [P, RH])
        key_decay = sb("ret_key_decay", [P, RH])
        mean_square = sb("ret_mean_square", [P, NT, RH])
        with ExitStack() as inner:
            def isb(name, shape, dt=F32):
                return inner.enter_context(nc.sbuf_tensor(name, shape, dt))

            turned = isb("ret_x_turned", [P, DC, T])
            w_all = isb("ret_w_all", [P, DC, 3, CH])
            affine = isb("ret_affine", [P, 2, DC])
            rope = isb("ret_rope", [P, 2, NT, HALF])
            products = isb("ret_products", [P, 2, 2, QK])
            sigmoids = isb("ret_sigmoids", [P, 2, VW])

            def rows(name):
                return io[name].rearrange("(c p) n -> p c n", p=P)

            with nc.allow_non_contiguous_dma(reason="vectors of 256 values"):
                norm_block(nc, "norm_0c", ident, R, X, NT, P, True, loads=[
                    (w_all[:, :, 0, 0:D], rows("L1_attn_Wq")), (w_all[:, :, 0, D:QK], rows("L1_attn_Wk")),
                    (w_all[:, :, 1, :], rows("L1_attn_Wv")), (w_all[:, :, 2, :], rows("L1_attn_Wg")),
                    (w_out[:], io["L1_attn_Wo"].rearrange("(h p) n -> p h n", p=P)),
                    (affine[:, 0, :], io["L1_attn_ln_w"].rearrange("(c p) -> p c", p=P)),
                    (affine[:, 1, :], io["L1_attn_ln_b"].rearrange("(c p) -> p c", p=P)),
                    (norm_w[:], io["L1_attn_g_norm_w"].rearrange("(p a) -> p a", a=1)),
                    (rope[:], io["const_rope"]), (decay[:], io["const_decay"]), (cross[:], io["const_cross"]),
                    (key_decay[:], io["const_key_decay"]),
                ])
            norm_block(nc, "ret_norm", ident, X, R, NT, P, True, turned=turned, gain=affine[:, 0, :],
                       shift=affine[:, 1, :])

            with ExitStack() as sems:
                def sem(name):
                    return sems.enter_context(semaphore(nc, name))

                projected = sem("ret_projected")
                multiplied = sem("ret_multiplied")
                rotated = sem("ret_rotated")
                values_out = sem("ret_values_out")
                sigmoid_out = sem("ret_sigmoid_out")
                gates_out = sem("ret_gates_out")
                banks = sems.enter_context(nc.psum_tensor("ret_banks", [P, 2, 3, CH], F32))
                block = sems.enter_context(nc.Block())

                @block.tensor
                def _(pe):
                    for t in range(NT):
                        if t >= 2:
                            pe.wait_ge(gates_out, t - 1)
                            pe.wait_ge(sigmoid_out, t - 1)
                            pe.wait_ge(values_out, t - 1)
                            pe.wait_ge(multiplied, t - 1)
                        for w in range(3):
                            for k in range(DC):
                                last = pe.matmul(banks[:, t % 2, w, :], turned[:, k, t * P:(t + 1) * P],
                                                 w_all[:, k, w, :], start=(k == 0), stop=(k == DC - 1))
                        last.then_inc(projected, 1)

                @block.scalar
                def _(act):
                    for t in range(NT):
                        act.wait_ge(projected, t + 1)
                        act.activation(values[:, t, :], banks[:, t % 2, 1, :], ACT.Copy).then_inc(values_out, 1)
                        if t >= 2:
                            act.wait_ge(gates_out, t - 1)
                        act.activation(sigmoids[:, t % 2, :], banks[:, t % 2, 2, :], ACT.Sigmoid).then_inc(sigmoid_out, 1)

                @block.vector
                def _(dve):
                    for t in range(NT):
                        dve.wait_ge(projected, t + 1)
                        if t >= 2:
                            dve.wait_ge(rotated, t - 1)
                        for f in range(2):
                            last = dve.tensor_tensor(
                                products[:, t % 2, f, :].rearrange("p (h j) -> p h j", j=HALF),
                                banks[:, t % 2, 0, :].rearrange("p (h j) -> p h j", j=HALF),
                                spread(rope[:, f, t, :], 1, QK // HALF), ALU.mult)
                        last.then_inc(multiplied, 1)
                        dve.wait_ge(sigmoid_out, t + 1)
                        dve.tensor_tensor(gates[:, t, :], banks[:, t % 2, 2, :], sigmoids[:, t % 2, :],
                                          ALU.mult).then_inc(gates_out, 1)

                @block.gpsimd
                def _(pool):
                    for t in range(NT):
                        pool.wait_ge(multiplied, t + 1)
                        cos_x, sin_x = (products[:, t % 2, f, :].rearrange("p (h u j) -> p h u j", u=2, j=HALF)
                                        for f in range(2))
                        out = qk[:, t, :].rearrange("p (h u j) -> p h u j", u=2, j=HALF)
                        pool.tensor_tensor(out[:, :, 0], cos_x[:, :, 0], sin_x[:, :, 1], ALU.subtract)
                        pool.tensor_tensor(out[:, :, 1], cos_x[:, :, 1], sin_x[:, :, 0], ALU.add).then_inc(rotated, 1)

        with ExitStack() as sems:
            def sem(name):
                return sems.enter_context(semaphore(nc, name))

            def isb(name, shape, dt=F32):
                return sems.enter_context(nc.sbuf_tensor(name, shape, dt))

            qk_turned = isb("ret_qk_turned", [DK, 2, 2 * RH, P])
            decayed = isb("ret_decayed", [P, 2, RH, P])
            keys_decayed = isb("ret_keys_decayed", [P, 2, RH, DK])
            state = isb("ret_state", [DK, RH, DV])
            squares = isb("ret_squares", [P, 2, VW])
            turned_banks = sems.enter_context(nc.psum_tensor("ret_turned", [DK, 2 * RH, P], F32))
            score_banks = sems.enter_context(nc.psum_tensor("ret_scores", [P, 2, RH, P], F32))
            out_banks = sems.enter_context(nc.psum_tensor("ret_out", [P, 2, RH, DV], F32))
            state_bank = sems.enter_context(nc.psum_tensor("ret_state_bank", [DK, RH, DV], F32))
            qk_transposed = sem("ret_qk_transposed")
            turned_copied = sem("ret_turned_copied")
            scored = sem("ret_scored")
            decayed_out = sem("ret_decayed_out")
            keys_out = sem("ret_keys_out")
            chunk_out = sem("ret_chunk_out")
            state_out = sem("ret_state_out")
            state_in = sem("ret_state_in")
            head_out = sem("ret_head_out")
            squared = sem("ret_squared")
            reduced = sem("ret_reduced")
            block = sems.enter_context(nc.Block())

            @block.tensor
            def _(pe):
                def turn(t):
                    if t:
                        pe.wait_ge(turned_copied, t)
                    for b in range(2 * RH):
                        last = pe.transpose(turned_banks[:, b, :], qk[:, t, b * DK:(b + 1) * DK], ident[:])
                    last.then_inc(qk_transposed, 1)

                def score(t):
                    pe.wait_ge(turned_copied, t + 1)
                    if t >= 2:
                        pe.wait_ge(decayed_out, t - 1)
                    for h in range(RH):
                        last = pe.matmul(score_banks[:, t % 2, h, :], qk_turned[:, t % 2, RH + h, :],
                                         qk_turned[:, t % 2, h, :], start=True, stop=True)
                    last.then_inc(scored, 1)

                turn(0)
                score(0)
                turn(1)
                for t in range(NT):
                    if t + 1 < NT:
                        score(t + 1)
                    pe.wait_ge(decayed_out, t + 1)
                    if t >= 2:
                        pe.wait_ge(head_out, t - 1)
                    if t:
                        pe.wait_ge(state_in, t)
                    for h in range(RH):
                        out = out_banks[:, t % 2, h, :]
                        last = pe.matmul(out, decayed[:, t % 2, h, :], values[:, t, h * DV:(h + 1) * DV],
                                         start=True, stop=(t == 0))
                        if t:
                            last = pe.matmul(out, qk_turned[:, t % 2, h, :], state[:, h, :],
                                             start=False, stop=True)
                    last.then_inc(chunk_out, 1)
                    if t + 1 < NT:
                        pe.wait_ge(keys_out, t + 1)
                        for h in range(RH):
                            last = pe.matmul(state_bank[:, h, :], keys_decayed[:, t % 2, h, :],
                                             values[:, t, h * DV:(h + 1) * DV], start=True, stop=True)
                        last.then_inc(state_out, 1)
                    if t + 2 < NT:
                        turn(t + 2)

            @block.scalar
            def _(act):
                for t in range(NT + 2):
                    if t < NT:
                        act.wait_ge(qk_transposed, t + 1)
                        if t >= 2:
                            act.wait_ge(chunk_out, t - 1)
                        act.activation(qk_turned[:, t % 2].rearrange("p b n -> p (b n)"),
                                       turned_banks[:].rearrange("p b n -> p (b n)"), ACT.Copy).then_inc(turned_copied, 1)
                    if t >= 2:
                        u = t - 2
                        act.wait_ge(head_out, u + 1)
                        if u >= 2:
                            act.wait_ge(reduced, u - 1)
                        act.activation(squares[:, u % 2, :], qk[:, u, :], ACT.Square).then_inc(squared, 1)

            @block.gpsimd
            def _(pool):
                for t in range(NT - 1):
                    if t >= 2:
                        pool.wait_ge(state_out, t - 1)
                    pool.tensor_tensor(keys_decayed[:, t % 2], qk[:, t, D:QK].rearrange("p (h d) -> p h d", h=RH),
                                       spread(key_decay[:], 2, DK), ALU.mult).then_inc(keys_out, 1)

            @block.vector
            def _(dve):
                def decay_scores(t):
                    dve.wait_ge(scored, t + 1)
                    if t >= 2:
                        dve.wait_ge(chunk_out, t - 1)
                    dve.tensor_tensor(decayed[:, t % 2], score_banks[:, t % 2], decay[:], ALU.mult).then_inc(decayed_out, 1)

                decay_scores(0)
                for t in range(NT):
                    if t + 1 < NT:
                        decay_scores(t + 1)
                        dve.wait_ge(state_out, t + 1)
                        if t == 0:
                            dve.tensor_copy(state[:], state_bank[:]).then_inc(state_in, 1)
                        else:
                            for h in range(RH):
                                last = dve.scalar_tensor_tensor(
                                    out=state[:, h, :], in0=state[:, h, :], scalar=CHUNK_DECAY[h],
                                    in1=state_bank[:, h, :], op0=ALU.mult, op1=ALU.add)
                            last.then_inc(state_in, 1)
                    dve.wait_ge(chunk_out, t + 1)
                    if t + 1 < NT:
                        dve.wait_ge(keys_out, t + 1)
                    dve.tensor_tensor(qk[:, t, :].rearrange("p (h d) -> p h d", h=RH), out_banks[:, t % 2],
                                      spread(cross[:], 2, DV), ALU.mult).then_inc(head_out, 1)
                    if t:
                        dve.wait_ge(squared, t)
                        dve.tensor_reduce(mean_square[:, t - 1, :], squares[:, (t - 1) % 2].rearrange(
                            "p (h d) -> p h d", h=RH), AX.X, ALU.add).then_inc(reduced, 1)
                dve.wait_ge(squared, NT)
                dve.tensor_reduce(mean_square[:, NT - 1, :], squares[:, (NT - 1) % 2].rearrange(
                    "p (h d) -> p h d", h=RH), AX.X, ALU.add).then_inc(reduced, 1)

        with ExitStack() as sems:
            def sem(name):
                return sems.enter_context(semaphore(nc, name))

            out_turned = sems.enter_context(nc.sbuf_tensor("ret_out_turned", [P, 2, CH], F32))
            inverse = sems.enter_context(nc.sbuf_tensor("ret_inverse", [P, NT, RH], F32))
            step = sem("ret_norm_step")
            variance = sem("ret_variance")
            rooted = sem("ret_rooted")
            normed = sem("ret_normed")
            gated = sem("ret_gated")
            w_scaled = sem("ret_w_scaled")
            heads_turned = sem("ret_heads_turned")
            heads_copied = sem("ret_heads_copied")
            out_done = sem("ret_out_done")
            summed = sem("ret_summed")
            turned_banks = sems.enter_context(nc.psum_tensor("ret_heads_banks", [P, 2, CH], F32))
            out_banks = sems.enter_context(nc.psum_tensor("ret_proj_banks", [P, 2, CH], F32))
            block = sems.enter_context(nc.Block())

            @block.vector
            def _(dve):
                chain = Chain(dve, step)
                dve.tensor_scalar(mean_square[:], mean_square[:], 1.0 / DV, EPS, ALU.mult, ALU.add).then_inc(variance, 1)
                for h in range(RH):
                    last = dve.tensor_scalar(w_out[:, h, :], w_out[:, h, :], norm_w[:, 0:1], None, ALU.mult)
                last.then_inc(w_scaled, 1)
                dve.wait_ge(rooted, 1)
                chain.step(dve.reciprocal(inverse[:], mean_square[:]))
                for t in range(NT + 2):
                    if t < NT:
                        heads = qk[:, t, :].rearrange("p (h d) -> p h d", h=RH)
                        dve.tensor_tensor(heads, heads, spread(inverse[:, t, :], 2, DV), ALU.mult).then_inc(normed, 1)
                    if t >= 2:
                        u = t - 2
                        dve.wait_ge(out_done, u + 1)
                        dve.scalar_tensor_tensor(out=R[:, u, :], in0=X[:, u, :], scalar=2.0,
                                                 in1=out_banks[:, u % 2, 0:D], op0=ALU.mult, op1=ALU.add).then_inc(summed, 1)

            @block.gpsimd
            def _(pool):
                for t in range(NT):
                    pool.wait_ge(normed, t + 1)
                    pool.tensor_tensor(qk[:, t, :], qk[:, t, :], gates[:, t, :], ALU.mult).then_inc(gated, 1)

            @block.scalar
            def _(act):
                act.wait_ge(variance, 1)
                act.activation(mean_square[:], mean_square[:], ACT.Sqrt).then_inc(rooted, 1)
                for t in range(NT):
                    act.wait_ge(heads_turned, t + 1)
                    if t >= 2:
                        act.wait_ge(out_done, t - 1)
                    act.activation(out_turned[:, t % 2, :], turned_banks[:, t % 2, :], ACT.Copy).then_inc(heads_copied, 1)

            @block.tensor
            def _(pe):
                pe.wait_ge(w_scaled, 1)
                for t in range(NT + 1):
                    if t < NT:
                        pe.wait_ge(gated, t + 1)
                        if t >= 2:
                            pe.wait_ge(heads_copied, t - 1)
                        for h in range(RH):
                            last = pe.transpose(turned_banks[:, t % 2, h * P:(h + 1) * P], qk[:, t, h * DV:(h + 1) * DV],
                                                ident[:])
                        last.then_inc(heads_turned, 1)
                    if t:
                        u = t - 1
                        pe.wait_ge(heads_copied, u + 1)
                        if u >= 2:
                            pe.wait_ge(summed, u - 1)
                        for h in range(RH):
                            last = pe.matmul(out_banks[:, u % 2, 0:D], out_turned[:, u % 2, h * P:(h + 1) * P],
                                             w_out[:, h, :], start=(h == 0), stop=(h == RH - 1))
                        last.then_inc(out_done, 1)


def retention_constants():
    f4 = np.float32
    inv_freq = (f4(1) / f4(10000) ** (np.arange(0, DK, 2, dtype=f4) / f4(DK))).astype(f4)
    angles = np.arange(T, dtype=f4)[:, None] * inv_freq[None, :]
    rope = np.stack([np.cos(angles), np.sin(angles)]).astype(f4).reshape(2, NT, P, HALF).transpose(2, 0, 1, 3)
    gamma = np.array(GAMMA)
    i = np.arange(P)
    decay = np.where(i[None, None, :] >= i[:, None, None], gamma[None, :, None] ** -(1.0 + i[:, None, None]), 0.0)
    cross = gamma[None, :] ** (i[:, None] + 1.0) * DK ** -0.5
    key_decay = gamma[None, :] ** (P - 1.0 - i[:, None])
    return {"const_rope": np.ascontiguousarray(rope), "const_decay": decay.astype(f4), "const_cross": cross.astype(f4),
            "const_key_decay": key_decay.astype(f4)}


BF16 = mybir.dt.bfloat16
I16 = mybir.dt.int16
BF16_ONE = 0x3F80


E = 16
EG = 4
GS = E // EG
EI = 128
SC = 4
UNITS = E + SC
TOP_K = 4
TOPK_GROUP = 2
ROUTED_SCALING = 2.5


def experts_ffn(nc, ident, io, X, R):
    with ExitStack() as ctx:
        def sb(name, shape, dt=F32):
            return ctx.enter_context(nc.sbuf_tensor(name, shape, dt))

        x_turned = sb("moe_x_turned", [P, DC, T])
        w_up = sb("moe_w_up", [P, UNITS, DC, EI])
        w_down = sb("moe_w_down", [P, UNITS, D])
        combine = sb("moe_combine", [P, T], BF16)
        pick = sb("moe_pick", [P, E, EI], BF16)
        shared = sb("moe_shared", [P, SC, T])
        with ExitStack() as sems:
            def isb(name, shape, dt=F32):
                return sems.enter_context(nc.sbuf_tensor(name, shape, dt))

            shared_up = isb("moe_shared_up", [P, 2, CH])
            gate_rows = isb("moe_gate_rows", [E, D])
            gate_turned = isb("moe_gate_turned", [P, DC, E])
            earlier = isb("moe_earlier", [P, E, E])
            norm_block(nc, "norm_1b", ident, X, X, NT, P, True, turned=x_turned, loads=[
                (gate_rows[:], io["L1_ffn_gate_weight"]), (earlier[:], io["const_earlier"]), (pick[:].bitcast(I16), io["const_pick"]),
                (w_up[:, 0:E], io["L1_ffn_expert_up"].rearrange("e (c p) n -> p e c n", p=P)),
                (w_down[:, 0:E, :], io["L1_ffn_expert_down"].rearrange("e p n -> p e n")),
            ] + [(w_up[:, E + s], io["L1_ffn_shared_up"].rearrange("(c p) (s n) -> p s c n", p=P, n=EI)[:, s])
                 for s in range(SC)]
                + [(w_down[:, E:UNITS, :], io["L1_ffn_shared_down"].rearrange("(s p) n -> p s n", p=P))])

            scores = isb("moe_scores", [P, NT, E])
            masked = isb("moe_masked", [P, NT, E])
            chosen = isb("moe_chosen", [P, NT, E])
            compare = isb("moe_compare", [P, NT, E, E])
            ties = isb("moe_ties", [P, NT, E, E])
            rank = isb("moe_rank", [P, NT, E])
            group_score = isb("moe_group_score", [P, NT, EG])
            total = isb("moe_total", [P, NT])
            rest = isb("moe_rest", [E, 2, T])
            banks = sems.enter_context(nc.psum_tensor("moe_route_banks", [P, 8, CH], F32))

            def sem(name):
                return sems.enter_context(semaphore(nc, name))

            gate_done = sem("moe_gate_done")
            gate_copied = sem("moe_gate_copied")
            logits_done = sem("moe_logits_done")
            scores_done = sem("moe_scores_done")
            step = sem("moe_route_step")
            combined = sem("moe_combined")
            combine_turned = sem("moe_combine_turned")
            shared_ready = sem("moe_shared_ready")
            shared_out = sem("moe_shared_out")
            shared_gated = sem("moe_shared_gated")
            shared_jobs = [(s, slice(q * CH, (q + 1) * CH)) for s in range(SC) for q in range(NC_T)]
            block = sems.enter_context(nc.Block())

            @block.tensor
            def _(pe):
                for c in range(DC):
                    last = pe.transpose(banks[:, 0, c * E:(c + 1) * E], gate_rows[:, c * P:(c + 1) * P], ident[0:E, 0:E])
                last.then_inc(gate_done, 1)
                pe.wait_ge(gate_copied, 1)
                for t in range(NT):
                    for c in range(DC):
                        last = pe.matmul(banks[:, 1, t * E:(t + 1) * E], x_turned[:, c, t * P:(t + 1) * P],
                                         gate_turned[:, c, :], start=(c == 0), stop=(c == DC - 1))
                last.then_inc(logits_done, 1)
                for i, (s, at) in enumerate(shared_jobs):
                    if i >= 2:
                        pe.wait_ge(shared_out, i - 1)
                    for k in range(DC):
                        last = pe.matmul(banks[:, 2 + i % 2, :], w_up[:, E + s, k, :], x_turned[:, k, at],
                                         start=(k == 0), stop=(k == DC - 1))
                    last.then_inc(shared_ready, 1)
                pe.wait_ge(combined, 1)
                for t in range(NT):
                    last = pe.transpose(banks[0:E, 4 + t // 4, (t % 4) * P:(t % 4 + 1) * P], masked[:, t, :], ident[:])
                last.then_inc(combine_turned, 1)

            @block.scalar
            def _(act):
                act.wait_ge(gate_done, 1)
                act.activation(gate_turned[:].rearrange("p c e -> p (c e)"), banks[:, 0, 0:DC * E], ACT.Copy).then_inc(gate_copied, 1)
                act.wait_ge(logits_done, 1)
                act.activation(scores[:].rearrange("p t e -> p (t e)"), banks[:, 1, 0:NT * E], ACT.Sigmoid).then_inc(scores_done, 1)
                for i, (s, at) in enumerate(shared_jobs):
                    act.wait_ge(shared_ready, i + 1)
                    if i >= 2:
                        act.wait_ge(shared_gated, i - 1)
                    act.activation(shared[:, s, at], banks[:, 2 + i % 2, :], ACT.Sigmoid)
                    act.activation(shared_up[:, i % 2, :], banks[:, 2 + i % 2, :], ACT.Copy).then_inc(shared_out, 1)

            @block.gpsimd
            def _(pool):
                for i, (s, at) in enumerate(shared_jobs):
                    pool.wait_ge(shared_out, i + 1)
                    pool.tensor_tensor(shared[:, s, at], shared[:, s, at], shared_up[:, i % 2, :],
                                       ALU.mult).then_inc(shared_gated, 1)

            @block.vector
            def _(dve):
                chain = Chain(dve, step)

                def select(values, n, k, count, out):
                    def square(ap):
                        return ap.rearrange("p t e j -> p (t e j)")[:, 0:n * k * k].rearrange(
                            "p (n a b) -> p n a b", a=k, b=k)
                    larger, equal = square(compare[:]), square(ties[:])
                    other, own = spread(values, 2, k), spread(values, 3, k)
                    chain(dve.tensor_tensor(larger, other, own, ALU.is_gt))
                    chain.step(dve.tensor_tensor(equal, other, own, ALU.is_equal))
                    before = spread(earlier[:, 0:k, 0:k], 1, n)
                    chain.step(dve.tensor_tensor(equal, equal, before, ALU.mult))
                    chain.step(dve.tensor_tensor(larger, larger, equal, ALU.add))
                    ranks = rank[:].rearrange("p t e -> p (t e)")[:, 0:n * k].rearrange("p (n e) -> p n e", e=k)
                    chain.step(dve.tensor_reduce(ranks, larger, AX.X, ALU.add))
                    chain.step(dve.tensor_scalar(out, ranks, float(count), None, ALU.is_lt))

                dve.wait_ge(scores_done, 1)
                by_group = scores[:].rearrange("p t (g s) -> p (t g) s", s=GS)
                chosen_by_group = chosen[:].rearrange("p t (g s) -> p (t g) s", s=GS)
                select(by_group, NT * EG, GS, 2, chosen_by_group)
                chain.step(dve.tensor_tensor(chosen[:], chosen[:], scores[:], ALU.mult))
                chain.step(dve.tensor_reduce(group_score[:].rearrange("p t g -> p (t g)"), chosen_by_group, AX.X, ALU.add))
                group_chosen = masked[:, :, 0:EG]
                select(group_score[:], NT, EG, TOPK_GROUP, group_chosen)
                chain.step(dve.tensor_copy(group_score[:], group_chosen))
                chain.step(dve.tensor_tensor(masked[:].rearrange("p t (g s) -> p (t g) s", s=GS), by_group,
                                             spread(group_score[:].rearrange("p t g -> p (t g)"), 2, GS), ALU.mult))
                select(masked[:], NT, E, TOP_K, chosen[:])
                chain.step(dve.tensor_tensor(chosen[:], chosen[:], scores[:], ALU.mult))
                chain.step(dve.tensor_reduce(total[:], chosen[:], AX.X, ALU.add))
                chain.step(dve.tensor_scalar(total[:], total[:], 1e-20, None, ALU.add))
                chain.step(dve.reciprocal(total[:], total[:]))
                chain.step(dve.tensor_tensor(chosen[:], chosen[:], spread(total[:], 2, E), ALU.mult))
                chain(dve.memset(combine[:], 0.0))
                dve.tensor_scalar(masked[:], chosen[:], ROUTED_SCALING, None, ALU.mult).then_inc(combined, 1)
                dve.wait_ge(combine_turned, 1)
                chain.wait()
                turned = banks[0:E, 4:8, :].rearrange("p b n -> p (b n)")
                chain.step(dve.tensor_copy(combine[0:E, :], turned))
                chain.step(dve.tensor_tensor(rest[:, 0, :], turned, combine[0:E, :], ALU.subtract))
                chain.step(dve.tensor_copy(combine[32:32 + E, :], rest[:, 0, :]))
                chain.step(dve.tensor_copy(rest[:, 1, :], combine[32:32 + E, :]))
                chain.step(dve.tensor_tensor(rest[:, 1, :], rest[:, 0, :], rest[:, 1, :], ALU.subtract))
                dve.tensor_copy(combine[64:64 + E, :], rest[:, 1, :])

        with ExitStack() as sems:
            def sem(name):
                return sems.enter_context(semaphore(nc, name))

            def isb(name, shape, dt=F32):
                return sems.enter_context(nc.sbuf_tensor(name, shape, dt))

            sigmoids = isb("moe_sigmoids", [P, 2, CH])
            hidden = isb("moe_hidden", [P, 2, CH])
            out_rows = isb("moe_out_rows", [P, DC, CH])
            up_banks = sems.enter_context(nc.psum_tensor("moe_up_banks", [P, 2, CH], F32))
            weight_banks = sems.enter_context(nc.psum_tensor("moe_weight_banks", [P, 2, CH], F32))
            out_banks = sems.enter_context(nc.psum_tensor("moe_out_banks", [P, DC, CH], F32))
            turned_banks = sems.enter_context(nc.psum_tensor("moe_turned_banks", [P, DC, CH], F32))
            up_done = sem("moe_up_done")
            sigmoid_done = sem("moe_sigmoid_done")
            gated = sem("moe_gated")
            hidden_done = sem("moe_hidden_done")
            down_done = sem("moe_down_done")
            out_copied = sem("moe_out_copied")
            out_turned = sem("moe_out_turned")
            summed = sem("moe_summed")
            block = sems.enter_context(nc.Block())

            @block.tensor
            def _(pe):
                pe.sem_inc(down_done, 2)
                with pe.Fori(0, NC_T, 1) as n:
                    def up(u):
                        pe.wait_ge(hidden_done, n * E + (u + 1))
                        for k in range(DC):
                            pe.matmul(up_banks[:, u % 2, :], w_up[:, u, k, :], x_turned[:, k, bass.ds(n * CH, CH)],
                                      start=(k == 0), stop=(k == DC - 1))
                        pe.matmul(weight_banks[:, u % 2, :], pick[:, u, :], combine[:, bass.ds(n * CH, CH)],
                                  start=True, stop=True).then_inc(up_done, 1)

                    up(0)
                    up(1)
                    pe.wait_ge(out_copied, n + 1)
                    for s in range(SC):
                        for c in range(DC):
                            pe.matmul(out_banks[:, c, :], w_down[:, E + s, c * P:(c + 1) * P],
                                      shared[:, s, bass.ds(n * CH, CH)], start=(s == 0), stop=False)
                    for u in range(E):
                        if 0 < u < E - 1:
                            up(u + 1)
                        pe.wait_ge(hidden_done, n * E + (u + 3))
                        for c in range(DC):
                            last = pe.matmul(out_banks[:, c, :], w_down[:, u, c * P:(c + 1) * P], hidden[:, u % 2, :],
                                             start=False, stop=(u == E - 1))
                        last.then_inc(down_done, 1)
                    pe.wait_ge(out_copied, n + 2)
                    pe.wait_ge(summed, n + 1)
                    for j in range(4):
                        for c in range(DC):
                            last = pe.transpose(turned_banks[:, j // 2, ((j % 2) * DC + c) * P:((j % 2) * DC + c + 1) * P],
                                                out_rows[:, c, j * P:(j + 1) * P], ident[:])
                    last.then_inc(out_turned, 1)

            @block.scalar
            def _(act):
                act.sem_inc(out_copied, 1)
                with act.Fori(0, NC_T, 1) as n:
                    for u in range(E):
                        act.wait_ge(up_done, n * E + (u + 1))
                        act.wait_ge(hidden_done, n * E + (u + 1))
                        act.activation(sigmoids[:, u % 2, :], up_banks[:, u % 2, :], ACT.Sigmoid).then_inc(sigmoid_done, 1)
                    act.wait_ge(down_done, n * E + (E + 2))
                    act.wait_ge(summed, n + 1)
                    for c in range(DC):
                        last = act.activation(out_rows[:, c, :], out_banks[:, c, :], ACT.Copy)
                    last.then_inc(out_copied, 1)

            @block.vector
            def _(dve):
                dve.sem_inc(hidden_done, 2)
                dve.sem_inc(summed, 1)
                with dve.Fori(0, NC_T, 1) as n:
                    for u in range(E):
                        dve.wait_ge(sigmoid_done, n * E + (u + 1))
                        dve.wait_ge(down_done, n * E + (u + 1))
                        s = sigmoids[:, u % 2, :]
                        dve.tensor_tensor(s, up_banks[:, u % 2, :], s, ALU.mult).then_inc(gated, 1)
                        dve.wait_ge(gated, n * E + (u + 1))
                        dve.tensor_tensor(hidden[:, u % 2, :], weight_banks[:, u % 2, :], s, ALU.mult).then_inc(hidden_done, 1)
                    dve.wait_ge(out_turned, n + 1)
                    for b in range(2):
                        last = dve.tensor_tensor(R[:, bass.ds(n * 4 + 2 * b, 2), :].rearrange("p a b -> p (a b)"),
                                                 turned_banks[:, b, :],
                                                 X[:, bass.ds(n * 4 + 2 * b, 2), :].rearrange("p a b -> p (a b)"), ALU.add)
                    last.then_inc(summed, 1)


def expert_constants():
    e = np.arange(E)
    earlier = np.broadcast_to((e[None, :] < e[:, None]).astype(np.float32), (P, E, E))
    row = np.arange(P)
    pick = np.where((row[:, None] % 32 == e[None, :]) & (row[:, None] < 96), BF16_ONE, 0).astype(np.int16)
    return {"const_earlier": np.ascontiguousarray(earlier),
            "const_pick": np.ascontiguousarray(np.broadcast_to(pick[:, :, None], (P, E, EI)))}



XH = 16
XD = D // XH
PAIRS = XH // 2
NEG = -1e9
S_CH = [(n * CH, min(CH, S2 - n * CH)) for n in range((S2 + CH - 1) // CH)]
KEY_ROWS = [P] * (CT - 1) + [CLAST]
LT = 3
L_SLOTS = 4
PT_SLOTS = 8
BY_SCALAR, BY_VECTOR = (0, 1), (2, 3)
WEIGHTED = 8 * P


def masked_attention(nc, ident, io, X, scratch):
    q_parts = nc.dram_tensor("xa_q_parts", (2, D, T), F16, kind="Internal").ap()
    k_parts = nc.dram_tensor("xa_k_parts", (2, D, S2), F16, kind="Internal").ap()
    with ExitStack() as ctx:
        def sb(name, shape, dt=F32):
            return ctx.enter_context(nc.sbuf_tensor(name, shape, dt))

        k_stack = sb("xa_k_stack", [P, PAIRS, S2], F16)
        q_stack = sb("xa_q_stack", [P, 2, XH, P], F16)
        v = sb("xa_v", [P, CT, D + XD])
        w_out = sb("xa_w_out", [P, DC, D])
        k_rows, q_rows = (1, 1, 0, 0), (1, 0, 1, 0)

        def stack_rows(parity, term):
            lo = 64 * parity + XD * term
            return slice(lo, lo + XD)

        with ExitStack() as inner:
            def isb(name, shape, dt=F32):
                return inner.enter_context(nc.sbuf_tensor(name, shape, dt))

            def sem(name):
                return inner.enter_context(semaphore(nc, name))

            context = isb("xa_context", [P, CT, D])
            c_turned = isb("xa_c_turned", [P, DC, S2])
            x_turned = isb("xa_x_turned", [P, DC, T])
            w = isb("xa_w", [P, 3, DC, D])
            bias = isb("xa_bias", [P, 2, DC])
            v_bias = isb("xa_v_bias", [P, D])
            out_bias = isb("xa_out_bias", [P, D])
            parts = isb("xa_parts", [P, 2, DC, T], F16)
            ctx_rows = io["ctx_1024"].rearrange("a s d -> (a s) d")
            with nc.allow_non_contiguous_dma(reason="vectors of 256 values"):
                norm_block(nc, "norm_1a", ident, scratch, X, NT, P, True, turned=x_turned, loads=[
                    (context[:, 0:CT - 1, :], ctx_rows[0:(CT - 1) * P].rearrange("(i p) d -> p i d", p=P)),
                    (context[0:CLAST, CT - 1, :], ctx_rows[(CT - 1) * P:S2]),
                    (w_out[:], io["L1_xattn_wo_k"].rearrange("(c p) n -> p c n", p=P)),
                    (v_bias[:], io["L1_xattn_wv_b"].rearrange("(a n) -> a n", a=1).broadcast_to([P, D])),
                    (out_bias[:], io["L1_xattn_wo_b"].rearrange("(a n) -> a n", a=1).broadcast_to([P, D])),
                ] + [(w[:, n], io[f"L1_xattn_w{x}_k"].rearrange("(c p) n -> p c n", p=P)) for n, x in enumerate("qkv")]
                    + [(bias[:, n, :], io[f"L1_xattn_w{x}_b"].rearrange("(c p) -> p c", p=P)) for n, x in enumerate("qk")])
            norm_block(nc, "xa_turn_c", ident, context, context, CT, CLAST, False, turned=c_turned)

            projected = sem("xa_projected")
            high_out = sem("xa_high_out")
            low_out = sem("xa_low_out")
            v_out = sem("xa_v_out")
            cleared = sem("xa_cleared")
            kept = sem("xa_kept")
            stacked = sem("xa_stacked")
            banks = inner.enter_context(nc.psum_tensor("xa_prep_banks", [P, 4, CH], F32))
            v_banks = inner.enter_context(nc.psum_tensor("xa_v_banks", [P, 4, 2, D], F32))
            v_done = sem("xa_v_done")
            jobs = [(1, c, lo, n) for c in range(DC) for lo, n in S_CH]
            k_jobs = len(jobs)
            jobs += [(0, c, lo, CH) for c in range(DC) for lo in range(0, T, CH)]
            v_pairs = (CT + 1) // 2
            block = inner.enter_context(nc.Block())

            @block.tensor
            def _(pe):
                for j, (n, c, lo, width) in enumerate(jobs):
                    if j >= 4:
                        pe.wait_ge(low_out, j - 3)
                    src = x_turned if n == 0 else c_turned
                    for k in range(DC):
                        last = pe.matmul(banks[:, j % 4, 0:width], w[:, n, k, c * P:(c + 1) * P],
                                         src[:, k, lo:lo + width], start=(k == 0), stop=(k == DC - 1))
                    last.then_inc(projected, 1)
                for i in range(v_pairs):
                    if i >= 4:
                        pe.wait_ge(v_out, i - 3)
                    for t in range(2 * i, min(2 * i + 2, CT)):
                        n = KEY_ROWS[t]
                        for k in range(DC):
                            last = pe.matmul(v_banks[0:n, i % 4, t % 2, :], c_turned[:, k, t * P:t * P + n], w[:, 2, k, :],
                                             start=(k == 0), stop=(k == DC - 1))
                    last.then_inc(v_done, 1)

            @block.scalar
            def _(act):
                for j, (n, c, lo, width) in enumerate(jobs):
                    act.wait_ge(projected, j + 1)
                    if j == k_jobs:
                        act.wait_ge(kept, 16)
                    act.activation(parts[:, 0, c, lo:lo + width], banks[:, j % 4, 0:width], ACT.Identity,
                                   bias=bias[:, n, c:c + 1]).then_inc(high_out, 1)

            @block.vector
            def _(dve):
                for j, (n, c, lo, width) in enumerate(jobs):
                    dve.wait_ge(high_out, j + 1)
                    dve.scalar_tensor_tensor(out=parts[:, 1, c, lo:lo + width], in0=banks[:, j % 4, 0:width],
                                             scalar=bias[:, n, c:c + 1], in1=parts[:, 0, c, lo:lo + width],
                                             op0=ALU.add, op1=ALU.subtract).then_inc(low_out, 1)
                for i in range(v_pairs):
                    dve.wait_ge(v_done, i + 1)
                    members = range(2 * i, min(2 * i + 2, CT))
                    for t in members:
                        n = KEY_ROWS[t]
                        last = dve.tensor_tensor(v[0:n, t, 0:D], v_banks[0:n, i % 4, t % 2, :], v_bias[0:n, :], ALU.add)
                    last.then_inc(v_out, 1)

            @block.gpsimd
            def _(pool):
                pool.memset(v[:, :, D:D + XD], 0.0)
                pool.memset(q_stack[:], 0.0)
                pool.tensor_tensor(X[:], X[:], spread(out_bias[:], 1, NT), ALU.add)

            @block.sync
            def _(sync):
                sync.wait_ge(high_out, k_jobs)
                sync.wait_ge(low_out, k_jobs)
                sync.dma_start(k_parts.rearrange("u (c p) s -> p (u c) s", p=P),
                               parts[:, :, :, 0:S2].rearrange("p u c s -> p (u c) s")).then_inc(kept, 16)
                sync.wait_ge(kept, 16)
                for b in range(4):
                    for parity in range(2):
                        sync.dma_start(k_stack[stack_rows(parity, b)], k_parts[k_rows[b]].rearrange(
                            "(i a j) s -> a j i s", a=2, j=XD)[parity]).then_inc(stacked, 16)
                sync.wait_ge(high_out, len(jobs))
                sync.wait_ge(low_out, len(jobs))
                sync.dma_start(q_parts.rearrange("u (c p) s -> p (u c) s", p=P),
                               parts[:].rearrange("p u c s -> p (u c) s")).then_inc(kept, 16)
                sync.wait_ge(kept, 32)
                sync.wait_ge(stacked, 8 * 16)

        with ExitStack() as inner:
            def isb(name, shape, dt=F32):
                return inner.enter_context(nc.sbuf_tensor(name, shape, dt))

            def sem(name):
                return inner.enter_context(semaphore(nc, name))

            negative = isb("xa_negative", [P, 2, S2])
            group = isb("xa_group", [P, 2, S2])
            group_turned = isb("xa_group_turned", [P, 2, CT - WEIGHTED // P, P])
            more_rows = isb("xa_more_rows", [P, 2, S2])
            spare = scratch[:].rearrange("p i d -> p (i d)")
            rows = [spare[:, 0:S2], spare[:, S2 + 7:2 * S2 + 7], more_rows[:, 0, :], more_rows[:, 1, :]]
            turned = isb("xa_probs_turned", [P, PT_SLOTS, CT, P])
            peaks = isb("xa_peaks", [P, 2 * XH])
            sums = isb("xa_sums", [P, 2, XH])
            inverse = isb("xa_inverse", [P, 2, XH])
            heads = isb("xa_heads", [P, 4, P])
            heads_normed = isb("xa_heads_normed", [P, D])
            heads_turned = isb("xa_heads_turned", [P, DC, P])
            gate = isb("xa_gate", [P, 4])
            score_banks = inner.enter_context(nc.psum_tensor("xa_score_banks", [P, 4 * CH], F32))
            turn_banks = inner.enter_context(nc.psum_tensor("xa_turn_banks", [P, 2, CH], F32))
            value_bank = inner.enter_context(nc.psum_tensor("xa_value_bank", [P, 4, P], F32))
            misc_bank = inner.enter_context(nc.psum_tensor("xa_misc_bank", [P, CH], F32))

            q_loaded = [sem(f"xa_q_loaded_{b}") for b in range(2)]
            mask_loaded = [sem(f"xa_mask_loaded_{b}") for b in range(2)]
            group_loaded = [sem(f"xa_group_loaded_{b}") for b in range(2)]
            negated = sem("xa_negated")
            mask_flipped = sem("xa_mask_flipped")
            scored = sem("xa_scored")
            logits_out = sem("xa_logits_out")
            exp_out = sem("xa_exp_out")
            weighted = sem("xa_weighted")
            bank_turned = [sem(f"xa_bank_turned_{b}") for b in range(2)]
            bank_moved = [sem(f"xa_bank_moved_{b}") for b in range(2)]
            group_valued = sem("xa_group_valued")
            heads_copied = sem("xa_heads_copied")
            misc_ready = sem("xa_misc_ready")
            misc_read = sem("xa_misc_read")
            inverted = sem("xa_inverted")
            gate_cleared = sem("xa_gate_cleared")
            block = inner.enter_context(nc.Block())

            n_pairs = NT // 2
            FINISHED = 10
            VALUE_PARTS = [range(n * CT // 4, (n + 1) * CT // 4) for n in range(4)]

            def await_(eng, semaphore, value):
                if not isinstance(value, int) or value > 0:
                    eng.wait_ge(semaphore, value)

            def back(j, u, lag):
                return (j, u - lag) if u >= lag else (j - 1, u - lag + 2 * XH)

            def misc_number(j, u, k):
                if isinstance(j, int) and j == n_pairs:
                    return j * 10 + (k - 1) - 2
                return j * 10 + (5 * (u // XH) + k - 1)

            class Step:

                def __init__(self, u, first, last, tail):
                    h = u % XH
                    self.head = not tail
                    self.turn = (not first or u >= LT) and (not tail or u < LT)
                    part = (u - LT) % 4
                    self.value = part if (not first or u - part >= LT + 4) and (not tail or u < LT + 4) else None
                    self.copy_heads = h == 6 and (not first or u >= XH)
                    self.finish = h - 7 if 7 <= h < FINISHED and (not first or u >= XH) else None
                    self.next_group = h - FINISHED if FINISHED <= h < FINISHED + 2 and not tail and not (last and u >= XH) else None

            def stream(eng, step):
                def pair(j, first=False, last=False):
                    for u in range(2 * XH):
                        step(j, u, Step(u, first, last, False))
                pair(0, first=True)
                with eng.Fori(1, n_pairs - 1, 1) as j:
                    pair(j)
                pair(n_pairs - 1, last=True)
                for u in range(FINISHED):
                    step(n_pairs, u, Step(u, False, False, True))

            def group_blocks(b):
                return [(i, KEY_ROWS[i]) for i in range(4 * b, min(4 * b + 4, CT))]

            @block.tensor
            def _(pe):
                def turn_group(tile, b):
                    for i, n in group_blocks(2 + b):
                        last = pe.transpose(misc_bank[0:n, (i % 4) * P:(i % 4 + 1) * P], group[:, tile, i * P:i * P + n],
                                            ident[:])
                    last.then_inc(misc_ready, 1)

                def turn_bank(tj, tu, k):
                    await_(pe, bank_moved[k % 2], tj * 64 + (2 * tu + k // 2))
                    for i, n in group_blocks(k):
                        last = pe.transpose(turn_banks[0:n, k % 2, (i % 4) * P:(i % 4 + 1) * P],
                                            rows[tu % L_SLOTS][:, i * P:i * P + n], ident[:])
                    last.then_inc(bank_turned[k % 2], 1)

                def step(j, u, what):
                    tile, h = u // XH, u % XH
                    tj, tu = back(j, u, LT)
                    if what.head:
                        if h == 0:
                            pe.wait_ge(q_loaded[tile], j * 128 + 128)
                        await_(pe, logits_out, j * 32 + u)
                        for lo, n in S_CH:
                            last = pe.matmul(score_banks[:, lo:lo + n], q_stack[:, tile, h, :],
                                             k_stack[:, h // 2, lo:lo + n], start=True, stop=True)
                        last.then_inc(scored, 1)
                    if what.turn:
                        pe.wait_ge(weighted, tj * 32 + (tu + 1))
                        for k in (0, 1):
                            turn_bank(tj, tu, k)
                    if what.value is not None:
                        part = what.value
                        vj, vu = back(j, u, LT + 1 + part)
                        g = vu % XH // 4
                        if part == 0:
                            if g == 0:
                                await_(pe, heads_copied, vj * 2 + vu // XH)
                            for b in range(2):
                                pe.wait_ge(bank_moved[b], vj * 64 + (2 * vu + 2))
                        for i in VALUE_PARTS[part]:
                            n = KEY_ROWS[i]
                            for q in range(4):
                                at = (4 * g + q) * XD
                                last = pe.matmul(value_bank[32 * q:32 * q + 32, g, :], v[0:n, i, at:at + 2 * XD],
                                                 turned[0:n, (vu - 3 + q) % PT_SLOTS, i, :], start=(i == 0), stop=(i == CT - 1))
                        if part == 3:
                            last.then_inc(group_valued, 1)
                    for k in (2, 3) if what.turn else ():
                        turn_bank(tj, tu, k)
                    if what.finish is not None:
                        k = what.finish
                        pe.wait_ge(misc_read, misc_number(j, u, k))
                        if k == 0:
                            pe.wait_ge(heads_copied, j * 2 + u // XH)
                            for g in range(4):
                                last = pe.transpose(misc_bank[:, g * P:(g + 1) * P], heads[:, g, :], ident[:])
                        elif k == 1:
                            for c in range(DC):
                                last = pe.transpose(misc_bank[:, c * P:(c + 1) * P], heads_normed[:, c * P:(c + 1) * P],
                                                    ident[:])
                        else:
                            for c in range(DC):
                                last = pe.matmul(misc_bank[:, 0:D], heads_turned[:, c, :], w_out[:, c, :],
                                                 start=(c == 0), stop=(c == DC - 1))
                        last.then_inc(misc_ready, 1)
                    if what.next_group is not None:
                        b = what.next_group
                        pe.wait_ge(misc_read, misc_number(j, u, 3 + b))
                        if b == 0:
                            pe.wait_ge(group_loaded[1 - tile], j * 16 + 16 * (tile + 1))
                        turn_group(1 - tile, b)

                pe.wait_ge(group_loaded[0], 16)
                for b in range(2):
                    await_(pe, misc_read, b)
                    turn_group(0, b)
                stream(pe, step)

            def await_bank(j, u, k, eng):
                eng.wait_ge(bank_turned[k % 2], j * 64 + (2 * u + k // 2 + 1))
                if k in (BY_SCALAR[0], BY_VECTOR[0]):
                    await_(eng, group_valued, j * 8 + ((u - PT_SLOTS) // 4 + 1))

            def bank_target(u, k):
                members = [i for i, _ in group_blocks(k)]
                n = KEY_ROWS[members[0]]
                tiles = slice(members[0], members[-1] + 1)
                return (turned[0:n, u % PT_SLOTS, tiles, :].rearrange("p i n -> p (i n)"),
                        turn_banks[0:n, k % 2, 0:P * len(members)], members)

            @block.scalar
            def _(act):
                def copy_group(tile, b):
                    members = group_blocks(2 + b)
                    n = members[0][1]
                    act.activation(group_turned[0:n, tile, 4 * b:4 * b + len(members), :].rearrange("p i n -> p (i n)"),
                                   misc_bank[0:n, 0:P * len(members)], ACT.Copy).then_inc(misc_read, 1)

                def step(j, u, what):
                    tile, h = u // XH, u % XH
                    tj, tu = back(j, u, LT)
                    for k in BY_SCALAR if what.turn else ():
                        await_bank(tj, tu, k, act)
                        target, source, _ = bank_target(tu, k)
                        act.activation(target, source, ACT.Copy).then_inc(bank_moved[k % 2], 1)
                    if what.head:
                        act.wait_ge(logits_out, j * 32 + (u + 1))
                        act.activation(rows[u % L_SLOTS], rows[u % L_SLOTS], ACT.Exp, bias=peaks[:, u:u + 1], scale=-1.0,
                                       accum_out=sums[:, tile, h:h + 1]).then_inc(exp_out, 1)
                    if what.copy_heads:
                        act.wait_ge(group_valued, j * 8 + 4 * tile)
                        await_(act, misc_ready, j * 10 + (5 * tile - 5))
                        act.activation(heads[:], value_bank[:], ACT.Copy).then_inc(heads_copied, 1)
                    if what.finish == 1:
                        act.wait_ge(misc_ready, misc_number(j, u, 1) + 1)
                        act.activation(heads_turned[:].rearrange("p c n -> p (c n)"), misc_bank[:, 0:D],
                                       ACT.Copy).then_inc(misc_read, 1)
                    if what.next_group is not None:
                        b = what.next_group
                        act.wait_ge(misc_ready, misc_number(j, u, 3 + b) + 1)
                        if b == 0:
                            await_(act, bank_moved[1], j * 64 + 32 * tile)
                        copy_group(1 - tile, b)

                for b in range(2):
                    act.wait_ge(misc_ready, b + 1)
                    copy_group(0, b)
                stream(act, step)

            @block.vector
            def _(dve):
                def step(j, u, what):
                    tile, h = u // XH, u % XH
                    if what.head:
                        dve.wait_ge(scored, j * 32 + (u + 1))
                        if h == 0:
                            dve.wait_ge(negated, j * 2 + (tile + 1))
                        for b in range(2):
                            await_(dve, bank_turned[b], j * 64 + (2 * (u - L_SLOTS) + 2))
                        dve.memset(gate[:, 0:1], 0.0)
                        dve.tensor_tensor_reduce(rows[u % L_SLOTS], score_banks[:, 0:S2], negative[:, tile, :],
                                                 -(XD ** -0.5), 3e38, ALU.add, ALU.min,
                                                 peaks[:, u:u + 1]).then_inc(logits_out, 1)
                    tj, tu = back(j, u, LT)
                    for k in BY_VECTOR if what.turn else ():
                        if k == BY_VECTOR[0] and tu % XH == 0:
                            dve.wait_ge(misc_read, 2 if isinstance(tj, int) and tj == 0 and tu == 0
                                        else tj * 10 + (5 * (tu // XH) - 1))
                        await_bank(tj, tu, k, dve)
                        target, source, members = bank_target(tu, k)
                        weights = group_turned[0:KEY_ROWS[members[0]], tu // XH,
                                               members[0] - WEIGHTED // P:members[-1] + 1 - WEIGHTED // P, :]
                        dve.tensor_tensor(target, source, weights.rearrange("p i n -> p (i n)"),
                                          ALU.mult).then_inc(bank_moved[k % 2], 1)
                    before = (tile + 1) % 2
                    if what.finish == 0:
                        dve.wait_ge(exp_out, j * 32 + XH * tile)
                        dve.reciprocal(inverse[:, before, :], sums[:, before, :]).then_inc(inverted, 1)
                        dve.wait_ge(inverted, j * 2 + tile)
                        dve.wait_ge(misc_ready, misc_number(j, u, 0) + 1)
                        dve.tensor_tensor(heads_normed[:].rearrange("p (h d) -> p h d", h=XH),
                                          misc_bank[:].rearrange("p (h e) -> p h e", h=XH)[:, :, 0:XD],
                                          spread(inverse[:, before, :], 2, XD), ALU.mult).then_inc(misc_read, 1)
                    if what.finish == 2:
                        dve.wait_ge(misc_ready, misc_number(j, u, 2) + 1)
                        x = X[:, bass.ds(j * 2 + (tile - 1), 1), :].rearrange("p a d -> p (a d)")
                        dve.tensor_tensor(x, x, misc_bank[:, 0:D], ALU.add).then_inc(misc_read, 1)

                stream(dve, step)

            @block.gpsimd
            def _(pool):
                def negate(tile, loads, number):
                    pool.wait_ge(mask_loaded[tile], loads)
                    mask = negative[:, tile, :]
                    pool.tensor_tensor(gate[:, 1:2], gate[:, 3:4], gate[:, 3:4], ALU.add)
                    pool.tensor_scalar(mask, mask.bitcast(I32), -1.0, 1.0, ALU.mult, ALU.add).then_inc(mask_flipped, 1)
                    pool.wait_ge(mask_flipped, number)
                    pool.tensor_tensor(gate[:, 2:3], gate[:, 3:4], gate[:, 3:4], ALU.add)
                    pool.tensor_scalar(mask, mask, NEG, XD ** 0.5, ALU.mult, ALU.mult).then_inc(negated, 1)

                def step(j, u, what):
                    tile, h = u // XH, u % XH
                    if what.head:
                        pool.wait_ge(exp_out, j * 32 + (u + 1))
                        if h == 0:
                            pool.wait_ge(group_loaded[tile], j * 16 + 16)
                        r = rows[u % L_SLOTS][:, 0:WEIGHTED]
                        pool.tensor_tensor(r, r, group[:, tile, 0:WEIGHTED], ALU.mult).then_inc(weighted, 1)
                    if what.next_group == 1:
                        negate(1 - tile, j * 16 + 16 * (tile + 1), j * 2 + (tile + 2))

                pool.memset(gate[:, 3:4], 0.0).then_inc(gate_cleared, 1)
                pool.wait_ge(gate_cleared, 1)
                negate(0, 16, 1)
                stream(pool, step)

            @block.sync
            def _(sync):
                def load(parity, row):
                    for b in range(4):
                        for a in range(2):
                            sync.dma_start(q_stack[stack_rows(a, b), parity, a::2, :], q_parts[q_rows[b]].rearrange(
                                "(i a j) t -> a j i t", a=2, j=XD)[a][:, :, bass.ds(row, P)]).then_inc(q_loaded[parity], 16)

                def load_rows(parity, row):
                    sync.dma_start(negative[:, parity, :].bitcast(I32), io["mask_BxSxS2_ik1"].rearrange(
                        "a t s -> (a t) s")[bass.ds(row, P), :]).then_inc(mask_loaded[parity], 16)

                def load_group(parity, row):
                    sync.dma_start(group[:, parity, :], io["fside_BxSxS2_0"].rearrange(
                        "a t s -> (a t) s")[bass.ds(row, P), :]).then_inc(group_loaded[parity], 16)

                def following(j, last=False):
                    for tile in range(1 if last else 2):
                        row = j * (2 * P) + (tile + 1) * P
                        await_(sync, scored, j * 32 + XH * tile)
                        load(1 - tile, row)
                        await_(sync, logits_out, j * 32 + XH * tile)
                        load_rows(1 - tile, row)
                        await_(sync, weighted, j * 32 + XH * tile)
                        load_group(1 - tile, row)

                load(0, 0)
                load_rows(0, 0)
                load_group(0, 0)
                following(0)
                with sync.Fori(1, n_pairs - 1, 1) as j:
                    following(j)
                following(n_pairs - 1, last=True)



AH = 16
AD = 64
NK = T + S2
KT = (NK + P - 1) // P
K_ROWS = [P] * (KT - 1) + [NK - (KT - 1) * P]
K_CH = [(lo, min(CH, NK - lo)) for lo in range(0, NK, CH)]
QW = 2 * CH
PASSES = T // QW
HS = PASSES * KT
PS = 2 * HS
P_SLOTS = 4
MAX_UNIT = 64.0


def big_attention(nc, ident, io, X, R):
    with ExitStack() as ctx:
        def sb(name, shape, dt=F32):
            return ctx.enter_context(nc.sbuf_tensor(name, shape, dt))

        def sem(name):
            return ctx.enter_context(semaphore(nc, name))

        kv = sb("ba_kv", [P, DC, NK])
        affine = sb("ba_affine", [P, 4, DC])
        rows = io["ctx_1024"].rearrange("a s d -> (a s) d")
        with nc.sbuf_tensor("ba_context", [P, CT, D], F32) as context:
            with nc.allow_non_contiguous_dma(reason="vectors of 256 values"):
                norm_block(nc, "norm_0a", ident, R, X, NT, P, True, loads=[(context[:, 0:CT - 1, :], rows[0:(CT - 1) * P].rearrange("(i p) d -> p i d", p=P)),
                                (context[0:CLAST, CT - 1, :], rows[(CT - 1) * P:S2])]
                           + [(affine[:, n, :], io[f"L0_xattn_ln{n // 2 + 1}_{'wb'[n % 2]}"].rearrange("(c p) -> p c", p=P))
                              for n in range(4)])
            norm_block(nc, "ba_norm_x", ident, X, R, NT, P, True, turned=kv, gain=affine[:, 2, :], shift=affine[:, 3, :])
            norm_block(nc, "ba_norm_c", ident, context, context, CT, CLAST, True, turned=kv[:, :, T:NK],
                       gain=affine[:, 0, :], shift=affine[:, 1, :])

        k_high = sb("ba_k_high", [P, 2, NK], F16)
        k_low = sb("ba_k_low", [P, 2, NK], F16)
        q_both = sb("ba_q_both", [P, 2, T], F16)
        q_high = sb("ba_q_high", [P, 2, T], F16)
        v_next = sb("ba_v_next", [P, KT, P])
        v_use = sb("ba_v_use", [P, KT, P])
        probs = sb("ba_probs", [P, P_SLOTS, QW])
        sums_pool = sb("ba_sums_pool", [P, 2, QW])
        sums_vector = sb("ba_sums_vector", [P, 2, QW])
        out_raw = sb("ba_out_raw", [P, CH])
        out_pair = sb("ba_out_pair", [P, T])
        inverse = sb("ba_inverse", [P, CH])
        chunk_max = sb("ba_chunk_max", [P, NT, len(K_CH)])
        row_max = sb("ba_row_max", [P, NT])
        tile_rows = sb("ba_tile_rows", [NT, NT])
        ones = sb("ba_ones", [P, AD])
        w_qk = sb("ba_w_qk", [P, 2, 2, DC, AD])
        w_v = sb("ba_w_v", [P, DC, P])
        w_o = sb("ba_w_o", [P, D])
        score_banks = ctx.enter_context(nc.psum_tensor("ba_score_banks", [P, 2, 2, CH], F32))
        value_bank = ctx.enter_context(nc.psum_tensor("ba_value_bank", [P, CH], F32))
        misc_bank = ctx.enter_context(nc.psum_tensor("ba_misc_bank", [P, CH], F32))
        unit_banks = ctx.enter_context(nc.psum_tensor("ba_unit_banks", [P, 2, CH], F32))

        qk_loaded = [sem(f"ba_qk_loaded_{b}") for b in range(2)]
        v_loaded = sem("ba_v_loaded")
        o_loaded = sem("ba_o_loaded")
        set_up = sem("ba_set_up")
        scored = sem("ba_scored")
        exp_out = sem("ba_exp_out")
        valued = sem("ba_valued")
        pool_summed = sem("ba_pool_summed")
        vector_summed = sem("ba_vector_summed")
        unit_ready = [sem(f"ba_unit_ready_{b}") for b in range(2)]
        unit_free = [sem(f"ba_unit_free_{b}") for b in range(2)]
        high_out = sem("ba_high_out")
        v_copied = sem("ba_v_copied")
        pool_set = sem("ba_pool_set")
        out_copied = sem("ba_out_copied")
        out_placed = sem("ba_out_placed")
        max_ready = sem("ba_max_ready")
        misc_ready = sem("ba_misc_ready")
        misc_read = sem("ba_misc_read")
        block = ctx.enter_context(nc.Block())

        Q_UNITS = T // CH // 2
        K_UNITS = (len(K_CH) + 1) // 2

        def units_of(even):
            units = [("q", n, 0) for n in range(Q_UNITS)]
            for c in range(len(K_CH)):
                if c % 2 == 0:
                    units.append(("k", c // 2, 0))
                if even:
                    units.append(("v", c, 0))
                units += [("max", c, t) for t in range(NT)]
            return units

        EVEN, ODD = units_of(True), units_of(False)
        BOTH = len(EVEN) + len(ODD)
        assert len(EVEN) % 2 == 0 and len(ODD) % 2 == 0
        WEIGHT = {"q": 8, "k": 8, "v": 4, "max": 4}
        SUM_LOAD, INVERT_LOAD = 2, 1
        LAST_UNIT = 51
        MAX_STEP, ROWS_STEP = 51, 53
        SUM_STEPS = (4, KT + 4)
        OUT_STEPS = tuple(range(16, 32, 2))
        V_COPY = {87 + 4 * c + 5: c for c in range(6)} | {115: 6}
        PASS_OF = {9: 0, 11: 1, 12: 2, 0: 3}
        MISC = len(OUT_STEPS) + 6
        n_pairs = AH // 2

        def await_(eng, semaphore, value):
            if not isinstance(value, int) or value > 0:
                eng.wait_ge(semaphore, value)

        def on_vector(s):
            return s % 4 == 2

        PIECES = 8

        def unit_plan(odd_window):
            units, base = (EVEN, len(ODD)) if odd_window else (ODD, 0)
            plan = {}
            other = [SUM_LOAD * on_vector(w % KT) + sum(INVERT_LOAD for v in SUM_STEPS if 0 <= w - v <= PIECES + 1)
                     for w in range(LAST_UNIT)]
            total = sum(WEIGHT[kind] for kind, _, _ in units)
            share = (total + sum(other)) / LAST_UNIT
            at, w, end = 0, 0, share - other[0]
            for i, unit in enumerate(units):
                while at >= end and w < LAST_UNIT - 1:
                    w += 1
                    end += share - other[w]
                plan.setdefault(w, []).append((base + i, unit))
                at += WEIGHT[unit[0]]
            return plan

        PLANS = unit_plan(False), unit_plan(True)

        POOL_OPS = sum(not on_vector(s) for s in range(KT)) - 1
        VECTOR_OPS = sum(on_vector(s) for s in range(KT))

        def summed(j, u):
            f, s = u // KT, u % KT
            if on_vector(s):
                return vector_summed, j * (4 * VECTOR_OPS) + (f * VECTOR_OPS + sum(on_vector(i) for i in range(s + 1)))
            mine = max(1, sum(not on_vector(i) for i in range(s + 1)) - 1)
            return pool_summed, j * (4 * POOL_OPS) + (f * POOL_OPS + mine)

        def misc_number(j, k):
            number = j * MISC + (k - len(OUT_STEPS))
            return number - 1 if isinstance(j, int) and j == n_pairs else number

        def sums_use(f):
            return ((0, 9), (0, 11), (0, 12), (1, 0))[f]

        class Step:

            def __init__(self, u, first, last, tail):
                odd, w = u // HS, u % HS
                self.main = not tail
                self.units = [] if tail or (last and odd) else PLANS[odd].get(w, [])
                self.score_ahead = not tail and not (last and u >= PS - 2)
                self.sums = None
                if w in SUM_STEPS and not (first and u == SUM_STEPS[0]) and (not tail or u == SUM_STEPS[0]):
                    self.sums = (0, 9, 11, 12)[2 * odd + SUM_STEPS.index(w)]
                self.invert = None
                for piece in range(PIECES + 2):
                    v = w - piece
                    if v in SUM_STEPS and not (first and u - piece == SUM_STEPS[0]) and (not tail or u - piece == SUM_STEPS[0]):
                        self.invert = (0, 9, 11, 12)[2 * odd + SUM_STEPS.index(v)], piece
                self.project = OUT_STEPS.index(u) if u in OUT_STEPS and not first else None
                self.maximum = w == MAX_STEP and not tail and not (last and odd)
                self.rows = (13 if odd else 10) if w == ROWS_STEP and not tail and not (last and odd) else None
                self.copy_out = u % KT == 0 and not (first and u == 0) and (not tail or u == 0)
                self.copy_v = V_COPY.get(u) if not last and not tail else None
                if u == 2 and not first and not tail:
                    self.copy_v = 7

        def stream(eng, step):
            def pair(j, first=False, last=False):
                for u in range(PS):
                    step(j, u, Step(u, first, last, False))
            pair(0, first=True)
            with eng.Fori(1, n_pairs - 1, 1) as j:
                pair(j)
            pair(n_pairs - 1, last=True)
            for u in range(OUT_STEPS[-1] + 1):
                step(n_pairs, u, Step(u, False, False, True))

        def slot_uses(j, i):
            return j * (BOTH // 2) + (len(EVEN) + i) // 2

        def qk_units(j, odd_window, c):
            per = Q_UNITS + K_UNITS
            return j * (2 * per) + (per * (1 + odd_window) + c + 1)

        def qk_index(unit):
            kind, c, _ = unit
            return c if kind == "q" else Q_UNITS + c

        def chunks_of(unit):
            kind, c, _ = unit
            chunks = [(lo, CH) for lo in range(0, T, CH)] if kind == "q" else K_CH
            return [(half, *chunk) for half, chunk in enumerate(chunks[2 * c:2 * c + 2])]

        def value_tiles(c):
            return [(i, K_ROWS[i]) for i in range(4 * c, min(4 * c + 4, KT))]

        @block.tensor
        def _(pe):
            def do_unit(j, i, unit, odd_window):
                kind, c, t = unit
                slot = i % 2
                target = 1 - odd_window
                bank = unit_banks[:, slot, :]
                await_(pe, unit_free[slot], slot_uses(j, i))
                if kind in "qk":
                    if kind == "q" and c == 0:
                        pe.wait_ge(qk_loaded[target], j * 32 + 32 * (1 + odd_window))
                    for k in range(DC):
                        for half, lo, n in chunks_of(unit):
                            last = pe.matmul(bank[half * AD:(half + 1) * AD, 0:n], w_qk[:, target, 0 if kind == "q" else 1, k, :],
                                             kv[:, k, lo:lo + n], start=(k == 0), stop=(k == DC - 1))
                elif kind == "v":
                    if c == 0:
                        pe.wait_ge(v_loaded, j * 16 + 32)
                    for m, (key, n) in enumerate(value_tiles(c)):
                        for k in range(DC):
                            last = pe.matmul(bank[0:n, m * P:(m + 1) * P], kv[:, k, key * P:key * P + n], w_v[:, k, :],
                                             start=(k == 0), stop=(k == DC - 1))
                else:
                    lo, n = K_CH[c]
                    if t == 0 and c % 2 == 0:
                        base = len(ODD) + EVEN.index(("k", c // 2, 0)) if odd_window else ODD.index(("k", c // 2, 0))
                        pe.wait_ge(unit_free[base % 2], slot_uses(j, base) + 1)
                        if c == 0:
                            pe.wait_ge(unit_free[(base - 1) % 2], slot_uses(j, base - 1) + 1)
                    last = pe.matmul(bank[:, 0:n], q_both[:, target, t * P:(t + 1) * P], k_high[:, target, lo:lo + n],
                                     start=True, stop=True)
                last.then_inc(unit_ready[slot], 1)

            def score(u, between):
                h, f, key = u // HS % 2, u // KT % 2, u % KT
                n = K_ROWS[key]
                for part_k, part_q, which in ((k_high, q_both, 0), (k_low, q_high, 1)):
                    if which == 1:
                        for unit in between:
                            do_unit(*unit)
                    for half in range(2):
                        at = f * QW + half * CH
                        last = pe.matmul(score_banks[0:n, u % 2, half, :], part_k[:, h, key * P:key * P + n],
                                         part_q[:, h, at:at + CH], start=(which == 0), stop=(which == 1))
                last.then_inc(scored, 1)

            def turn_maxima(number, use):
                pe.wait_ge(max_ready, number)
                await_(pe, misc_read, use)
                pe.transpose(misc_bank[0:NT, 0:P], row_max[:], ident[:]).then_inc(misc_ready, 1)

            def step(j, u, what):
                odd, w, key = u // HS, u % HS, u % KT
                units = list(what.units)
                if units:
                    do_unit(j, *units.pop(0), odd)
                if what.main:
                    pe.wait_ge(exp_out, j * PS + (u + 1))
                    if key == 0:
                        await_(pe, out_copied, j * 4 + u // KT)
                    if u < KT and key % 4 == 0:
                        pe.wait_ge(v_copied, j * 8 + (key // 4 + 1))
                    n = K_ROWS[key]
                    for half in range(2):
                        if half and units:
                            do_unit(j, *units.pop(0), odd)
                        last = pe.matmul(value_bank[half * AD:(half + 1) * AD, :], v_use[0:n, key, odd * AD:(odd + 1) * AD],
                                         probs[0:n, u % P_SLOTS, half * CH:(half + 1) * CH],
                                         start=(key == 0), stop=(key == KT - 1))
                    last.then_inc(valued, 1)
                if what.score_ahead:
                    if w == HS - 2:
                        pe.wait_ge(misc_read, misc_number(j, 13 if odd else 10) + 1)
                    between = [(j, *units.pop(0), odd)] if units else []
                    score(u + 2, between)
                for unit in units:
                    do_unit(j, *unit, odd)
                if what.sums is not None:
                    k = what.sums
                    f = PASS_OF[k]
                    fj = j - 1 if k == 0 else j
                    pe.wait_ge(misc_read, misc_number(j, k))
                    pe.wait_ge(*summed(fj, f * KT + KT - 1))
                    pe.wait_ge(*summed(fj, f * KT + KT - 3))
                    for half in range(2):
                        out = misc_bank[half * AD:(half + 1) * AD, :]
                        pe.matmul(out, ones[:], sums_pool[:, f % 2, half * CH:(half + 1) * CH], start=True, stop=False)
                        last = pe.matmul(out, ones[:], sums_vector[:, f % 2, half * CH:(half + 1) * CH],
                                         start=False, stop=True)
                    last.then_inc(misc_ready, 1)
                if what.project is not None:
                    k = what.project
                    pe.wait_ge(misc_read, misc_number(j, 1 + k))
                    if k == 0:
                        pe.wait_ge(o_loaded, j * 16)
                        pe.wait_ge(out_placed, j * 4)
                    for m in range(2):
                        t = 2 * k + m
                        last = pe.matmul(misc_bank[:, m * D:(m + 1) * D], out_pair[:, t * P:(t + 1) * P], w_o[:],
                                         start=True, stop=True)
                    last.then_inc(misc_ready, 1)
                if what.rows is not None:
                    turn_maxima(j * 2 + (2 + odd), misc_number(j, what.rows))

            pe.wait_ge(set_up, 1)
            for i, unit in enumerate(EVEN):
                do_unit(-1, len(ODD) + i, unit, 1)
            turn_maxima(1, 0)
            pe.wait_ge(misc_read, 1)
            pe.wait_ge(pool_set, 5)
            score(0, [])
            score(1, [])
            stream(pe, step)

        @block.scalar
        def _(act):
            def do_unit(j, i, unit, odd_window):
                kind, c, _ = unit
                slot, target = i % 2, 1 - odd_window
                if kind == "max":
                    return
                act.wait_ge(unit_ready[slot], slot_uses(j, i) + 1)
                bank = unit_banks[:, slot, :]
                if kind == "v":
                    if c == 0:
                        await_(act, v_copied, j * 8 + 8)
                    members = value_tiles(c)
                    n = members[0][1]
                    act.activation(v_next[0:n, 4 * c:4 * c + len(members), :].rearrange("p i n -> p (i n)"),
                                   bank[0:n, 0:P * len(members)], ACT.Copy).then_inc(unit_free[slot], 1)
                    return
                if kind == "q":
                    if c == 0:
                        await_(act, scored, j * PS + HS * odd_window)
                for half, lo, n in chunks_of(unit):
                    src = bank[half * AD:(half + 1) * AD, 0:n]
                    for dst in (q_high[0:AD], q_both[0:AD]) if kind == "q" else (k_high[0:AD], k_high[AD:P]):
                        last = act.activation(dst[:, target, lo:lo + n], src, ACT.Copy)
                last.then_inc(high_out, 1)

            def copy_v(j, c, staged):
                act.wait_ge(unit_free[staged[0]], staged[1])
                members = value_tiles(c)
                n = members[0][1]
                act.activation(v_use[0:n, 4 * c:4 * c + len(members), :], v_next[0:n, 4 * c:4 * c + len(members), :],
                               ACT.Copy).then_inc(v_copied, 1)

            def staged_by(j, c):
                i = len(ODD) + EVEN.index(("v", c, 0))
                return i % 2, slot_uses(j, i) + 1

            def step(j, u, what):
                odd, key = u // HS, u % KT
                if what.main:
                    act.wait_ge(scored, j * PS + (u + 1))
                    await_(act, valued, j * PS + (u - 3))
                    if not (isinstance(j, int) and j == 0 and u < P_SLOTS):
                        act.wait_ge(*(summed(j, u - 4) if u >= 4 else summed(j - 1, u - 4 + PS)))
                    n = K_ROWS[key]
                    act.activation(probs[0:n, u % P_SLOTS, :], score_banks[0:n, u % 2].rearrange("p a n -> p (a n)"),
                                   ACT.Exp, scale=AD ** -0.5).then_inc(exp_out, 1)
                if what.copy_out:
                    act.wait_ge(valued, j * PS + u)
                    await_(act, out_placed, j * 4 + (u // KT - 1))
                    act.activation(out_raw[:], value_bank[:], ACT.Copy).then_inc(out_copied, 1)
                for i, unit in what.units:
                    do_unit(j, i, unit, odd)
                if what.copy_v is not None:
                    c = what.copy_v
                    if c == 7:
                        act.wait_ge(valued, j * PS)
                        copy_v(j, c, staged_by(j - 1, c))
                    else:
                        act.wait_ge(valued, j * PS + (3 * KT + 4 * c + 4))
                        copy_v(j, c, staged_by(j, c))

            act.wait_ge(set_up, 1)
            for i, unit in enumerate(EVEN):
                do_unit(-1, len(ODD) + i, unit, 1)
            for c in range(8):
                copy_v(-1, c, staged_by(-1, c))
            stream(act, step)

        @block.vector
        def _(dve):
            def do_unit(j, i, unit, odd_window):
                kind, c, t = unit
                slot, target = i % 2, 1 - odd_window
                bank = unit_banks[:, slot, :]
                if kind == "v":
                    return
                if kind == "max":
                    n = K_CH[c][1]
                    dve.wait_ge(unit_ready[slot], slot_uses(j, i) + 1)
                    dve.tensor_reduce(chunk_max[:, t, c:c + 1], bank[:, 0:n], AX.X, ALU.max).then_inc(unit_free[slot], 1)
                    return
                dve.wait_ge(high_out, qk_units(j, odd_window, qk_index(unit)))
                for half, lo, n in chunks_of(unit):
                    src = bank[half * AD:(half + 1) * AD, 0:n]
                    high, low = (q_high, q_both[AD:P]) if kind == "q" else (k_high, k_low[0:AD])
                    last = dve.tensor_tensor(low[:, target, lo:lo + n], src, high[0:AD, target, lo:lo + n], ALU.subtract)
                last.then_inc(unit_free[slot], 1)

            def finish_max(j, odd_window):
                end = (len(ODD) if not odd_window else BOTH)
                for i in (end - 2, end - 1):
                    dve.wait_ge(unit_free[i % 2], slot_uses(j, i) + 1)
                dve.tensor_reduce(row_max[:], chunk_max[:], AX.X, ALU.max).then_inc(max_ready, 1)

            def place_rows(target, use):
                dve.wait_ge(misc_ready, use + 1)
                dve.tensor_tensor(q_high[AD:AD + NT, target, :].rearrange("r (t n) -> r t n", t=NT),
                                  spread(misc_bank[0:NT, 0:P], 1, NT), spread(tile_rows[:], 2, P),
                                  ALU.mult).then_inc(misc_read, 1)

            def step(j, u, what):
                odd, s, f = u // HS, u % KT, u // KT
                units = list(what.units)
                if units:
                    do_unit(j, *units.pop(0), odd)
                if what.main and on_vector(s):
                    dve.wait_ge(exp_out, j * PS + (u + 1))
                    if s == 2:
                        if not (isinstance(j, int) and j == 0 and f < 2):
                            later, use = sums_use((f - 2) % 4)
                            dve.wait_ge(misc_ready, misc_number(j - 1 + later if f < 2 else j + later, use) + 1)
                    else:
                        sem_, value = summed(j, u - 4)
                        dve.wait_ge(sem_, value)
                    for half in range(2):
                        total = sums_vector[:, f % 2, half * CH:(half + 1) * CH]
                        part = probs[:, u % P_SLOTS, half * CH:(half + 1) * CH]
                        if s == 2:
                            last = dve.tensor_copy(total, part)
                        else:
                            last = dve.tensor_tensor(total, total, part, ALU.add)
                        if half == 0 and units:
                            do_unit(j, *units.pop(0), odd)
                    last.then_inc(vector_summed, 1)
                for unit in units:
                    do_unit(j, *unit, odd)
                if what.invert is not None:
                    k, piece = what.invert
                    number = misc_number(j, k)
                    done = (j - 1 if k == 0 else j) * 4 + PASS_OF[k]
                    if piece == 0:
                        dve.wait_ge(misc_ready, number + 1)
                        await_(dve, out_placed, done)
                    if piece < PIECES:
                        at = slice(piece * (CH // PIECES), (piece + 1) * (CH // PIECES))
                        last = dve.reciprocal(inverse[:, at], misc_bank[:, at])
                        if piece == PIECES - 1:
                            last.then_inc(misc_read, 1)
                    else:
                        g = PASS_OF[k]
                        half = piece - PIECES
                        if half == 0:
                            dve.wait_ge(misc_read, number + 1)
                            dve.wait_ge(out_copied, done + 1)
                        rows = slice(half * AD, (half + 1) * AD)
                        at = (g % 2) * QW + half * CH
                        last = dve.tensor_tensor(out_pair[g // 2 * AD:(g // 2 + 1) * AD, at:at + CH], out_raw[rows, :],
                                                 inverse[rows, :], ALU.mult)
                        if half == 1:
                            last.then_inc(out_placed, 1)
                if what.project is not None:
                    k = what.project
                    dve.wait_ge(misc_ready, misc_number(j, 1 + k) + 1)
                    r = R[:, 2 * k:2 * k + 2, :].rearrange("p a d -> p (a d)")
                    dve.tensor_tensor(r, r, misc_bank[:], ALU.add).then_inc(misc_read, 1)
                if what.maximum:
                    finish_max(j, odd)
                if what.rows is not None:
                    place_rows(1 - odd, misc_number(j, what.rows))

            dve.tensor_scalar(tile_rows[:], ident[0:NT, 0:NT], -1.0 / MAX_UNIT, None, ALU.mult)
            dve.memset(ones[:], 1.0).then_inc(set_up, 1)
            for i, unit in enumerate(EVEN):
                do_unit(-1, len(ODD) + i, unit, 1)
            finish_max(-1, 1)
            dve.wait_ge(pool_set, 5)
            place_rows(0, 0)
            stream(dve, step)

        @block.gpsimd
        def _(pool):
            def step(j, u, what):
                s, f = u % KT, u // KT
                if not what.main or on_vector(s) or s == 0:
                    return
                pool.wait_ge(exp_out, j * PS + (u + 1))
                n = K_ROWS[s]
                total, part = sums_pool[0:n, f % 2, :], probs[0:n, u % P_SLOTS, :]
                if s == 1:
                    if not (isinstance(j, int) and j == 0 and f < 2):
                        later, use = sums_use((f - 2) % 4)
                        pool.wait_ge(misc_ready, misc_number(j - 1 + later if f < 2 else j + later, use) + 1)
                    total, other = sums_pool[:, f % 2, :], probs[:, (u - 1) % P_SLOTS, :]
                else:
                    before = u - 1 if not on_vector(s - 1) else u - 2
                    pool.wait_ge(*summed(j, before))
                    other = total
                pool.tensor_tensor(total, other, part, ALU.add).then_inc(pool_summed, 1)

            pool.memset(q_high[AD:P, :, :], 0.0).then_inc(pool_set, 1)
            pool.wait_ge(pool_set, 1)
            pool.memset(k_low[AD:P, :, :], 0.0).then_inc(pool_set, 1)
            pool.wait_ge(pool_set, 2)
            pool.memset(k_low[AD:AD + NT, :, :], MAX_UNIT).then_inc(pool_set, 1)
            pool.wait_ge(pool_set, 3)
            pool.memset(sums_vector[:], 0.0).then_inc(pool_set, 1)
            pool.wait_ge(pool_set, 4)
            pool.tensor_copy(R[:], X[:]).then_inc(pool_set, 1)
            pool.wait_ge(pool_set, 5)
            stream(pool, step)

        @block.sync
        def _(sync):
            def load_qk(parity, head):
                for n, name in enumerate(("L0_xattn_Wq", "L0_xattn_Wkv")):
                    src = io[name].rearrange("(c p) n -> p c n", p=P)[:, :, bass.ds(head * AD, AD)]
                    sync.dma_start(w_qk[:, parity, n], src).then_inc(qk_loaded[parity], 16)

            def load_v(pair):
                src = io["L0_xattn_Wkv"].rearrange("(c p) n -> p c n", p=P)[:, :, bass.ds(pair * P + AH * AD, P)]
                sync.dma_start(w_v[:], src).then_inc(v_loaded, 16)

            def windows(j, last=False):
                if not last:
                    sync.wait_ge(unit_ready[1], slot_uses(j, 0))
                    load_qk(0, j * 2 + 2)
                    load_v(j + 1)
                if not (isinstance(j, int) and j == 0):
                    sync.wait_ge(misc_ready, misc_number(j, 8) + 1)
                sync.dma_start(w_o[:], io["L0_xattn_Wo"][bass.ds(j * P, P), :]).then_inc(o_loaded, 16)
                if not last:
                    sync.wait_ge(unit_ready[1], slot_uses(j, len(ODD)))
                    load_qk(1, j * 2 + 3)

            load_qk(0, 0)
            load_qk(1, 1)
            load_v(0)
            windows(0)
            with sync.Fori(1, n_pairs - 1, 1) as j:
                windows(j)
            windows(n_pairs - 1, last=True)


def decoder(nc, io, out):
    with ExitStack() as ctx:
        ident = ctx.enter_context(nc.sbuf_tensor("identity", [P, P], F32))
        X = ctx.enter_context(nc.sbuf_tensor("X", [P, NT, D], F32))
        R = ctx.enter_context(nc.sbuf_tensor("R", [P, NT, D], F32))
        with nc.cleanup_on_exit():
            local_attention(nc, io, ident, X, R)
        with nc.cleanup_on_exit():
            big_attention(nc, ident, io, X, R)
        with nc.cleanup_on_exit():
            quantised_ffn(nc, ident, io, X, R)
        with nc.cleanup_on_exit():
            retention(nc, ident, io, X, R)
        with nc.cleanup_on_exit():
            masked_attention(nc, ident, io, X, R)
        with nc.cleanup_on_exit():
            experts_ffn(nc, ident, io, X, R)
            norm_block(nc, "norm_1c", ident, R, X, NT, P, True)
        with semaphore(nc, "stored") as stored, nc.Block() as block:
            @block.sync
            def _(sync):
                sync.dma_start(out.rearrange("a (i p) d -> p (a i) d", p=P), X[:]).then_inc(stored, 16)
                sync.wait_ge(stored, 16)


def kernel(**inputs):
    import concourse.bacc as bacc
    from concourse.bass_utils import run_bass_kernel_spmd

    nc = bacc.Bacc("TRN2", target_bir_lowering=False, num_devices=1)
    constants = {**basic_constants(), **retention_constants(), **expert_constants()}
    arrays, io = {}, {}
    for name, value in {**inputs, **constants}.items():
        a = np.ascontiguousarray(value)
        arrays[f"in_{name}"] = a
        io[name] = nc.dram_tensor(f"in_{name}", a.shape, mybir.dt.from_np(a.dtype), kind="ExternalInput").ap()
    out = nc.dram_tensor("out_0", (1, T, D), F32, kind="ExternalOutput").ap()
    decoder(nc, io, out)
    r = run_bass_kernel_spmd(nc, [arrays], core_ids=[0])
    return r.results[0]["out_0"]
```
